# Optimizing a Trainium2 kernel written in Bass

```python
import numpy as np
import jax
import jax.numpy as jnp

def _softmax(x, axis=-1):
    return jax.nn.softmax(x, axis=axis)

def _gelu(x):
    return jax.nn.gelu(x, approximate=True)

def _silu(x):
    return jax.nn.silu(x)

def _sigmoid(x):
    return jax.nn.sigmoid(x)

def _layernorm(x, axis=-1, eps=1e-05):
    m = jnp.mean(x, axis=axis, keepdims=True)
    v = jnp.var(x, axis=axis, keepdims=True)
    return (x - m) / jnp.sqrt(v + eps)

def _scatter_add(tgt, idx, src, axis=0):
    return tgt.at[idx].add(src)

def _segment_sum(src, seg, n):
    return jax.ops.segment_sum(src, seg, n)
kernel_name = 'mk_hybrid_d1_jaxref_r8_e983fb'

def setup_inputs(seed: int=0):
    np.random.seed(seed)
    _w = jnp.asarray

    def _L0_attn_a_setup():
        import jax, jax.numpy as jnp
        import numpy as np
        B, T, D_IN, D_OUT = (2, 256, 256, 256)
        N_HEADS, N_KV_HEADS = (32, 8)
        HEAD_DIM = D_OUT // N_HEADS
        N_REP = N_HEADS // N_KV_HEADS
        ROPE_BASE = 10000.0

        def _rope_freqs(head_dim, length, base=ROPE_BASE):
            theta = 1.0 / base ** (jnp.arange(0, head_dim, 2, dtype=jnp.float32) / head_dim)
            pos = jnp.arange(length, dtype=jnp.float32)
            freqs = jnp.outer(pos, theta)
            return (jnp.cos(freqs), jnp.sin(freqs))

        def _apply_rope(x, cos, sin):
            half = x.shape[-1] // 2
            x1, x2 = (x[..., :half], x[..., half:])
            c = cos[None, None, :, :]
            s = sin[None, None, :, :]
            return jnp.concatenate([x1 * c - x2 * s, x2 * c + x1 * s], axis=-1)
        key = jax.random.key(seed)
        ks = jax.random.split(key, 5)
        scale = 1.0 / np.sqrt(D_IN)
        return {'x': jax.random.normal(ks[0], (B, T, D_IN), dtype=jnp.float32), 'Wq': jax.random.normal(ks[1], (D_IN, D_OUT), dtype=jnp.float32) * scale, 'Wk': jax.random.normal(ks[2], (D_IN, N_KV_HEADS * HEAD_DIM), dtype=jnp.float32) * scale, 'Wv': jax.random.normal(ks[3], (D_IN, N_KV_HEADS * HEAD_DIM), dtype=jnp.float32) * scale, 'Wo': jax.random.normal(ks[4], (D_OUT, D_OUT), dtype=jnp.float32) * scale}
    _L0_attn_a_in = _L0_attn_a_setup()

    def _L0_attn_b_setup():
        import jax, jax.numpy as jnp
        import numpy as np
        B, T, D = (1, 256, 256)
        H, DK = (16, 128)
        ROPE, NOPE, VD = (64, 64, 128)
        KVR, QR = (64, 96)
        SCALE = DK ** (-0.5)
        EPS = float(np.finfo(np.float32).eps)

        def rms_norm(h, w):
            var = jnp.mean(h * h, axis=-1, keepdims=True)
            return h * jax.lax.rsqrt(var + EPS) * w

        def rope(x):
            half = ROPE // 2
            inv_freq = 1.0 / 10000.0 ** (jnp.arange(0, ROPE, 2, dtype=jnp.float32) / ROPE)
            t = jnp.arange(x.shape[-2], dtype=jnp.float32)
            freqs = jnp.outer(t, inv_freq)
            cos, sin = (jnp.cos(freqs), jnp.sin(freqs))
            x1, x2 = (x[..., :half], x[..., half:])
            return jnp.concatenate([x1 * cos - x2 * sin, x1 * sin + x2 * cos], axis=-1)
        key = jax.random.key(seed)
        ks = jax.random.split(key, 6)
        s = 0.02
        return {'x': jax.random.normal(ks[0], (B, T, D), jnp.float32), 'wq_a': jax.random.normal(ks[1], (D, QR), jnp.float32) * s, 'q_a_norm_w': jnp.ones((QR,), jnp.float32), 'wq_b': jax.random.normal(ks[2], (QR, H * DK), jnp.float32) * s, 'wkv_a': jax.random.normal(ks[3], (D, KVR + ROPE), jnp.float32) * s, 'kv_a_norm_w': jnp.ones((KVR,), jnp.float32), 'wkv_b': jax.random.normal(ks[4], (KVR, H * (NOPE + VD)), jnp.float32) * s, 'wo': jax.random.normal(ks[5], (H * VD, D), jnp.float32) * s}
    _L0_attn_b_in = _L0_attn_b_setup()

    def _L0_ffn_setup():
        import jax, jax.numpy as jnp
        import numpy as np
        H = 256
        I = 128
        E = 32
        K = 4
        N_SHARED = 1
        EPS = 1e-06

        def _rmsnorm(x, w, eps=EPS):
            var = jnp.mean(jnp.square(x), axis=-1, keepdims=True)
            return x * jax.lax.rsqrt(var + eps) * w

        def _moe_core(x, gate_w, w13, w2):
            T = x.shape[0]
            N = T * K
            C = 2 * N // E
            logits = jnp.einsum('th,eh->te', x.astype(jnp.float32), gate_w.astype(jnp.float32))
            scores = jax.nn.softmax(logits, axis=-1)
            topk_w, topk_ids = jax.lax.top_k(scores, K)
            topk_w = topk_w / jnp.sum(topk_w, axis=-1, keepdims=True)
            flat_ids = topk_ids.reshape(-1)
            flat_w = topk_w.reshape(-1)
            order = jnp.argsort(flat_ids)
            sorted_eid = flat_ids[order]
            tok = order // K
            counts = jnp.zeros((E,), jnp.int32).at[flat_ids].add(1)
            starts = jnp.cumsum(counts) - counts
            pos = jnp.arange(N) - starts[sorted_eid]
            buf = jnp.zeros((E, C, x.shape[1]), x.dtype).at[sorted_eid, pos].set(x[tok], mode='drop')
            gu = jnp.einsum('ech,ehf->ecf', buf, w13)
            g, u = jnp.split(gu, 2, axis=-1)
            act = jax.nn.silu(g) * u
            eo = jnp.einsum('eci,eih->ech', act, w2)
            out_slots = eo[sorted_eid, pos]
            routed = jnp.zeros_like(x).at[tok].add(out_slots * flat_w[order][:, None])
            return routed
        key = jax.random.key(seed)
        ks = jax.random.split(key, 8)
        s = 1.0 / np.sqrt(H)
        si = 1.0 / np.sqrt(I)
        return {'hidden_states': jax.random.normal(ks[0], (1, 512, H), jnp.float32), 'norm_w': jnp.ones((H,), jnp.float32), 'gate_w': jax.random.normal(ks[1], (E, H), jnp.float32) * s, 'w13': jax.random.normal(ks[2], (E, H, 2 * I), jnp.float32) * s, 'w2': jax.random.normal(ks[3], (E, I, H), jnp.float32) * si, 'shared_gate_w': jax.random.normal(ks[4], (H, I * N_SHARED), jnp.float32) * s, 'shared_up_w': jax.random.normal(ks[5], (H, I * N_SHARED), jnp.float32) * s, 'shared_down_w': jax.random.normal(ks[6], (I * N_SHARED, H), jnp.float32) * si}
    _L0_ffn_in = _L0_ffn_setup()
    _d = {'L0_attn_a_x': _L0_attn_a_in['x'], 'L0_attn_a_Wq': _L0_attn_a_in['Wq'], 'L0_attn_a_Wk': _L0_attn_a_in['Wk'], 'L0_attn_a_Wv': _L0_attn_a_in['Wv'], 'L0_attn_a_Wo': _L0_attn_a_in['Wo'], 'L0_attn_b_wq_a': _L0_attn_b_in['wq_a'], 'L0_attn_b_q_a_norm_w': _L0_attn_b_in['q_a_norm_w'], 'L0_attn_b_wq_b': _L0_attn_b_in['wq_b'], 'L0_attn_b_wkv_a': _L0_attn_b_in['wkv_a'], 'L0_attn_b_kv_a_norm_w': _L0_attn_b_in['kv_a_norm_w'], 'L0_attn_b_wkv_b': _L0_attn_b_in['wkv_b'], 'L0_attn_b_wo': _L0_attn_b_in['wo'], 'L0_ffn_norm_w': _L0_ffn_in['norm_w'], 'L0_ffn_gate_w': _L0_ffn_in['gate_w'], 'L0_ffn_w13': _L0_ffn_in['w13'], 'L0_ffn_w2': _L0_ffn_in['w2'], 'L0_ffn_shared_gate_w': _L0_ffn_in['shared_gate_w'], 'L0_ffn_shared_up_w': _L0_ffn_in['shared_up_w'], 'L0_ffn_shared_down_w': _L0_ffn_in['shared_down_w']}
    _x0 = _d['L0_attn_a_x']
    _d['L0_attn_a_x'] = jax.random.normal(jax.random.fold_in(jax.random.key(seed), 1), (8, 256, 256), dtype=_x0.dtype)
    del _x0
    return _d

def reference(L0_attn_a_x, L0_attn_a_Wq, L0_attn_a_Wk, L0_attn_a_Wv, L0_attn_a_Wo, L0_attn_b_wq_a, L0_attn_b_q_a_norm_w, L0_attn_b_wq_b, L0_attn_b_wkv_a, L0_attn_b_kv_a_norm_w, L0_attn_b_wkv_b, L0_attn_b_wo, L0_ffn_norm_w, L0_ffn_gate_w, L0_ffn_w13, L0_ffn_w2, L0_ffn_shared_gate_w, L0_ffn_shared_up_w, L0_ffn_shared_down_w):

    def _L0_attn_a_ref(x, Wq, Wk, Wv, Wo):
        import jax, jax.numpy as jnp
        import numpy as np
        B, T, D_IN, D_OUT = (2, 256, 256, 256)
        N_HEADS, N_KV_HEADS = (32, 8)
        HEAD_DIM = D_OUT // N_HEADS
        N_REP = N_HEADS // N_KV_HEADS
        ROPE_BASE = 10000.0

        def _rope_freqs(head_dim, length, base=ROPE_BASE):
            theta = 1.0 / base ** (jnp.arange(0, head_dim, 2, dtype=jnp.float32) / head_dim)
            pos = jnp.arange(length, dtype=jnp.float32)
            freqs = jnp.outer(pos, theta)
            return (jnp.cos(freqs), jnp.sin(freqs))

        def _apply_rope(x, cos, sin):
            half = x.shape[-1] // 2
            x1, x2 = (x[..., :half], x[..., half:])
            c = cos[None, None, :, :]
            s = sin[None, None, :, :]
            return jnp.concatenate([x1 * c - x2 * s, x2 * c + x1 * s], axis=-1)
        Bx, Tx, _ = x.shape
        cos, sin = _rope_freqs(HEAD_DIM, Tx)
        q = (x @ Wq).reshape(Bx, Tx, N_HEADS, HEAD_DIM).transpose(0, 2, 1, 3)
        k = (x @ Wk).reshape(Bx, Tx, N_KV_HEADS, HEAD_DIM).transpose(0, 2, 1, 3)
        v = (x @ Wv).reshape(Bx, Tx, N_KV_HEADS, HEAD_DIM).transpose(0, 2, 1, 3)
        q = _apply_rope(q, cos, sin)
        k = _apply_rope(k, cos, sin)
        k = jnp.repeat(k, N_REP, axis=1)
        v = jnp.repeat(v, N_REP, axis=1)
        scores = jnp.einsum('bhtd,bhsd->bhts', q, k)
        causal = jnp.triu(jnp.ones((Tx, Tx), dtype=bool), k=1)
        scores = jnp.where(causal[None, None], -jnp.inf, scores)
        attn = jax.nn.softmax(scores / np.sqrt(HEAD_DIM), axis=-1)
        ctx = jnp.einsum('bhts,bhsd->bthd', attn, v).reshape(Bx, Tx, D_OUT)
        return ctx @ Wo

    def _L0_attn_b_ref(x, wq_a, q_a_norm_w, wq_b, wkv_a, kv_a_norm_w, wkv_b, wo):
        import jax, jax.numpy as jnp
        import numpy as np
        B, T, D = (1, 256, 256)
        H, DK = (16, 128)
        ROPE, NOPE, VD = (64, 64, 128)
        KVR, QR = (64, 96)
        SCALE = DK ** (-0.5)
        EPS = float(np.finfo(np.float32).eps)

        def rms_norm(h, w):
            var = jnp.mean(h * h, axis=-1, keepdims=True)
            return h * jax.lax.rsqrt(var + EPS) * w

        def rope(x):
            half = ROPE // 2
            inv_freq = 1.0 / 10000.0 ** (jnp.arange(0, ROPE, 2, dtype=jnp.float32) / ROPE)
            t = jnp.arange(x.shape[-2], dtype=jnp.float32)
            freqs = jnp.outer(t, inv_freq)
            cos, sin = (jnp.cos(freqs), jnp.sin(freqs))
            x1, x2 = (x[..., :half], x[..., half:])
            return jnp.concatenate([x1 * cos - x2 * sin, x1 * sin + x2 * cos], axis=-1)
        b, t, _ = x.shape
        q = rms_norm(x @ wq_a, q_a_norm_w) @ wq_b
        q = q.reshape(b, t, H, DK).transpose(0, 2, 1, 3)
        q_nope, q_pe = (q[..., :NOPE], q[..., NOPE:])
        ckv = x @ wkv_a
        c, k_pe = (ckv[..., :KVR], ckv[..., KVR:])
        kv = rms_norm(c, kv_a_norm_w) @ wkv_b
        kv = kv.reshape(b, t, H, NOPE + VD).transpose(0, 2, 1, 3)
        k_nope, v = (kv[..., :NOPE], kv[..., NOPE:])
        q_pe = rope(q_pe)
        k_pe = rope(k_pe[:, None])
        k_pe = jnp.broadcast_to(k_pe, (b, H, t, ROPE))
        qs = jnp.concatenate([q_nope, q_pe], axis=-1)
        ks = jnp.concatenate([k_nope, k_pe], axis=-1)
        scores = jnp.einsum('bhqd,bhkd->bhqk', qs, ks) * SCALE
        attn = jax.nn.softmax(scores, axis=-1)
        out = jnp.einsum('bhqk,bhkd->bhqd', attn, v)
        out = out.transpose(0, 2, 1, 3).reshape(b, t, H * VD)
        return out @ wo

    def _L0_ffn_ref(hidden_states, norm_w, gate_w, w13, w2, shared_gate_w, shared_up_w, shared_down_w):
        import jax, jax.numpy as jnp
        import numpy as np
        H = 256
        I = 128
        E = 32
        K = 4
        N_SHARED = 1
        EPS = 1e-06

        def _rmsnorm(x, w, eps=EPS):
            var = jnp.mean(jnp.square(x), axis=-1, keepdims=True)
            return x * jax.lax.rsqrt(var + eps) * w

        def _moe_core(x, gate_w, w13, w2):
            T = x.shape[0]
            N = T * K
            C = 2 * N // E
            logits = jnp.einsum('th,eh->te', x.astype(jnp.float32), gate_w.astype(jnp.float32))
            scores = jax.nn.softmax(logits, axis=-1)
            topk_w, topk_ids = jax.lax.top_k(scores, K)
            topk_w = topk_w / jnp.sum(topk_w, axis=-1, keepdims=True)
            flat_ids = topk_ids.reshape(-1)
            flat_w = topk_w.reshape(-1)
            order = jnp.argsort(flat_ids)
            sorted_eid = flat_ids[order]
            tok = order // K
            counts = jnp.zeros((E,), jnp.int32).at[flat_ids].add(1)
            starts = jnp.cumsum(counts) - counts
            pos = jnp.arange(N) - starts[sorted_eid]
            buf = jnp.zeros((E, C, x.shape[1]), x.dtype).at[sorted_eid, pos].set(x[tok], mode='drop')
            gu = jnp.einsum('ech,ehf->ecf', buf, w13)
            g, u = jnp.split(gu, 2, axis=-1)
            act = jax.nn.silu(g) * u
            eo = jnp.einsum('eci,eih->ech', act, w2)
            out_slots = eo[sorted_eid, pos]
            routed = jnp.zeros_like(x).at[tok].add(out_slots * flat_w[order][:, None])
            return routed
        B, S, Hd = hidden_states.shape
        residual = hidden_states
        h = _rmsnorm(hidden_states, norm_w)
        x = h.reshape(-1, Hd)
        routed = _moe_core(x, gate_w, w13, w2)
        shared = jax.nn.silu(x @ shared_gate_w) * (x @ shared_up_w) @ shared_down_w
        out = residual + (routed + shared).reshape(B, S, Hd)
        return out
    x = L0_attn_a_x
    x = x + _L0_attn_a_ref(_layernorm(x, axis=-1), L0_attn_a_Wq, L0_attn_a_Wk, L0_attn_a_Wv, L0_attn_a_Wo)
    x = x + _L0_ffn_ref(_layernorm(x, axis=-1), L0_ffn_norm_w, L0_ffn_gate_w, L0_ffn_w13, L0_ffn_w2, L0_ffn_shared_gate_w, L0_ffn_shared_up_w, L0_ffn_shared_down_w)
    x = x + _L0_attn_b_ref(_layernorm(x, axis=-1), L0_attn_b_wq_a, L0_attn_b_q_a_norm_w, L0_attn_b_wq_b, L0_attn_b_wkv_a, L0_attn_b_kv_a_norm_w, L0_attn_b_wkv_b, L0_attn_b_wo)
    x = x + _L0_ffn_ref(_layernorm(x, axis=-1), L0_ffn_norm_w, L0_ffn_gate_w, L0_ffn_w13, L0_ffn_w2, L0_ffn_shared_gate_w, L0_ffn_shared_up_w, L0_ffn_shared_down_w)
    return x

_drawn_inputs = setup_inputs


def setup_inputs(seed=0):
    import zlib

    import numpy as np

    out = dict(_drawn_inputs(seed))
    spreads = {'L0_attn_b_q_a_norm_w': (1.0, 0.6),
     'L0_attn_b_kv_a_norm_w': (1.0, 0.6),
     'L0_ffn_norm_w': (1.0, 0.2)}
    factors = {'L0_attn_b_wq_a': 8.0,
     'L0_attn_b_wq_b': 8.0,
     'L0_attn_b_wkv_a': 5.913,
     'L0_attn_b_wkv_b': 5.985,
     'L0_attn_b_wo': 6.348}
    for name, (base, spread) in spreads.items():
        noise = np.random.default_rng([zlib.crc32(name.encode()), seed]).standard_normal(out[name].shape)
        drawn = base * np.exp(spread * noise) if base else spread * noise
        out[name] = jnp.asarray(drawn.astype(out[name].dtype))
    for name, factor in factors.items():
        out[name] = (out[name] * factor).astype(out[name].dtype)
    return out
```

```python
from contextlib import ExitStack

import numpy as np

import concourse.bass as bass
from concourse import mybir

ALU = mybir.AluOpType
ACT = mybir.ActivationFunctionType
AX = mybir.AxisListType
F32 = mybir.dt.float32
BF16 = mybir.dt.bfloat16
U32 = mybir.dt.uint32
I32 = mybir.dt.int32

P = 128
B, T, D = 8, 256, 256
NTOK = B * T
TILES = NTOK // P
KD = D // P
LN_EPS = 1e-5

E, TOPK, INNER = 32, 4, 128
CAP = 2 * NTOK * TOPK // E
RMS_EPS = 1e-6
RING = 4
BLOCKS = -(-((NTOK * TOPK + E * (P - 1)) // P) // RING) * RING
SLOTS = BLOCKS * P
GATES = E + 2 * INNER

HA, GA, DA = 32, 8, 8
REP = HA // GA
STACK = 64
HB, DK, ROPE, NOPE, VD, KVR, QR = 16, 128, 64, 64, 128, 64, 96

NEG = -1e30
DROPPED = 1 << 16
STAGES = "afbF"

_WIDTHS = [("ident", P), ("before", P), ("future", P), ("cos_a", 2 * DA), ("sin_a", 2 * DA),
           ("cos_b", 2 * ROPE), ("sin_b", 2 * ROPE), ("experts", E), ("blocks", 1), ("row_mod", REP), ("minus_group", GA)]
CONST = {}
_at = 0
for _name, _w in _WIDTHS:
    CONST[_name] = (_at, _at + _w)
    _at += _w
CONST_COLS = _at


def constants():
    c = np.zeros((P, CONST_COLS), np.float32)

    def put(name, value):
        a, b = CONST[name]
        c[:, a:b] = value

    p = np.arange(P)
    put("ident", np.eye(P))
    put("before", p[:, None] < p[None, :])
    put("future", np.where(p[None, :] > p[:, None], NEG, 0.0))
    for name, dim in (("a", DA), ("b", ROPE)):
        theta = (np.float32(1.0) / np.float32(10000.0) ** (np.arange(0, dim, 2, dtype=np.float32) / np.float32(dim))).astype(np.float32)
        angle = np.outer(np.arange(T, dtype=np.float32), theta).astype(np.float32)
        cos, sin = np.cos(angle), np.sin(angle)
        both = np.concatenate([cos, cos], 1).reshape(2, P, dim).transpose(1, 0, 2)
        sign = np.concatenate([-sin, sin], 1).reshape(2, P, dim).transpose(1, 0, 2)
        put("cos_" + name, both.reshape(P, 2 * dim))
        put("sin_" + name, sign.reshape(P, 2 * dim))
    put("experts", np.arange(E)[None, :])
    put("blocks", p[:, None])
    put("row_mod", (p[:, None] % REP) == np.arange(REP)[None, :])
    put("minus_group", -1.0 * ((p[:, None] // REP) == np.arange(GA)[None, :]))
    return c


def wait(eng, sem, value):
    if not (isinstance(value, int) and value <= 0):
        eng.wait_ge(sem, value)


class Chain:

    def __init__(self, eng, sem, per):
        self.eng, self.sem, self.per, self.k, self.i = eng, sem, per, 0, 0

    def at(self, i):
        assert self.k in (0, self.per), (self.k, self.per)
        self.i, self.k = i, 0

    def then(self, ins):
        self.k += 1
        ins.then_inc(self.sem, 1)
        self.eng.wait_ge(self.sem, self.i * self.per + self.k)


def pipeline(eng, n, stages, ring):
    depth = max(d for d, _ in stages)

    def emit(t):
        for d, body in stages:
            if 0 <= t - d < n:
                body(t - d, (t - d) % ring, (t - d) // ring)

    first = -(-(depth + ring) // ring)
    last = n // ring
    for t in range(min(first, last) * ring):
        emit(t)
    if last > first:
        with eng.Fori(first, last) as lap:
            for u in range(ring):
                for d, body in stages:
                    off = u - d
                    body(lap * ring + off, off % ring, lap + off // ring)
    for t in range(max(first, last) * ring, n + depth):
        emit(t)


class Memory:

    sems = []

    def __init__(self, nc, ctx, tag):
        self.nc, self.ctx, self.tag = nc, ctx, tag

    def sb(self, name, shape, dt=F32):
        return self.ctx.enter_context(self.nc.sbuf_tensor(f"{self.tag}_{name}", shape, dt))

    def ps(self, name, shape, dt=F32):
        return self.ctx.enter_context(self.nc.psum_tensor(f"{self.tag}_{name}", shape, dt))

    def sem(self, name):
        Memory.sems.append(self.nc.alloc_semaphore(name=f"{self.tag}_{name}"))
        return Memory.sems[-1]


def zero_semaphores(nc):
    nc.clear_and_free_semaphores(Memory.sems)
    Memory.sems.clear()
    nc.all_engine_barrier()



def load_all(nc, g, dram):
    with ExitStack() as ctx:
        m = Memory(nc, ctx, "load")
        loaded, zeroed, cleared, made = m.sem("loaded"), m.sem("zeroed"), m.sem("cleared"), m.sem("made")
        zeros = m.sb("zeros", [P, 8 * D])
        block = ctx.enter_context(nc.Block())

        @block.sync
        def _(sp):
            sp.dma_start(g.consts[:], dram["consts"]).then_inc(loaded, 16)
            sp.dma_start(g.x[:], dram["x"].rearrange("b (h p) d -> p (b h) d", p=P)).then_inc(loaded, 16)
            sp.dma_start(g.w_gates[:, :, 0:E], dram["gate_t"].rearrange("(k p) e -> p k e", p=P)).then_inc(loaded, 16)
            sp.dma_start(g.w_gates[:, :, E:E + INNER], dram["shared_gate_w"].rearrange("(k p) e -> p k e", p=P)).then_inc(loaded, 16)
            sp.dma_start(g.w_gates[:, :, E + INNER:GATES], dram["shared_up_w"].rearrange("(k p) e -> p k e", p=P)).then_inc(loaded, 16)
            sp.dma_start(g.w_down[:], dram["shared_down_w"]).then_inc(loaded, 16)
            sp.dma_start(g.norm_w[:], dram["norm_w"].rearrange("(a d) -> a d", a=1).broadcast_to([P, D])).then_inc(loaded, 16)
            for e in range(0, E, 8):
                sp.dma_start(g.w13[:, e:e + 8], dram["w13"][e:e + 8].rearrange("e (k p) f -> p e k f", p=P)).then_inc(loaded, 16)
                sp.dma_start(g.w2[:, e:e + 8], dram["w2"][e:e + 8].rearrange("e i h -> i e h")).then_inc(loaded, 16)
            sp.wait_ge(zeroed, 1)
            for j in range(0, SLOTS, 8 * P):
                sp.dma_start(g.slots_in[j:j + 8 * P].rearrange("(r p) d -> p r d", p=P),
                             zeros[:].rearrange("p (r d) -> p r d", d=D)).then_inc(cleared, 16)
            sp.wait_ge(cleared, 16 * (SLOTS // (8 * P)))
            sp.wait_ge(loaded, 16 * (7 + 2 * (E // 8)))

        @block.vector
        def _(dve):
            nc.vector.memset(zeros[:], 0.0).then_inc(zeroed, 1)
            nc.vector.memset(g.ones[:], 1.0).then_inc(made, 1)
            nc.vector.memset(g.minus_half[:], -0.5).then_inc(made, 1)
            dve.wait_ge(made, 2)



def normalise_tile(nc, dve, g, m, i, c, count, chain):
    chain.then(nc.vector.bn_stats(m.stats[:, c], g.x[:, i, :]))
    nc.vector.memset(m.pause[:], 0)
    chain.then(nc.vector.bn_aggr(m.mv[:, c], m.stats[:, c]))
    nc.vector.tensor_scalar(m.veps[:, c:c + 1], m.mv[:, c, 1:2], LN_EPS, None, ALU.add).then_inc(m.veps_ready, 1)
    dve.wait_ge(m.rstd_ready, count + 1)
    nc.vector.tensor_scalar(m.xn[:, c], g.x[:, i, :], m.mv[:, c, 0:1], m.rstd[:, c:c + 1],
                            ALU.subtract, ALU.mult).then_inc(m.xn_ready, 1)


def norm_buffers(m):
    m.stats, m.mv, m.xn = m.sb("stats", [P, 2, 6]), m.sb("mv", [P, 2, 2]), m.sb("xn", [P, 2, D])
    m.veps, m.rstd, m.pause = m.sb("veps", [P, 2]), m.sb("rstd", [P, 2]), m.sb("pause", [P, 1], U32)
    m.veps_ready, m.rstd_ready, m.xn_ready = m.sem("veps_ready"), m.sem("rstd_ready"), m.sem("xn_ready")


def attention_a(nc, g, dram):
    WQKV = D + 2 * GA * DA
    NQK = HA + GA
    with ExitStack() as ctx:
        m = Memory(nc, ctx, "a")
        norm_buffers(m)
        w_qkv, w_o = m.sb("w_qkv", [P, KD, WQKV]), m.sb("w_o", [P, KD, D])
        pool_pause = m.sb("pool_pause", [P, 6])
        ident_b, future_b = m.sb("ident_b", [P, P], BF16), m.sb("future_b", [P, P], BF16)
        minus_group = m.sb("minus_group", [HA, GA, P], BF16)
        x_t, ctx_n, ctx_t = m.sb("x_t", [P, KD, 2, P]), m.sb("ctx_n", [P, 2, D]), m.sb("ctx_t", [P, KD, 2, P])
        by_cos, by_sin, qk = m.sb("by_cos", [P, NQK, DA]), m.sb("by_sin", [P, NQK, DA]), m.sb("qk", [P, NQK, DA])
        rest, high, mid, low = m.sb("rest", [P, NQK, DA]), m.sb("high", [P, NQK, DA], BF16), m.sb("mid", [P, NQK, DA], BF16), m.sb("low", [P, NQK, DA], BF16)
        values = m.sb("values", [P, 2, GA, DA + 1])
        q_stack, k_stack = m.sb("q_stack", [P, 2, HA, 8, DA], BF16), m.sb("k_stack", [P, 2, GA, 8, DA], BF16)
        q_t, k_t = m.sb("q_t", [P, 2, HA // 2, P], BF16), m.sb("k_t", [P, 2, GA // 2, P], BF16)
        row_max, max_t = m.sb("row_max", [P, 2, HA], BF16), m.sb("max_t", [HA, 2, REP, P], BF16)
        probs, recip = m.sb("probs", [P, 2, 3, REP, P]), m.sb("recip", [P, 2, HA])
        ps_s, ps_o = m.ps("ps_s", [P, 2, 3, 512]), m.ps("ps_o", [P, 2, 512])

        w_loaded, made, chain_sem, rope_chain = m.sem("w_loaded"), m.sem("made"), m.sem("chain"), m.sem("rope_chain")
        x_turned, x_t_ready, qkv_ready, parts_ready = m.sem("x_turned"), m.sem("x_t_ready"), m.sem("qkv_ready"), m.sem("parts_ready")
        stacked, stack_turned, stack_moved = m.sem("stacked"), m.sem("stack_turned"), m.sem("stack_moved")
        smax_ready, smax_read, max_turned, max_t_ready = m.sem("smax_ready"), m.sem("smax_read"), m.sem("max_turned"), m.sem("max_t_ready")
        s_ready, p_ready, p_masked, pv_done = m.sem("s_ready"), m.sem("p_ready"), m.sem("p_masked"), m.sem("pv_done")
        recips, ctx_ready, ctx_turned, ctx_moved = m.sem("recips"), m.sem("ctx_ready"), m.sem("ctx_turned"), m.sem("ctx_moved")
        out_ready, x_added = m.sem("out_ready"), m.sem("x_added")
        ident = g.const("ident")
        block = ctx.enter_context(nc.Block())

        def stacks_bank(n):
            return ps_s[:, 1, n, :].bitcast(BF16)

        @block.sync
        def _(sp):
            sp.dma_start(w_qkv[:], dram["a_Wqkv"].rearrange("(k p) n -> p k n", p=P)).then_inc(w_loaded, 16)
            sp.dma_start(w_o[:], dram["a_Wo"].rearrange("(k p) n -> p k n", p=P)).then_inc(w_loaded, 16)
            sp.wait_ge(w_loaded, 32)

        @block.gpsimd
        def _(pool):
            def batch(b, s, lap):
                for c in range(2):
                    pool.wait_ge(m.veps_ready, b * 2 + c + 1)
                    nc.gpsimd.tensor_tensor(m.rstd[:, c:c + 1], m.veps[:, c:c + 1], g.minus_half[:], ALU.pow).then_inc(m.rstd_ready, 1)
                for c in range(2):
                    pool.wait_ge(parts_ready, b * 2 + c + 1)
                    wait(pool, stack_turned, b * 6)
                    nc.gpsimd.tensor_tensor(pool_pause[:, 4 + c:5 + c], g.minus_half[:], g.minus_half[:], ALU.add)
                    for n, (part, roles) in enumerate(((high, (0, 3)), (mid, (3, 6)), (low, (6, 8)))):
                        width = roles[1] - roles[0]
                        nc.gpsimd.tensor_copy(q_stack[:, c, :, roles[0]:roles[1], :],
                                              part[:, 0:HA].rearrange("p h (o d) -> p h o d", o=1).broadcast_to([P, HA, width, DA]))
                        width = len(range(n, 8, 3))
                        last = nc.gpsimd.tensor_copy(k_stack[:, c, :, n:8:3, :],
                                                     part[:, HA:].rearrange("p h (o d) -> p h o d", o=1).broadcast_to([P, GA, width, DA]))
                    last.then_inc(stacked, 1)
                for k in range(GA):
                    pool.wait_ge(p_ready, b * GA + k + 1)
                    nc.gpsimd.tensor_tensor(pool_pause[:, k % 4:k % 4 + 1], g.minus_half[:], g.minus_half[:], ALU.add)
                    view = probs[:, k % 2, 0:3:2]
                    nc.gpsimd.affine_select(out=view, in_=view, compare_op=ALU.is_ge, fill=0.0, base=0,
                                            pattern=[[0, 2], [0, REP], [1, P]], channel_multiplier=-1).then_inc(p_masked, 1)

            pipeline(pool, B, [(0, batch)], 1)

        @block.tensor
        def _(pe):
            pe.wait_ge(made, 4)
            pe.wait_ge(w_loaded, 32)

            def batch(b, s, lap):
                pe.wait_ge(m.xn_ready, b * 2 + 2)
                for c in range(2):
                    for k in range(KD):
                        last = nc.tensor.transpose(ps_s[:, 0, 0, (k * 2 + c) * P:(k * 2 + c + 1) * P], m.xn[:, c, k * P:(k + 1) * P], ident)
                last.then_inc(x_turned, 1)
                pe.wait_ge(x_t_ready, b + 1)
                wait(pe, x_added, b * 2)
                for c in range(2):
                    for k in range(KD):
                        last = nc.tensor.matmul(ps_s[:, 0, 1 + c, 0:WQKV], x_t[:, k, c], w_qkv[:, k, :], start=(k == 0), stop=(k == KD - 1))
                    last.then_inc(qkv_ready, 1)
                for c in range(2):
                    pe.wait_ge(stacked, b * 2 + c + 1)
                    for bank in range(3):
                        if c == 1:
                            pe.wait_ge(stack_moved, b * 6 + bank + 1)
                        for n in range(8 if bank < 2 else 4):
                            src = (q_stack[:, c, (bank * 8 + n) * 2:(bank * 8 + n) * 2 + 2] if bank < 2
                                   else k_stack[:, c, n * 2:n * 2 + 2])
                            last = nc.tensor.transpose(stacks_bank(bank)[:, n * P:(n + 1) * P], src.rearrange("p h r d -> p (h r d)"), ident_b[:])
                        last.then_inc(stack_turned, 1)
                pe.wait_ge(stack_moved, b * 6 + 6)
                for k in range(GA):
                    rows, gp = slice(STACK * (k % 2), STACK * (k % 2) + STACK), k // 2
                    if k >= 2:
                        pe.wait_ge(smax_read, b * GA + k - 1)
                    for c in range(2):
                        for half in range(c + 1):
                            bank = ps_s[:, k % 2, c + half, :].rearrange("p (r s) -> p r s", s=(c + 1) * P)
                            reps = bank.shape[1]
                            for r in range(reps):
                                nc.tensor.matmul(bank[:, r], q_t[rows, c, gp * REP + half * reps + r], k_t[rows, 0:c + 1, gp],
                                                 start=(r == 0), stop=False)
                            last = nc.tensor.matmul(bank[:, :, c * P:(c + 1) * P], ident_b[:],
                                                    future_b[:].rearrange("p (o s) -> p o s", o=1).broadcast_to([P, reps, P]),
                                                    start=False, stop=True)
                    last.then_inc(smax_ready, 1)
                pe.wait_ge(smax_read, b * GA + GA)
                for c in range(2):
                    last = nc.tensor.transpose(ps_s[0:HA, 0, 0, :].bitcast(BF16)[:, c * P:(c + 1) * P], row_max[:, c], ident_b[:])
                last.then_inc(max_turned, 1)
                pe.wait_ge(max_t_ready, b + 1)
                wait(pe, ctx_ready, b)

                def scores(k):
                    rows, gp = slice(STACK * (k % 2), STACK * (k % 2) + STACK), k // 2
                    if k >= 2:
                        pe.wait_ge(p_ready, b * GA + k - 1)
                    for bank, (s_blk, t_blk) in enumerate(((0, 0), (0, 1), (1, 1))):
                        nc.tensor.matmul(ps_s[:, k % 2, bank], k_t[rows, s_blk, gp], q_t[rows, t_blk, gp * REP:(gp + 1) * REP],
                                         start=True, stop=False)
                        last = nc.tensor.matmul(ps_s[:, k % 2, bank], minus_group[:, k], max_t[:, t_blk], start=False, stop=True)
                    last.then_inc(s_ready, 1)

                def weigh(k):
                    pe.wait_ge(p_masked, b * GA + k + 1)
                    for r in range(REP):
                        at = (k * REP + r) * (DA + 1)
                        nc.tensor.matmul(ps_o[:, 0, at:at + DA + 1], probs[:, k % 2, 0, r], values[:, 0, k], start=True, stop=True)
                        nc.tensor.matmul(ps_o[:, 1, at:at + DA + 1], probs[:, k % 2, 1, r], values[:, 0, k], start=True, stop=False)
                        last = nc.tensor.matmul(ps_o[:, 1, at:at + DA + 1], probs[:, k % 2, 2, r], values[:, 1, k], start=False, stop=True)
                    last.then_inc(pv_done, 1)

                for k in range(GA + 1):
                    if k < GA:
                        scores(k)
                    if k:
                        weigh(k - 1)
                pe.wait_ge(ctx_ready, b + 1)
                for c in range(2):
                    for k in range(KD):
                        last = nc.tensor.transpose(ps_s[:, 0, 0, (k * 2 + c) * P:(k * 2 + c + 1) * P], ctx_n[:, c, k * P:(k + 1) * P], ident)
                last.then_inc(ctx_turned, 1)
                pe.wait_ge(ctx_moved, b + 1)
                for c in range(2):
                    for k in range(KD):
                        last = nc.tensor.matmul(ps_s[:, 0, 1 + c, 0:D], ctx_t[:, k, c], w_o[:, k, :], start=(k == 0), stop=(k == KD - 1))
                    last.then_inc(out_ready, 1)

            pipeline(pe, B, [(0, batch)], 1)

        @block.scalar
        def _(act):
            def batch(b, s, lap):
                act.wait_ge(x_turned, b + 1)
                nc.scalar.copy(x_t[:].rearrange("p k c t -> p (k c t)"), ps_s[:, 0, 0, :]).then_inc(x_t_ready, 1)
                for c in range(2):
                    for bank in range(3):
                        act.wait_ge(stack_turned, b * 6 + c * 3 + bank + 1)
                        dst = q_t[:, c, bank * 8:bank * 8 + 8] if bank < 2 else k_t[:, c]
                        n = 8 if bank < 2 else 4
                        nc.scalar.copy(dst, stacks_bank(bank)[:, 0:n * P].rearrange("p (n t) -> p n t", t=P)).then_inc(stack_moved, 1)
                for k in range(GA):
                    act.wait_ge(s_ready, b * GA + k + 1)
                    wait(act, pv_done, b * GA + k - 1)
                    nc.scalar.activation(probs[:, k % 2].rearrange("p b r t -> p b (r t)"), ps_s[:, k % 2], ACT.Exp,
                                         scale=float(DA) ** -0.5).then_inc(p_ready, 1)
                act.wait_ge(ctx_turned, b + 1)
                nc.scalar.copy(ctx_t[:].rearrange("p k c t -> p (k c t)"), ps_s[:, 0, 0, :]).then_inc(ctx_moved, 1)

            pipeline(act, B, [(0, batch)], 1)

        @block.vector
        def _(dve):
            nc.vector.tensor_copy(ident_b[:], ident).then_inc(made, 1)
            nc.vector.tensor_copy(future_b[:], g.const("future")).then_inc(made, 1)
            nc.vector.tensor_copy(minus_group[:], g.const("minus_group")[0:HA].rearrange("p (g o) -> p g o", o=1).broadcast_to([HA, GA, P])).then_inc(made, 1)
            nc.vector.memset(values[:, :, :, DA:], 1.0).then_inc(made, 1)
            norm, rope = Chain(dve, chain_sem, 4), Chain(dve, rope_chain, 12)

            def batch(b, s, lap):
                norm.at(b)
                wait(dve, x_turned, b)
                for c in range(2):
                    normalise_tile(nc, dve, g, m, b * 2 + c, c, b * 2 + c, norm)
                rope.at(b)
                for c in range(2):
                    dve.wait_ge(qkv_ready, b * 2 + c + 1)
                    wait(dve, stacked, b * 2 + c)
                    src = ps_s[:, 0, 1 + c, 0:NQK * DA].rearrange("p (h d) -> p h d", d=DA)
                    cos = g.const("cos_a")[:, c * DA:(c + 1) * DA].rearrange("p (o d) -> p o d", o=1)
                    sin = g.const("sin_a")[:, c * DA:(c + 1) * DA].rearrange("p (o d) -> p o d", o=1)
                    half = DA // 2
                    nc.vector.tensor_tensor(by_cos[:], src, cos.broadcast_to([P, NQK, DA]), ALU.mult)
                    nc.vector.tensor_tensor(by_sin[:, :, 0:half], src[:, :, half:], sin[:, :, 0:half].broadcast_to([P, NQK, half]), ALU.mult)
                    nc.vector.tensor_tensor(by_sin[:, :, half:], src[:, :, 0:half], sin[:, :, half:].broadcast_to([P, NQK, half]), ALU.mult)
                    rope.then(nc.vector.tensor_copy(values[:, c, :, 0:DA], ps_s[:, 0, 1 + c, NQK * DA:WQKV].rearrange("p (h d) -> p h d", d=DA)))
                    rope.then(nc.vector.tensor_tensor(qk[:], by_cos[:], by_sin[:], ALU.add))
                    rope.then(nc.vector.tensor_copy(high[:], qk[:]))
                    rope.then(nc.vector.tensor_tensor(rest[:], qk[:], high[:], ALU.subtract))
                    rope.then(nc.vector.tensor_copy(mid[:], rest[:]))
                    rope.then(nc.vector.tensor_tensor(low[:], rest[:], mid[:], ALU.subtract))
                    nc.vector.memset(m.pause[:], 0).then_inc(parts_ready, 1)
                for k in range(GA):
                    dve.wait_ge(smax_ready, b * GA + k + 1)
                    nc.vector.tensor_reduce(row_max[:, 0, k * REP:(k + 1) * REP], ps_s[:, k % 2, 0].rearrange("p (r s) -> p r s", s=P), AX.X, ALU.max)
                    nc.vector.tensor_reduce(row_max[:, 1, k * REP:(k + 1) * REP],
                                            ps_s[:, k % 2, 1:3].rearrange("p b n -> p (b n)").rearrange("p (r s) -> p r s", s=2 * P),
                                            AX.X, ALU.max).then_inc(smax_read, 1)
                dve.wait_ge(max_turned, b + 1)
                for r in range(REP):
                    last = nc.vector.tensor_scalar(max_t[:, :, r], ps_s[0:HA, 0, 0, :].bitcast(BF16)[:, 0:2 * P].rearrange("p (c t) -> p c t", c=2),
                                                   g.const("row_mod")[0:HA, r:r + 1], None, ALU.mult)
                last.then_inc(max_t_ready, 1)
                dve.wait_ge(pv_done, b * GA + GA)
                out = ps_o[:, :, 0:HA * (DA + 1)].rearrange("p c (h d) -> p c h d", d=DA + 1)
                nc.vector.reciprocal(recip[:], out[:, :, :, DA]).then_inc(recips, 1)
                dve.wait_ge(recips, b + 1)
                for c in range(2):
                    last = nc.vector.tensor_tensor(ctx_n[:, c].rearrange("p (h d) -> p h d", d=DA), out[:, c, :, 0:DA],
                                                   recip[:, c].rearrange("p (h o) -> p h o", o=1).broadcast_to([P, HA, DA]), ALU.mult)
                last.then_inc(ctx_ready, 1)
                for c in range(2):
                    dve.wait_ge(out_ready, b * 2 + c + 1)
                    nc.vector.tensor_tensor(g.x[:, b * 2 + c, :], g.x[:, b * 2 + c, :], ps_s[:, 0, 1 + c, 0:D], ALU.add).then_inc(x_added, 1)

            pipeline(dve, B, [(0, batch)], 1)
            dve.wait_ge(x_added, 2 * B)





RMS_EPS_B = float(np.finfo(np.float32).eps)
PAIRS = HB // 2
HEAD_GROUP = 8


def attention_b_weights(nc, g, w, dram):
    with ExitStack() as ctx:
        m = Memory(nc, ctx, "b_weights")
        wqn_t, wk_t = m.sb("wqn_t", [NOPE, HB, QR]), m.sb("wk_t", [NOPE, HB, KVR])
        wv_t, wo, q_norm = m.sb("wv_t", [VD, HB, KVR]), m.sb("wo", [VD, HB, D]), m.sb("q_norm", [QR, 1])
        ps = m.ps("ps", [P, 6, 512])
        loaded, kept, multiplied, moved = m.sem("loaded"), m.sem("kept"), m.sem("multiplied"), m.sem("moved")
        block = ctx.enter_context(nc.Block())

        @block.sync
        def _(sp):
            sp.dma_start(wqn_t[:], dram["b_wqn_t"]).then_inc(loaded, 16)
            sp.dma_start(wk_t[:], dram["b_wk_t"]).then_inc(loaded, 16)
            sp.dma_start(wv_t[:], dram["b_wv_t"]).then_inc(loaded, 16)
            sp.dma_start(wo[:], dram["b_wo"].rearrange("(h v) n -> v h n", v=VD)).then_inc(loaded, 16)
            sp.dma_start(q_norm[:], dram["b_q_a_norm_w"].rearrange("(p a) -> p a", a=1)).then_inc(loaded, 16)
            sp.dma_start(w.wq[:, :, 0:ROPE], dram["b_wqp"]).then_inc(loaded, 16)
            sp.dma_start(w.w_a[:], dram["b_w_a"].rearrange("(k p) n -> p k n", p=P)).then_inc(loaded, 16)
            sp.dma_start(w.kv_norm[:], dram["b_kv_a_norm_w"].rearrange("(a d) -> a d", a=1).broadcast_to([P, KVR])).then_inc(loaded, 16)
            sp.wait_ge(loaded, 128)

        @block.tensor
        def _(pe):
            pe.wait_ge(loaded, 128)
            for h in range(HB):
                nc.tensor.matmul(ps[0:QR, h // 8, (h % 8) * KVR:(h % 8 + 1) * KVR], wqn_t[:, h], wk_t[:, h], start=True, stop=True)
            for h in range(HB):
                half = slice(KVR * (h % 2), KVR * (h % 2) + KVR)
                last = nc.tensor.matmul(ps[half, 2 + h // 4, (h // 2 % 2) * D:(h // 2 % 2 + 1) * D], wv_t[:, h], wo[:, h], start=True, stop=True)
            last.then_inc(multiplied, 1)

        @block.vector
        def _(dve):
            dve.wait_ge(multiplied, 1)
            nc.vector.tensor_copy(w.wvo[:].rearrange("p h n -> p (h n)"), ps[:, 2:6].rearrange("p b n -> p (b n)"))
            nc.vector.tensor_copy(w.wq[:, :, ROPE:], ps[0:QR, 0:2].rearrange("p b n -> p (b n)").rearrange("p (h c) -> p h c", c=KVR)).then_inc(moved, 1)
            dve.wait_ge(moved, 1)
            nc.vector.tensor_scalar(w.wq[:], w.wq[:], q_norm[:, 0:1], None, ALU.mult).then_inc(kept, 1)
            nc.vector.tensor_copy(w.ident_b[:], g.const("ident")).then_inc(kept, 1)
            nc.vector.tensor_copy(w.minus_head[:], g.const("ident")[0:HB, 0:HB].rearrange("p (h o) -> p h o", o=1).broadcast_to([HB, HB, P])).then_inc(kept, 1)
            dve.wait_ge(kept, 3)
            nc.vector.tensor_scalar(w.minus_head[:], w.minus_head[:], -1.0, None, ALU.mult).then_inc(kept, 1)
            nc.vector.memset(w.keys[:, :, DK:], 1.0).then_inc(kept, 1)
            dve.wait_ge(kept, 5)


def attention_b(nc, g, dram):
    NA = QR + KVR + ROPE
    with ExitStack() as ctx:
        m = Memory(nc, ctx, "b")
        norm_buffers(m)
        m.w_a, m.wq, m.wvo = m.sb("w_a", [P, KD, NA]), m.sb("wq", [QR, HB, DK]), m.sb("wvo", [P, PAIRS, D])
        m.kv_norm, m.ident_b, m.minus_head = m.sb("kv_norm", [P, KVR]), m.sb("ident_b", [P, P], BF16), m.sb("minus_head", [HB, HB, P], BF16)
        m.keys = m.sb("keys", [P, 2, DK + 1])
        attention_b_weights(nc, g, m, dram)
        x_t, junk, sums = m.sb("x_t", [P, KD, 2, P]), m.sb("junk", [P, QR]), m.sb("sums", [P, 2, 2])
        means, inverse, q_low = m.sb("means", [P, 2, 2]), m.sb("inverse", [P, 2, 2]), m.sb("q_low", [P, 2, QR])
        by_cos, by_sin = m.sb("by_cos", [P, 2, HEAD_GROUP, ROPE]), m.sb("by_sin", [P, 2, HEAD_GROUP, ROPE])
        k_cos, k_sin = m.sb("k_cos", [P, 2, ROPE]), m.sb("k_sin", [P, 2, ROPE])
        q_low_t, k_t, k_tb = m.sb("q_low_t", [QR, 2, P]), m.sb("k_t", [P, 2, P]), m.sb("k_tb", [P, 2, P], BF16)
        queries, q_t, q_tb = m.sb("queries", [P, 2, HEAD_GROUP, DK]), m.sb("q_t", [P, HB, 2, P]), m.sb("q_tb", [P, HB, 2, P], BF16)
        row_max, max_t = m.sb("row_max", [P, 2, HB], BF16), m.sb("max_t", [HB, 2 * P], BF16)
        probs, recip = m.sb("probs", [P, 2, 2, 2, 2 * P]), m.sb("recip", [P, 2, 2, 2, 1])
        ctx_n, ctx_t = m.sb("ctx_n", [P, 2, 2, 2, KVR]), m.sb("ctx_t", [P, 2, 2, P])
        ps_s, ps_o, ps_c, ps_y = m.ps("ps_s", [P, 2, 2, 512]), m.ps("ps_o", [P, 2, 512]), m.ps("ps_c", [P, 512]), m.ps("ps_y", [P, 512])

        chain_sem, low_chain, rope_sem = m.sem("chain"), m.sem("low_chain"), m.sem("rope")
        x_turned, x_t_ready, low_ready, sums_ready = m.sem("x_turned"), m.sem("x_t_ready"), m.sem("low_ready"), m.sem("sums_ready")
        means_ready, inverse_ready, keys_ready, low_turned = m.sem("means_ready"), m.sem("inverse_ready"), m.sem("keys_ready"), m.sem("low_turned")
        low_t_ready, q_made, q_rotated, q_ready = m.sem("low_t_ready"), m.sem("q_made"), m.sem("q_rotated"), m.sem("q_ready")
        q_turned, q_t_ready, q_tb_ready = m.sem("q_turned"), m.sem("q_t_ready"), m.sem("q_tb_ready")
        smax_ready, smax_read, max_turned, max_t_ready = m.sem("smax_ready"), m.sem("smax_read"), m.sem("max_turned"), m.sem("max_t_ready")
        s_ready, p_ready, pv_done, recips = m.sem("s_ready"), m.sem("p_ready"), m.sem("pv_done"), m.sem("recips")
        ctx_ready, ctx_turned, ctx_moved, y_ready, x_added = m.sem("ctx_ready"), m.sem("ctx_turned"), m.sem("ctx_moved"), m.sem("y_ready"), m.sem("x_added")
        ident = g.const("ident")
        block = ctx.enter_context(nc.Block())

        def skewed(first, second):
            for u in range(5):
                if u < 4:
                    first(u)
                if u:
                    second(u - 1)

        @block.gpsimd
        def _(pool):
            def batch(b, s, lap):
                for c in range(2):
                    pool.wait_ge(m.veps_ready, b * 2 + c + 1)
                    nc.gpsimd.tensor_tensor(m.rstd[:, c:c + 1], m.veps[:, c:c + 1], g.minus_half[:], ALU.pow).then_inc(m.rstd_ready, 1)
                for c in range(2):
                    pool.wait_ge(means_ready, b * 2 + c + 1)
                    nc.gpsimd.tensor_tensor(inverse[:, c], means[:, c], g.minus_half[:].broadcast_to([P, 2]), ALU.pow).then_inc(inverse_ready, 1)

            pipeline(pool, B, [(0, batch)], 1)

        @block.tensor
        def _(pe):
            def batch(b, s, lap):
                pe.wait_ge(m.xn_ready, b * 2 + 2)
                for c in range(2):
                    for k in range(KD):
                        last = nc.tensor.transpose(ps_s[:, 0, 0, (k * 2 + c) * P:(k * 2 + c + 1) * P], m.xn[:, c, k * P:(k + 1) * P], ident)
                last.then_inc(x_turned, 1)
                pe.wait_ge(x_t_ready, b + 1)
                for c in range(2):
                    for k in range(KD):
                        last = nc.tensor.matmul(ps_s[:, 1, c, 0:NA], x_t[:, k, c], m.w_a[:, k, :], start=(k == 0), stop=(k == KD - 1))
                    last.then_inc(low_ready, 1)
                pe.wait_ge(keys_ready, b * 2 + 2)
                for c in range(2):
                    nc.tensor.transpose(ps_s[0:QR, 0, 0, c * P:(c + 1) * P], q_low[:, c], ident)
                    last = nc.tensor.transpose(ps_s[:, 0, 1, c * P:(c + 1) * P], m.keys[:, c, 0:DK], ident)
                last.then_inc(low_turned, 1)
                pe.wait_ge(low_t_ready, b + 1)

                def make(u):
                    c, half = u // 2, u % 2
                    if u >= 2:
                        pe.wait_ge(q_ready, b * 4 + u - 1)
                    for n in range(2):
                        h = half * HEAD_GROUP + n * 4
                        last = nc.tensor.matmul(ps_s[:, u % 2, n], q_low_t[:, c], m.wq[:, h:h + 4, :].rearrange("p h d -> p (h d)"), start=True, stop=True)
                    last.then_inc(q_made, 1)

                def turn(u):
                    pe.wait_ge(q_ready, b * 4 + u + 1)
                    if u >= 1:
                        pe.wait_ge(q_t_ready, b * 4 + u)
                    for n in range(HEAD_GROUP):
                        last = nc.tensor.transpose(ps_o[:, n // 4, (n % 4) * P:(n % 4 + 1) * P], queries[:, u % 2, n], ident)
                    last.then_inc(q_turned, 1)

                skewed(make, turn)
                pe.wait_ge(q_tb_ready, b * 4 + 4)
                for j in range(PAIRS):
                    if j >= 2:
                        pe.wait_ge(smax_read, b * PAIRS + j - 1)
                    for c in range(2):
                        for n in range(2):
                            last = nc.tensor.matmul(ps_s[:, j % 2, c, n * T:(n + 1) * T], q_tb[:, j * 2 + n, c], k_tb[:].rearrange("p c s -> p (c s)"), start=True, stop=True)
                    last.then_inc(smax_ready, 1)
                pe.wait_ge(smax_read, b * PAIRS + PAIRS)
                for c in range(2):
                    last = nc.tensor.transpose(ps_s[0:HB, 0, 0, :].bitcast(BF16)[:, c * P:(c + 1) * P], row_max[:, c], m.ident_b[:])
                last.then_inc(max_turned, 1)
                pe.wait_ge(max_t_ready, b + 1)
                wait(pe, x_added, b)

                def scores(j):
                    if j >= 2:
                        pe.wait_ge(p_ready, b * PAIRS + j - 1)
                    for n in range(2):
                        h = j * 2 + n
                        for s_blk in range(2):
                            nc.tensor.matmul(ps_s[:, j % 2, n, s_blk * T:(s_blk + 1) * T], k_t[:, s_blk], q_t[:, h].rearrange("p c t -> p (c t)"),
                                             start=(s_blk == 0), stop=False)
                        last = nc.tensor.matmul(ps_s[:, j % 2, n].rearrange("p (a t) -> p a t", a=2), m.minus_head[:, h],
                                                max_t[:].rearrange("p (a t) -> p a t", a=1).broadcast_to([HB, 2, T]), start=False, stop=True)
                    last.then_inc(s_ready, 1)

                def weigh(j):
                    pe.wait_ge(p_ready, b * PAIRS + j + 1)
                    if j >= 2:
                        pe.wait_ge(ctx_ready, b * PAIRS + j - 1)
                    for c in range(2):
                        for n in range(2):
                            at = (c * 2 + n) * (KVR + 1)
                            for s_blk in range(2):
                                last = nc.tensor.matmul(ps_o[:, j % 2, at:at + KVR + 1], probs[:, j % 2, n, s_blk, c * P:(c + 1) * P],
                                                        m.keys[:, s_blk, ROPE:], start=(s_blk == 0), stop=(s_blk == 1))
                    last.then_inc(pv_done, 1)

                def turn_ctx(j):
                    pe.wait_ge(ctx_ready, b * PAIRS + j + 1)
                    if j >= 1:
                        pe.wait_ge(ctx_moved, b * PAIRS + j)
                    for c in range(2):
                        last = nc.tensor.transpose(ps_c[:, c * P:(c + 1) * P], ctx_n[:, j % 2, c].rearrange("p n d -> p (n d)"), ident)
                    last.then_inc(ctx_turned, 1)

                def project(j):
                    pe.wait_ge(ctx_moved, b * PAIRS + j + 1)
                    for c in range(2):
                        last = nc.tensor.matmul(ps_y[:, c * D:(c + 1) * D], ctx_t[:, j % 2, c], m.wvo[:, j, :],
                                                start=(j == 0 and c == 0), stop=(j == PAIRS - 1 and c == 1))
                    if j == PAIRS - 1:
                        last.then_inc(y_ready, 1)

                for j in range(PAIRS + 3):
                    for delay, part in enumerate((scores, weigh, turn_ctx, project)):
                        if 0 <= j - delay < PAIRS:
                            part(j - delay)

            pipeline(pe, B, [(0, batch)], 1)

        @block.scalar
        def _(act):
            def batch(b, s, lap):
                act.wait_ge(x_turned, b + 1)
                nc.scalar.copy(x_t[:].rearrange("p k c t -> p (k c t)"), ps_s[:, 0, 0, :]).then_inc(x_t_ready, 1)
                for c in range(2):
                    act.wait_ge(low_ready, b * 2 + c + 1)
                    wait(act, sums_ready, b * 4 + c * 2)
                    nc.scalar.activation(junk[:], ps_s[:, 1, c, 0:QR], ACT.Square, accum_out=sums[:, c, 0:1]).then_inc(sums_ready, 1)
                    act.wait_ge(sums_ready, b * 4 + c * 2 + 1)
                    nc.scalar.activation(junk[:, 0:KVR], ps_s[:, 1, c, QR:QR + KVR], ACT.Square, accum_out=sums[:, c, 1:2]).then_inc(sums_ready, 1)
                act.wait_ge(low_turned, b + 1)
                nc.scalar.copy(q_low_t[:].rearrange("p c t -> p (c t)"), ps_s[0:QR, 0, 0, 0:2 * P])
                nc.scalar.copy(k_t[:].rearrange("p c t -> p (c t)"), ps_s[:, 0, 1, 0:2 * P])
                nc.scalar.copy(k_tb[:].rearrange("p c t -> p (c t)"), ps_s[:, 0, 1, 0:2 * P]).then_inc(low_t_ready, 1)

                def plain(u):
                    act.wait_ge(q_rotated, b * 4 + u + 1)
                    nc.scalar.copy(queries[:, u % 2, :, ROPE:], ps_s[:, u % 2].rearrange("p b n -> p (b n)").rearrange("p (h d) -> p h d", d=DK)[:, :, ROPE:]).then_inc(q_ready, 1)

                def move(u):
                    c, half = u // 2, u % 2
                    act.wait_ge(q_turned, b * 4 + u + 1)
                    nc.scalar.copy(q_t[:, half * HEAD_GROUP:(half + 1) * HEAD_GROUP, c], ps_o[:].rearrange("p b n -> p (b n)").rearrange("p (h t) -> p h t", t=P)).then_inc(q_t_ready, 1)

                skewed(plain, move)

                def exponential(j):
                    act.wait_ge(s_ready, b * PAIRS + j + 1)
                    wait(act, pv_done, b * PAIRS + j - 1)
                    nc.scalar.activation(probs[:, j % 2].rearrange("p n a t -> p n (a t)"), ps_s[:, j % 2], ACT.Exp,
                                         scale=float(DK) ** -0.5).then_inc(p_ready, 1)

                def move_ctx(j):
                    act.wait_ge(ctx_turned, b * PAIRS + j + 1)
                    nc.scalar.copy(ctx_t[:, j % 2].rearrange("p c t -> p (c t)"), ps_c[:, 0:2 * P]).then_inc(ctx_moved, 1)

                for j in range(PAIRS + 2):
                    if j < PAIRS:
                        exponential(j)
                    if j >= 2:
                        move_ctx(j - 2)

            pipeline(act, B, [(0, batch)], 1)

        @block.vector
        def _(dve):
            norm, low = Chain(dve, chain_sem, 4), Chain(dve, low_chain, 2)

            def batch(b, s, lap):
                norm.at(b)
                wait(dve, x_turned, b)
                for c in range(2):
                    normalise_tile(nc, dve, g, m, b * 2 + c, c, b * 2 + c, norm)
                low.at(b)
                cos, sin = (g.const(name).rearrange("p (c o d) -> p c o d", c=2, o=1) for name in ("cos_b", "sin_b"))
                half = ROPE // 2
                for c in range(2):
                    dve.wait_ge(sums_ready, b * 4 + c * 2 + 2)
                    nc.vector.tensor_scalar(means[:, c, 0:1], sums[:, c, 0:1], 1.0 / QR, RMS_EPS_B, ALU.mult, ALU.add)
                    nc.vector.tensor_scalar(means[:, c, 1:2], sums[:, c, 1:2], 1.0 / KVR, RMS_EPS_B, ALU.mult, ALU.add).then_inc(means_ready, 1)
                    src = ps_s[:, 1, c, QR + KVR:NA]
                    nc.vector.tensor_tensor(k_cos[:, c], src, cos[:, c, 0], ALU.mult)
                    nc.vector.tensor_tensor(k_sin[:, c, 0:half], src[:, half:], sin[:, c, 0, 0:half], ALU.mult)
                    low.then(nc.vector.tensor_tensor(k_sin[:, c, half:], src[:, 0:half], sin[:, c, 0, half:], ALU.mult))
                    nc.vector.tensor_tensor(m.keys[:, c, 0:ROPE], k_cos[:, c], k_sin[:, c], ALU.add)
                    dve.wait_ge(inverse_ready, b * 2 + c + 1)
                    nc.vector.tensor_scalar(q_low[:, c], ps_s[:, 1, c, 0:QR], inverse[:, c, 0:1], None, ALU.mult)
                    nc.vector.scalar_tensor_tensor(out=m.keys[:, c, ROPE:DK], in0=ps_s[:, 1, c, QR:QR + KVR], scalar=inverse[:, c, 1:2],
                                                   in1=m.kv_norm[:], op0=ALU.mult, op1=ALU.mult).then_inc(keys_ready, 1)

                def rotate(u):
                    c = u // 2
                    dve.wait_ge(q_made, b * 4 + u + 1)
                    wait(dve, q_turned, b * 4 + u - 1)
                    src = ps_s[:, u % 2].rearrange("p b n -> p (b n)").rearrange("p (h d) -> p h d", d=DK)
                    nc.vector.tensor_tensor(by_cos[:, u % 2], src[:, :, 0:ROPE], cos[:, c].broadcast_to([P, HEAD_GROUP, ROPE]), ALU.mult)
                    nc.vector.tensor_tensor(by_sin[:, u % 2, :, 0:half], src[:, :, half:ROPE], sin[:, c, :, 0:half].broadcast_to([P, HEAD_GROUP, half]), ALU.mult)
                    nc.vector.tensor_tensor(by_sin[:, u % 2, :, half:], src[:, :, 0:half], sin[:, c, :, half:].broadcast_to([P, HEAD_GROUP, half]), ALU.mult).then_inc(rope_sem, 1)
                    dve.wait_ge(rope_sem, b * 4 + u + 1)
                    nc.vector.tensor_tensor(queries[:, u % 2, :, 0:ROPE], by_cos[:, u % 2], by_sin[:, u % 2], ALU.add).then_inc(q_rotated, 1)

                def narrow(u):
                    c, group = u // 2, u % 2
                    dve.wait_ge(q_t_ready, b * 4 + u + 1)
                    heads = slice(group * HEAD_GROUP, (group + 1) * HEAD_GROUP)
                    nc.vector.tensor_copy(q_tb[:, heads, c], q_t[:, heads, c]).then_inc(q_tb_ready, 1)

                skewed(rotate, narrow)
                for j in range(PAIRS):
                    dve.wait_ge(smax_ready, b * PAIRS + j + 1)
                    nc.vector.tensor_reduce(row_max[:, :, j * 2:j * 2 + 2], ps_s[:, j % 2].rearrange("p c (n s) -> p c n s", n=2), AX.X, ALU.max).then_inc(smax_read, 1)
                dve.wait_ge(max_turned, b + 1)
                nc.vector.tensor_copy(max_t[:], ps_s[0:HB, 0, 0, :].bitcast(BF16)[:, 0:2 * P]).then_inc(max_t_ready, 1)
                for j in range(PAIRS):
                    dve.wait_ge(pv_done, b * PAIRS + j + 1)
                    out = ps_o[:, j % 2, 0:4 * (KVR + 1)].rearrange("p (c n d) -> p c n d", c=2, n=2)
                    nc.vector.reciprocal(recip[:, j % 2], out[:, :, :, KVR:]).then_inc(recips, 1)
                    dve.wait_ge(recips, b * PAIRS + j + 1)
                    wait(dve, ctx_turned, b * PAIRS + j - 1)
                    nc.vector.tensor_tensor(ctx_n[:, j % 2], out[:, :, :, 0:KVR],
                                            recip[:, j % 2].broadcast_to([P, 2, 2, KVR]),
                                            ALU.mult).then_inc(ctx_ready, 1)
                dve.wait_ge(y_ready, b + 1)
                nc.vector.tensor_tensor(g.x[:, bass.ds(b * 2, 2), :], g.x[:, bass.ds(b * 2, 2), :], ps_y[:].rearrange("p (c d) -> p c d", c=2), ALU.add).then_inc(x_added, 1)

            pipeline(dve, B, [(0, batch)], 1)
            dve.wait_ge(x_added, B)



def ffn_router(nc, g, tag):
    with ExitStack() as ctx:
        m = Memory(nc, ctx, tag + "_router")
        stats, mv = m.sb("stats", [P, 2, 6]), m.sb("mv", [P, 2, 2])
        rstd, ssq, rrms = m.sb("rstd", [P, 2]), m.sb("ssq", [P, 2]), m.sb("rrms", [P, 2])
        veps, meps, pause = m.sb("veps", [P, 2]), m.sb("meps", [P, 2]), m.sb("pause", [P, 1], U32)
        veps_ready, rstd_ready, meps_ready = m.sem("veps_ready"), m.sem("rstd_ready"), m.sem("meps_ready")
        h, junk, xin = m.sb("h", [P, 2, D]), m.sb("junk", [P, D]), m.sb("xin", [P, 2, D])
        xin_t, act_t = m.sb("xin_t", [P, 2, KD, P]), m.sb("act_t", [P, 2, P])
        silu, act = m.sb("silu", [P, 2, INNER]), m.sb("act", [P, 2, INNER])
        logits, top8, idx8 = m.sb("logits", [P, 2, E]), m.sb("top8", [P, 2, 8]), m.sb("idx8", [P, 2, 8], U32)
        ps_t, ps_g, ps_o = m.ps("ps_t", [P, 2, 512]), m.ps("ps_g", [P, 2, 512]), m.ps("ps_o", [P, 2, 512])
        norm_chain, route_chain = m.sem("norm_chain"), m.sem("route_chain")
        h_ready, ssq_ready, xin_ready, xin_kept = m.sem("h_ready"), m.sem("ssq_ready"), m.sem("xin_ready"), m.sem("xin_kept")
        turned, xin_t_ready, gates_ready, silu_ready = m.sem("turned"), m.sem("xin_t_ready"), m.sem("gates_ready"), m.sem("silu_ready")
        act_ready, act_turned, act_t_ready, down_ready = m.sem("act_ready"), m.sem("act_turned"), m.sem("act_t_ready"), m.sem("down_ready")
        logits_read, rrms_ready, x_added = m.sem("logits_read"), m.sem("rrms_ready"), m.sem("x_added")
        ident = g.const("ident")
        block = ctx.enter_context(nc.Block())

        @block.vector
        def _(dve):
            norm, route = Chain(dve, norm_chain, 3), Chain(dve, route_chain, 3)

            def normalise(i, s, lap):
                norm.at(i)
                norm.then(nc.vector.bn_stats(stats[:, s], g.x[:, i, :]))
                nc.vector.memset(pause[:], 0)
                norm.then(nc.vector.bn_aggr(mv[:, s], stats[:, s]))
                nc.vector.tensor_scalar(veps[:, s:s + 1], mv[:, s, 1:2], LN_EPS, None, ALU.add).then_inc(veps_ready, 1)
                dve.wait_ge(rstd_ready, i + 1)
                nc.vector.tensor_scalar(h[:, s], g.x[:, i, :], mv[:, s, 0:1], rstd[:, s:s + 1],
                                        ALU.subtract, ALU.mult).then_inc(h_ready, 1)
                dve.wait_ge(h_ready, i + 1)
                norm.then(nc.vector.tensor_tensor(g.x[:, i, :], g.x[:, i, :], h[:, s], ALU.add))
                dve.wait_ge(ssq_ready, i + 1)
                nc.vector.tensor_scalar(meps[:, s:s + 1], ssq[:, s:s + 1], 1.0 / D, RMS_EPS, ALU.mult, ALU.add).then_inc(meps_ready, 1)
                dve.wait_ge(rrms_ready, i + 1)
                wait(dve, turned, i - 1)
                wait(dve, xin_kept, i - 1)
                nc.vector.scalar_tensor_tensor(out=xin[:, s], in0=h[:, s], scalar=rrms[:, s:s + 1], in1=g.norm_w[:],
                                               op0=ALU.mult, op1=ALU.mult).then_inc(xin_ready, 1)

            def route_tile(i, s, lap):
                dve.wait_ge(gates_ready, i + 1)
                route.at(i)
                nc.vector.tensor_copy(logits[:, s], ps_g[:, s, 0:E]).then_inc(logits_read, 1)
                dve.wait_ge(silu_ready, i + 1)
                wait(dve, act_turned, i - 1)
                nc.vector.tensor_tensor(act[:, s], silu[:, s], ps_g[:, s, E + INNER:GATES], ALU.mult).then_inc(act_ready, 1)
                dve.wait_ge(logits_read, i + 1)
                nc.vector.memset(pause[:], 0)
                route.then(nc.vector.max(top8[:, s], logits[:, s]))
                nc.vector.memset(pause[:], 0)
                route.then(nc.vector.max_index(idx8[:, s], top8[:, s], logits[:, s]))
                nc.vector.tensor_copy(g.top[:, i, :], top8[:, s, 0:TOPK])
                route.then(nc.vector.tensor_copy(g.chosen[:, i, :], idx8[:, s, 0:TOPK]))

            def add_shared(i, s, lap):
                dve.wait_ge(down_ready, i + 1)
                nc.vector.tensor_tensor(g.x[:, i, :], g.x[:, i, :], ps_o[:, s, 0:D], ALU.add).then_inc(x_added, 1)

            pipeline(dve, TILES, [(0, normalise), (1, route_tile), (2, add_shared)], 2)
            dve.wait_ge(x_added, TILES)

        @block.gpsimd
        def _(pool):
            def keep(i, s, lap):
                pool.wait_ge(veps_ready, i + 1)
                nc.gpsimd.tensor_tensor(rstd[:, s:s + 1], veps[:, s:s + 1], g.minus_half[:], ALU.pow).then_inc(rstd_ready, 1)
                pool.wait_ge(meps_ready, i + 1)
                nc.gpsimd.tensor_tensor(rrms[:, s:s + 1], meps[:, s:s + 1], g.minus_half[:], ALU.pow).then_inc(rrms_ready, 1)
                pool.wait_ge(xin_ready, i + 1)
                nc.gpsimd.tensor_copy(g.xin[:, i, :], xin[:, s]).then_inc(xin_kept, 1)

            pipeline(pool, TILES, [(0, keep)], 2)
            pool.wait_ge(xin_kept, TILES)

        @block.scalar
        def _(act_e):
            def squares(i, s, lap):
                act_e.wait_ge(h_ready, i + 1)
                wait(act_e, ssq_ready, i)
                nc.scalar.activation(junk[:], h[:, s], ACT.Square, accum_out=ssq[:, s:s + 1]).then_inc(ssq_ready, 1)

            def move_xin(i, s, lap):
                act_e.wait_ge(turned, i + 1)
                wait(act_e, gates_ready, i - 1)
                nc.scalar.copy(xin_t[:, s], ps_t[:, s, 0:D].rearrange("p (k t) -> p k t", k=KD)).then_inc(xin_t_ready, 1)

            def gate_silu(i, s, lap):
                act_e.wait_ge(logits_read, i + 1)
                wait(act_e, act_ready, i - 1)
                nc.scalar.activation(silu[:, s], ps_g[:, s, E:E + INNER], ACT.Silu).then_inc(silu_ready, 1)

            def move_act(i, s, lap):
                act_e.wait_ge(act_turned, i + 1)
                wait(act_e, down_ready, i - 1)
                nc.scalar.copy(act_t[:, s], ps_o[:, s, D:D + P]).then_inc(act_t_ready, 1)

            pipeline(act_e, TILES, [(0, squares), (0, move_xin), (1, gate_silu), (1, move_act)], 2)

        @block.tensor
        def _(pe):
            def turn(i, s, lap):
                pe.wait_ge(xin_ready, i + 1)
                wait(pe, xin_t_ready, i - 1)
                for k in range(KD):
                    last = nc.tensor.transpose(ps_t[:, s, k * P:(k + 1) * P], xin[:, s, k * P:(k + 1) * P], ident)
                last.then_inc(turned, 1)

            def gates(i, s, lap):
                pe.wait_ge(xin_t_ready, i + 1)
                wait(pe, act_ready, i - 1)
                wait(pe, logits_read, i - 1)
                for k in range(KD):
                    last = nc.tensor.matmul(ps_g[:, s, 0:GATES], xin_t[:, s, k], g.w_gates[:, k, :], start=(k == 0), stop=(k == KD - 1))
                last.then_inc(gates_ready, 1)

            def down(i, s, lap):
                pe.wait_ge(act_ready, i + 1)
                wait(pe, x_added, i - 1)
                nc.tensor.transpose(ps_o[:, s, D:D + P], act[:, s], ident).then_inc(act_turned, 1)
                pe.wait_ge(act_t_ready, i + 1)
                nc.tensor.matmul(ps_o[:, s, 0:D], act_t[:, s], g.w_down[:], start=True, stop=True).then_inc(down_ready, 1)

            pipeline(pe, TILES, [(0, turn), (0, gates), (1, down)], 2)



def ffn_route(nc, g, tag):
    with ExitStack() as ctx:
        m = Memory(nc, ctx, tag + "_route")
        hot, prod = m.sb("hot", [P, TOPK, TILES, E]), m.sb("prod", [P, TILES, E])
        sums = [m.sb(f"sum{i}", [P, TILES, E]) for i in range(2)]
        scan = [m.sb(f"scan{i}", [P, TILES, E]) for i in range(2)]
        count, nblocks = m.sb("count", [P, E]), [m.sb(f"nblocks{i}", [P, E]) for i in range(2)]
        ends = [m.sb(f"ends{i}", [P, E]) for i in range(2)]
        base, slot, over = m.sb("base", [P, E]), m.sb("slot", [P, TILES, E]), m.sb("over", [P, TILES, E])
        passed, owner, slots = m.sb("passed", [P, E]), m.sb("owner", [P, 1]), m.sb("slots", [P, TILES, TOPK])
        kept, off, total = m.sb("kept", [P, TILES, TOPK]), m.sb("off", [P, TILES, TOPK]), m.sb("total", [P, TILES])
        ps_pos, ps_cnt = m.ps("ps_pos", [P, 512]), m.ps("ps_cnt", [P, 512])
        chain, scanned, counted, owned, turned = m.sem("chain"), m.sem("scanned"), m.sem("counted"), m.sem("owned"), m.sem("turned")
        diffs, exps = m.sem("diffs"), m.sem("exps")
        block = ctx.enter_context(nc.Block())

        @block.tensor
        def _(pe):
            pe.wait_ge(scanned, 1)
            nc.tensor.matmul(ps_pos[:], g.const("before"), sums[0][:].rearrange("p a e -> p (a e)"), start=True, stop=False)
            nc.tensor.matmul(ps_pos[:, E:], g.ones[:], scan[0][:, 0:TILES - 1].rearrange("p a e -> p (a e)"), start=False, stop=True)
            nc.tensor.matmul(ps_cnt[:, 0:E], g.ones[:], scan[0][:, TILES - 1], start=True, stop=True).then_inc(counted, 1)
            pe.wait_ge(owned, 1)
            nc.tensor.matmul(ps_cnt[0:1, P:2 * P], owner[:], g.const("ident"), start=True, stop=True).then_inc(turned, 1)

        @block.scalar
        def _(act):
            act.wait_ge(diffs, 1)
            nc.scalar.activation(off[:], off[:], ACT.Exp).then_inc(exps, 1)

        @block.vector
        def _(dve):
            link = Chain(dve, chain, 0).then
            v = nc.vector
            link(v.tensor_tensor(off[:], g.top[:], g.top[:, :, 0:1].broadcast_to([P, TILES, TOPK]), ALU.subtract))
            v.tensor_copy(passed[:, 0:1], g.consts[:, 0:1]).then_inc(diffs, 1)
            experts = g.const("experts").rearrange("p (a e) -> p a e", a=1).broadcast_to([P, TILES, E])
            for k in range(TOPK):
                link(v.tensor_tensor(hot[:, k], experts, g.chosen[:, :, k:k + 1].broadcast_to([P, TILES, E]), ALU.is_equal))
            link(v.tensor_tensor(sums[0][:], hot[:, 0], hot[:, 1], ALU.add))
            link(v.tensor_tensor(sums[1][:], sums[0][:], hot[:, 2], ALU.add))
            link(v.tensor_tensor(sums[0][:], sums[1][:], hot[:, 3], ALU.add))
            src = sums[0]
            for n, step in enumerate((1, 2, 4, 8)):
                dst = scan[(n + 1) % 2]
                link(v.tensor_copy(dst[:, 0:step], src[:, 0:step]))
                link(v.tensor_tensor(dst[:, step:], src[:, step:], src[:, 0:TILES - step], ALU.add))
                src = dst
            v.tensor_copy(passed[:, 0:1], g.consts[:, 0:1]).then_inc(scanned, 1)
            dve.wait_ge(exps, 1)
            link(v.tensor_reduce(total[:], off[:], AX.X, ALU.add))
            link(v.reciprocal(total[:], total[:]))
            link(v.tensor_tensor(g.weight[:], off[:], total[:].rearrange("p (a o) -> p a o", o=1).broadcast_to([P, TILES, TOPK]), ALU.mult))
            dve.wait_ge(counted, 1)
            link(v.tensor_copy(count[:], ps_cnt[:, 0:E]))
            link(v.tensor_scalar(nblocks[0][:], count[:], 0.0, None, ALU.is_gt))
            for n, at in enumerate(range(P, CAP, P)):
                link(v.scalar_tensor_tensor(out=nblocks[(n + 1) % 2][:], in0=count[:], scalar=float(at), in1=nblocks[n % 2][:],
                                            op0=ALU.is_gt, op1=ALU.add))
            nb = nblocks[(CAP // P - 1) % 2]
            src, step, n = nb, 1, 0
            while step < E:
                dst = ends[n % 2]
                link(v.tensor_copy(dst[:, 0:step], src[:, 0:step]))
                link(v.tensor_tensor(dst[:, step:], src[:, step:], src[:, 0:E - step], ALU.add))
                src, step, n = dst, 2 * step, n + 1
            link(v.tensor_scalar(passed[:], src[:], g.const("blocks"), None, ALU.is_le))
            link(v.tensor_reduce(owner[:], passed[:], AX.X, ALU.add))
            link(v.tensor_scalar(owner[:], owner[:], float(E - 1), None, ALU.min))
            v.tensor_copy(passed[:, 0:1], g.consts[:, 0:1]).then_inc(owned, 1)
            link(v.tensor_tensor(base[:], src[:], nb[:], ALU.subtract))
            link(v.tensor_scalar(base[:], base[:], float(P), None, ALU.mult))
            pos = ps_pos[:].rearrange("p (a e) -> p a e", e=E)
            link(v.tensor_scalar(over[:], pos, float(CAP), float(DROPPED), ALU.is_ge, ALU.mult))
            link(v.scalar_tensor_tensor(out=slot[:], in0=pos, scalar=float(CAP - 1),
                                        in1=base[:].rearrange("p (a e) -> p a e", a=1).broadcast_to([P, TILES, E]),
                                        op0=ALU.min, op1=ALU.add))
            link(v.tensor_tensor(slot[:], slot[:], over[:], ALU.add))
            for k in range(TOPK):
                link(v.tensor_tensor(prod[:], hot[:, k], slot[:], ALU.mult))
                link(v.tensor_reduce(slots[:, :, k], prod[:], AX.X, ALU.add))
            link(v.tensor_copy(g.slot_in[:], slots[:]))
            link(v.tensor_scalar(kept[:], slots[:], float(DROPPED), float(-DROPPED), ALU.is_ge, ALU.mult))
            link(v.tensor_tensor(kept[:], kept[:], slots[:], ALU.add))
            link(v.tensor_copy(g.slot_out[:], kept[:]))
            dve.wait_ge(turned, 1)
            link(v.tensor_copy(g.owner[:], ps_cnt[0:1, P:2 * P]))


def ffn_dispatch(nc, g, tag):
    with ExitStack() as ctx:
        m = Memory(nc, ctx, tag + "_dispatch")
        sent = m.sem("sent")
        block = ctx.enter_context(nc.Block())

        @block.gpsimd
        def _(pool):
            for i in range(TILES):
                for k in range(TOPK):
                    nc.gpsimd.indirect_dma_start(
                        out=g.slots_in, out_offset=bass.IndirectOffsetOnAxis(ap=g.slot_in[:, i, k:k + 1], axis=0),
                        in_=g.xin[:, i, :], in_offset=None, bounds_check=SLOTS - 1, oob_is_err=False).then_inc(sent, 16)
            pool.wait_ge(sent, 16 * TILES * TOPK)


def ffn_experts(nc, g, tag):
    with ExitStack() as ctx:
        m = Memory(nc, ctx, tag + "_experts")
        rows, rows_t = m.sb("rows", [P, RING, D]), m.sb("rows_t", [P, RING, KD, P])
        silu = m.sb("silu", [P, RING, INNER])
        act, act_t, res = m.sb("act", [P, RING, INNER]), m.sb("act_t", [P, RING, P]), m.sb("res", [P, RING, D])
        ps_t, ps_g, ps_o = m.ps("ps_t", [P, 2, 512]), m.ps("ps_g", [P, 2, 512]), m.ps("ps_o", [P, 2, 512])
        loads = [m.sem(f"loaded{r}") for r in range(RING)]
        stores = [m.sem(f"stored{r}") for r in range(RING)]
        turned, rows_t_ready, gu_ready = m.sem("turned"), m.sem("rows_t_ready"), m.sem("gu_ready")
        silu_ready, act_ready, act_turned, act_t_ready = m.sem("silu_ready"), m.sem("act_ready"), m.sem("act_turned"), m.sem("act_t_ready")
        out_ready, res_ready = m.sem("out_ready"), m.sem("res_ready")
        ident = g.const("ident")
        block = ctx.enter_context(nc.Block())

        @block.sync
        def _(sp):
            def load(j, s, lap):
                wait(sp, turned, j - RING + 1)
                sp.dma_start(rows[:, s], g.slots_in[bass.ts(j, P), :]).then_inc(loads[s], 16)

            def store(j, s, lap):
                sp.wait_ge(res_ready, j + 1)
                sp.dma_start(g.slots_out[bass.ts(j, P), :], res[:, s]).then_inc(stores[s], 16)

            pipeline(sp, BLOCKS, [(0, load), (3, store)], RING)
            for s in range(RING):
                sp.wait_ge(stores[s], 16 * (BLOCKS // RING))

        @block.tensor
        def _(pe):
            def turn(j, s, lap):
                pe.wait_ge(loads[s], lap * 16 + 16)
                wait(pe, rows_t_ready, j - 1)
                for k in range(KD):
                    last = nc.tensor.transpose(ps_t[:, s % 2, k * P:(k + 1) * P], rows[:, s, k * P:(k + 1) * P], ident)
                last.then_inc(turned, 1)

            def gate_up(j, s, lap):
                e = pe.value_load(g.owner[0:1, bass.ds(j, 1)], min_val=0, max_val=E - 1)
                pe.wait_ge(rows_t_ready, j + 1)
                wait(pe, act_ready, j - 1)
                for k in range(KD):
                    last = nc.tensor.matmul(ps_g[:, s % 2, 0:2 * INNER], rows_t[:, s, k],
                                            g.w13[:, bass.ds(e, 1), k, :].rearrange("p o f -> p (o f)"), start=(k == 0), stop=(k == KD - 1))
                last.then_inc(gu_ready, 1)

            def turn_act(j, s, lap):
                pe.wait_ge(act_ready, j + 1)
                wait(pe, res_ready, j - 1)
                nc.tensor.transpose(ps_o[:, s % 2, D:D + P], act[:, s], ident).then_inc(act_turned, 1)

            def down(j, s, lap):
                e = pe.value_load(g.owner[0:1, bass.ds(j, 1)], min_val=0, max_val=E - 1)
                pe.wait_ge(act_t_ready, j + 1)
                nc.tensor.matmul(ps_o[:, s % 2, 0:D], act_t[:, s], g.w2[:, bass.ds(e, 1), :].rearrange("p o f -> p (o f)"),
                                 start=True, stop=True).then_inc(out_ready, 1)

            pipeline(pe, BLOCKS, [(0, turn), (1, gate_up), (2, turn_act), (3, down)], RING)

        @block.scalar
        def _(act_e):
            def move_rows(j, s, lap):
                act_e.wait_ge(turned, j + 1)
                wait(act_e, gu_ready, j - RING + 1)
                nc.scalar.copy(rows_t[:, s], ps_t[:, s % 2, 0:D].rearrange("p (k t) -> p k t", k=KD)).then_inc(rows_t_ready, 1)

            def gate_silu(j, s, lap):
                act_e.wait_ge(gu_ready, j + 1)
                wait(act_e, act_ready, j - RING + 1)
                nc.scalar.activation(silu[:, s], ps_g[:, s % 2, 0:INNER], ACT.Silu).then_inc(silu_ready, 1)

            def move_act(j, s, lap):
                act_e.wait_ge(act_turned, j + 1)
                wait(act_e, out_ready, j - RING + 1)
                nc.scalar.copy(act_t[:, s], ps_o[:, s % 2, D:D + P]).then_inc(act_t_ready, 1)

            pipeline(act_e, BLOCKS, [(0, move_rows), (1, gate_silu), (2, move_act)], RING)

        @block.vector
        def _(dve):
            def activate(j, s, lap):
                dve.wait_ge(silu_ready, j + 1)
                wait(dve, act_turned, j - RING + 1)
                nc.vector.tensor_tensor(act[:, s], silu[:, s], ps_g[:, s % 2, INNER:2 * INNER], ALU.mult).then_inc(act_ready, 1)

            def move_out(j, s, lap):
                dve.wait_ge(out_ready, j + 1)
                wait(dve, stores[s], lap * 16)
                nc.vector.tensor_copy(res[:, s], ps_o[:, s % 2, 0:D]).then_inc(res_ready, 1)

            pipeline(dve, BLOCKS, [(1, activate), (3, move_out)], RING)


def ffn_combine(nc, g, tag):
    with ExitStack() as ctx:
        m = Memory(nc, ctx, tag + "_combine")
        DEEP = 8
        got = m.sb("got", [P, DEEP, D])
        gathered = [m.sem(f"gathered{r}") for r in range(DEEP)]
        added = m.sem("added")
        block = ctx.enter_context(nc.Block())

        @block.gpsimd
        def _(pool):
            for n in range(TILES * TOPK):
                wait(pool, added, n - DEEP + 1)
                nc.gpsimd.indirect_dma_start(
                    out=got[:, n % DEEP], out_offset=None, in_=g.slots_out,
                    in_offset=bass.IndirectOffsetOnAxis(ap=g.slot_out[:, n // TOPK, n % TOPK:n % TOPK + 1], axis=0),
                    bounds_check=SLOTS - 1, oob_is_err=False).then_inc(gathered[n % DEEP], 16)

        @block.vector
        def _(dve):
            for n in range(TILES * TOPK):
                i, k = n // TOPK, n % TOPK
                dve.wait_ge(gathered[n % DEEP], 16 * (n // DEEP + 1))
                wait(dve, added, n)
                nc.vector.scalar_tensor_tensor(out=g.x[:, i, :], in0=got[:, n % DEEP], scalar=g.weight[:, i, k:k + 1],
                                               in1=g.x[:, i, :], op0=ALU.mult, op1=ALU.add).then_inc(added, 1)
            dve.wait_ge(added, TILES * TOPK)


def ffn(nc, g, tag):
    with nc.sbuf_tensor(f"{tag}_xin", [P, TILES, D], F32) as g.xin:
        ffn_router(nc, g, tag)
        ffn_route(nc, g, tag)
        ffn_dispatch(nc, g, tag)
        ffn_experts(nc, g, tag)
        ffn_combine(nc, g, tag)


def store_all(nc, g, out):
    with ExitStack() as ctx:
        stored = Memory(nc, ctx, "store").sem("stored")
        block = ctx.enter_context(nc.Block())

        @block.sync
        def _(sp):
            sp.dma_start(out.rearrange("b (h p) d -> p (b h) d", p=P), g.x[:]).then_inc(stored, 16)
            sp.wait_ge(stored, 16)


class Globals:

    def __init__(self, nc, ctx):
        m = Memory(nc, ctx, "g")
        self.consts = m.sb("consts", [P, CONST_COLS])
        self.ones, self.minus_half = m.sb("ones", [P, P]), m.sb("minus_half", [P, 1])
        self.x = m.sb("x", [P, TILES, D])
        self.w_gates, self.w_down = m.sb("w_gates", [P, KD, GATES]), m.sb("w_down", [P, D])
        self.norm_w = m.sb("norm_w", [P, D])
        self.w13, self.w2 = m.sb("w13", [P, E, KD, 2 * INNER]), m.sb("w2", [P, E, D])
        self.top, self.chosen = m.sb("top", [P, TILES, TOPK]), m.sb("chosen", [P, TILES, TOPK])
        self.weight = m.sb("weight", [P, TILES, TOPK])
        self.slot_in, self.slot_out = m.sb("slot_in", [P, TILES, TOPK], U32), m.sb("slot_out", [P, TILES, TOPK], U32)
        self.owner = m.sb("owner", [1, P], I32)
        self.slots_in = nc.dram_tensor("slots_in", [SLOTS, D], F32, kind="Internal").ap()
        self.slots_out = nc.dram_tensor("slots_out", [SLOTS, D], F32, kind="Internal").ap()

    def const(self, name):
        a, b = CONST[name]
        return self.consts[:, a:b]


def build(nc, dram, out):
    Memory.sems.clear()
    with ExitStack() as ctx:
        g = Globals(nc, ctx)
        load_all(nc, g, dram)
        if "a" in STAGES:
            attention_a(nc, g, dram)
        if "f" in STAGES:
            ffn(nc, g, "f1")
        zero_semaphores(nc)
        if "b" in STAGES:
            attention_b(nc, g, dram)
        if "F" in STAGES:
            ffn(nc, g, "f2")
        store_all(nc, g, out)


def kernel(**inputs):
    import concourse.bacc as bacc
    from concourse.bass_utils import run_bass_kernel_spmd

    nc = bacc.Bacc("TRN2", target_bir_lowering=False, num_devices=1)
    laid = {
        "x": inputs["L0_attn_a_x"], "consts": constants(),
        "gate_t": np.asarray(inputs["L0_ffn_gate_w"]).T,
    }
    for name in inputs:
        if name not in ("L0_attn_a_x", "L0_ffn_gate_w"):
            laid[name.replace("L0_ffn_", "").replace("L0_attn_a_", "a_").replace("L0_attn_b_", "b_")] = np.asarray(inputs[name])
    wq = laid.pop("a_Wq").reshape(D, GA // 2, 2, REP, DA).transpose(0, 1, 3, 2, 4).reshape(D, HA * DA)
    laid["a_Wqkv"] = np.concatenate([wq, laid.pop("a_Wk"), laid.pop("a_Wv")], 1)
    wq_b = laid.pop("b_wq_b").reshape(QR, HB, DK)
    laid["b_wqn_t"], laid["b_wqp"] = wq_b[:, :, :NOPE].transpose(2, 1, 0), wq_b[:, :, NOPE:]
    wkv_b = laid.pop("b_wkv_b").reshape(KVR, HB, NOPE + VD)
    laid["b_wk_t"], laid["b_wv_t"] = wkv_b[:, :, :NOPE].transpose(2, 1, 0), wkv_b[:, :, NOPE:].transpose(2, 1, 0)
    laid["b_w_a"] = np.concatenate([laid.pop("b_wq_a"), laid.pop("b_wkv_a")], 1)
    arrays, dram = {}, {}
    for name, value in laid.items():
        value = np.ascontiguousarray(value)
        arrays[f"in_{name}"] = value
        dram[name] = nc.dram_tensor(f"in_{name}", value.shape, mybir.dt.from_np(value.dtype), kind="ExternalInput").ap()
    out = nc.dram_tensor("out_x", (B, T, D), F32, kind="ExternalOutput").ap()
    build(nc, dram, out)
    return run_bass_kernel_spmd(nc, [arrays], core_ids=[0]).results[0]["out_x"]
```

```python
from contextlib import ExitStack

import numpy as np

import concourse.bass as bass
from concourse import mybir

ALU = mybir.AluOpType
ACT = mybir.ActivationFunctionType
AX = mybir.AxisListType
F32 = mybir.dt.float32
BF16 = mybir.dt.bfloat16
U32 = mybir.dt.uint32
I32 = mybir.dt.int32

P = 128
B, T, D = 8, 256, 256
NTOK = B * T
TILES = NTOK // P
KD = D // P
LN_EPS = 1e-5

E, TOPK, INNER = 32, 4, 128
CAP = 2 * NTOK * TOPK // E
RMS_EPS = 1e-6
RING = 8
BLOCKS = -(-((NTOK * TOPK + E * (P - 1)) // P) // RING) * RING
SLOTS = BLOCKS * P
GATES = E + 2 * INNER

HA, GA, DA = 32, 8, 8
REP = HA // GA
STACK = 64
HB, DK, ROPE, NOPE, VD, KVR, QR = 16, 128, 64, 64, 128, 64, 96

NEG = -1e30
DROPPED = 1 << 16
STAGES = "afbF"

_WIDTHS = [("ident", P), ("before", P), ("future", P), ("cos_a", 2 * DA), ("sin_a", 2 * DA),
           ("cos_b", 2 * ROPE), ("sin_b", 2 * ROPE), ("experts", E), ("blocks", 1), ("row_mod", REP), ("minus_group", GA)]
CONST = {}
_at = 0
for _name, _w in _WIDTHS:
    CONST[_name] = (_at, _at + _w)
    _at += _w
CONST_COLS = _at


def constants():
    c = np.zeros((P, CONST_COLS), np.float32)

    def put(name, value):
        a, b = CONST[name]
        c[:, a:b] = value

    p = np.arange(P)
    put("ident", np.eye(P))
    put("before", p[:, None] < p[None, :])
    put("future", np.where(p[None, :] > p[:, None], NEG, 0.0))
    for name, dim in (("a", DA), ("b", ROPE)):
        theta = (np.float32(1.0) / np.float32(10000.0) ** (np.arange(0, dim, 2, dtype=np.float32) / np.float32(dim))).astype(np.float32)
        angle = np.outer(np.arange(T, dtype=np.float32), theta).astype(np.float32)
        cos, sin = np.cos(angle), np.sin(angle)
        both = np.concatenate([cos, cos], 1).reshape(2, P, dim).transpose(1, 0, 2)
        sign = np.concatenate([-sin, sin], 1).reshape(2, P, dim).transpose(1, 0, 2)
        put("cos_" + name, both.reshape(P, 2 * dim))
        put("sin_" + name, sign.reshape(P, 2 * dim))
    put("experts", np.arange(E)[None, :])
    put("blocks", p[:, None])
    put("row_mod", (p[:, None] % REP) == np.arange(REP)[None, :])
    put("minus_group", -1.0 * ((p[:, None] // REP) == np.arange(GA)[None, :]))
    return c


def wait(eng, sem, value):
    if not (isinstance(value, int) and value <= 0):
        eng.wait_ge(sem, value)


class Chain:

    def __init__(self, eng, sem, per):
        self.eng, self.sem, self.per, self.k, self.i = eng, sem, per, 0, 0

    def at(self, i):
        assert self.k in (0, self.per), (self.k, self.per)
        self.i, self.k = i, 0

    def then(self, ins):
        self.k += 1
        ins.then_inc(self.sem, 1)
        self.eng.wait_ge(self.sem, self.i * self.per + self.k)


def pipeline(eng, n, stages, ring):
    depth = max(d for d, _ in stages)

    def emit(t):
        for d, body in stages:
            if 0 <= t - d < n:
                body(t - d, (t - d) % ring, (t - d) // ring)

    first = -(-(depth + ring) // ring)
    last = n // ring
    for t in range(min(first, last) * ring):
        emit(t)
    if last > first:
        with eng.Fori(first, last) as lap:
            for u in range(ring):
                for d, body in stages:
                    off = u - d
                    body(lap * ring + off, off % ring, lap + off // ring)
    for t in range(max(first, last) * ring, n + depth):
        emit(t)


class Memory:

    sems = []

    def __init__(self, nc, ctx, tag):
        self.nc, self.ctx, self.tag = nc, ctx, tag

    def sb(self, name, shape, dt=F32):
        return self.ctx.enter_context(self.nc.sbuf_tensor(f"{self.tag}_{name}", shape, dt))

    def ps(self, name, shape, dt=F32):
        return self.ctx.enter_context(self.nc.psum_tensor(f"{self.tag}_{name}", shape, dt))

    def sem(self, name):
        Memory.sems.append(self.nc.alloc_semaphore(name=f"{self.tag}_{name}"))
        return Memory.sems[-1]


def zero_semaphores(nc):
    nc.clear_and_free_semaphores(Memory.sems)
    Memory.sems.clear()
    nc.all_engine_barrier()



def load_all(nc, g, dram):
    with ExitStack() as ctx:
        m = Memory(nc, ctx, "load")
        loaded, zeroed, cleared, made = m.sem("loaded"), m.sem("zeroed"), m.sem("cleared"), m.sem("made")
        zeros = m.sb("zeros", [P, 8 * D])
        block = ctx.enter_context(nc.Block())

        @block.sync
        def _(sp):
            sp.dma_start(g.consts[:], dram["consts"]).then_inc(loaded, 16)
            sp.dma_start(g.x[:], dram["x"].rearrange("b (h p) d -> p (b h) d", p=P)).then_inc(loaded, 16)
            sp.dma_start(g.w_gates[:, :, 0:E], dram["gate_t"].rearrange("(k p) e -> p k e", p=P)).then_inc(loaded, 16)
            sp.dma_start(g.w_gates[:, :, E:E + INNER], dram["shared_gate_w"].rearrange("(k p) e -> p k e", p=P)).then_inc(loaded, 16)
            sp.dma_start(g.w_gates[:, :, E + INNER:GATES], dram["shared_up_w"].rearrange("(k p) e -> p k e", p=P)).then_inc(loaded, 16)
            sp.dma_start(g.w_down[:], dram["shared_down_w"]).then_inc(loaded, 16)
            sp.dma_start(g.norm_w[:], dram["norm_w"].rearrange("(a d) -> a d", a=1).broadcast_to([P, D])).then_inc(loaded, 16)
            for e in range(0, E, 8):
                sp.dma_start(g.w13[:, e:e + 8], dram["w13"][e:e + 8].rearrange("e (k p) f -> p e k f", p=P)).then_inc(loaded, 16)
                sp.dma_start(g.w2[:, e:e + 8], dram["w2"][e:e + 8].rearrange("e i h -> i e h")).then_inc(loaded, 16)
            sp.wait_ge(zeroed, 1)
            for j in range(0, SLOTS, 8 * P):
                sp.dma_start(g.slots_in[j:j + 8 * P].rearrange("(r p) d -> p r d", p=P),
                             zeros[:].rearrange("p (r d) -> p r d", d=D)).then_inc(cleared, 16)
            sp.wait_ge(cleared, 16 * (SLOTS // (8 * P)))
            sp.wait_ge(loaded, 16 * (7 + 2 * (E // 8)))

        @block.vector
        def _(dve):
            nc.vector.memset(zeros[:], 0.0).then_inc(zeroed, 1)
            nc.vector.memset(g.ones[:], 1.0).then_inc(made, 1)
            nc.vector.memset(g.minus_half[:], -0.5).then_inc(made, 1)
            dve.wait_ge(made, 2)



def normalise_tile(nc, dve, g, m, i, c, count, chain):
    chain.then(nc.vector.bn_stats(m.stats[:, c], g.x[:, i, :]))
    nc.vector.memset(m.pause[:], 0)
    chain.then(nc.vector.bn_aggr(m.mv[:, c], m.stats[:, c]))
    nc.vector.tensor_scalar(m.veps[:, c:c + 1], m.mv[:, c, 1:2], LN_EPS, None, ALU.add).then_inc(m.veps_ready, 1)
    dve.wait_ge(m.rstd_ready, count + 1)
    nc.vector.tensor_scalar(m.xn[:, c], g.x[:, i, :], m.mv[:, c, 0:1], m.rstd[:, c:c + 1],
                            ALU.subtract, ALU.mult).then_inc(m.xn_ready, 1)


def norm_buffers(m):
    m.stats, m.mv, m.xn = m.sb("stats", [P, 2, 6]), m.sb("mv", [P, 2, 2]), m.sb("xn", [P, 2, D])
    m.veps, m.rstd, m.pause = m.sb("veps", [P, 2]), m.sb("rstd", [P, 2]), m.sb("pause", [P, 1], U32)
    m.veps_ready, m.rstd_ready, m.xn_ready = m.sem("veps_ready"), m.sem("rstd_ready"), m.sem("xn_ready")


def attention_a(nc, g, dram):
    WQKV = D + 2 * GA * DA
    NQK = HA + GA
    UNITS = 3 * GA
    BLOCKS_OF = ((0, 0), (0, 1), (1, 1))
    VROW = 32
    AFTER = {3: ["X"], 4: ["Q0", "Q1"], 5: ["H1"], 7: ["C"], 8: ["K0"], 9: ["O"], 10: ["K1", "S0"], 12: ["S1"],
             14: ["U0"], 17: ["H0"], 23: ["U1"], 24: ["M"]}
    MAX_FROM = 13
    TAKES = {"X": (0,), "Q0": (1,), "Q1": (0,), "H1": (0, 1), "C": (0,), "O": (1,), "S0": (0, 1, 0), "S1": (0, 1, 0),
             "H0": (0, 1), "M": (1,)}
    LAG = {"X": 0, "Q0": 0, "Q1": 0, "K0": 0, "K1": 0, "S0": 0, "S1": 0, "M": 0, "U0": 1, "U1": 1, "H0": 1, "H1": 2, "C": 2, "O": 2}
    STEPS = B + 2
    order = [name for v in sorted(AFTER) for name in AFTER[v] if name in TAKES]

    def present(t, lag):
        return not isinstance(t, int) or 0 <= t - lag < B

    def uses_before(t, name, bank):
        def in_step(step, names):
            return sum(TAKES[n].count(bank) for n in names if present(step, LAG[n]))
        ahead = order[:order.index(name)]
        if isinstance(t, int):
            return sum(in_step(u, order) for u in range(t)) + in_step(t, ahead)
        full = in_step(None, order)
        return (t - 2) * full + (in_step(0, order) + in_step(1, order) + in_step(None, ahead))

    def run_steps(eng, body):
        body(0, 0)
        body(1, 1)
        with eng.Fori(1, B // 2) as lap:
            for s in range(2):
                body(lap * 2 + s, s)
        body(B, 0)
        body(B + 1, 1)

    with ExitStack() as ctx:
        m = Memory(nc, ctx, "a")
        norm_buffers(m)
        w_qkv, w_o = m.sb("w_qkv", [P, KD, WQKV]), m.sb("w_o", [P, KD, D])
        pool_pause = m.sb("pool_pause", [P, 8])
        ident_b, future_b = m.sb("ident_b", [P, P], BF16), m.sb("future_b", [P, P], BF16)
        minus_group = m.sb("minus_group", [HA, GA, P], BF16)
        x_t, ctx_n, ctx_t = m.sb("x_t", [P, KD, 2, P]), m.sb("ctx_n", [P, 2, HA, DA]), m.sb("ctx_t", [P, KD, 2, P])
        by_cos, by_sin, qk = m.sb("by_cos", [P, NQK, DA]), m.sb("by_sin", [P, NQK, DA]), m.sb("qk", [P, NQK, DA])
        rest = m.sb("rest", [P, NQK, DA])
        high, mid, low = (m.sb(name, [P, 2, NQK, DA], BF16) for name in ("high", "mid", "low"))
        q_stack, k_stack = m.sb("q_stack", [P, 2, HA, 8, DA], BF16), m.sb("k_stack", [P, 2, GA, 8, DA], BF16)
        values = m.sb("values", [P, 2, 2, GA, VROW])
        q_t, k_t = m.sb("q_t", [P, 2, 2, HA // 2, P], BF16), m.sb("k_t", [P, 2, 2, GA // 2, P], BF16)
        max_t = m.sb("max_t", [HA, 2, 2, REP, P], BF16)
        row_max, probs = m.sb("row_max", [P, 2, HA], BF16), m.sb("probs", [P, 4, REP, P])
        weighted, recip = m.sb("weighted", [P, 2, 2, REP, P]), m.sb("recip", [P, 2, REP, 4, 1])
        ps_s, ps_m, ps_u, ps_w = (m.ps(name, [P, 2, 512]) for name in ("ps_s", "ps_m", "ps_u", "ps_w"))

        w_loaded, made, chain_sem, rope_chain = m.sem("w_loaded"), m.sem("made"), m.sem("chain"), m.sem("rope_chain")
        ready = {name: m.sem(f"{name}_ready") for name in TAKES}
        left = [m.sem("left_w0"), m.sem("left_w1")]
        parts_ready, q_stacked, k_stacked = m.sem("parts_ready"), m.sem("q_stacked"), m.sem("k_stacked")
        smax_ready, smax_read, s_ready, p_ready = m.sem("smax_ready"), m.sem("smax_read"), m.sem("s_ready"), m.sem("p_ready")
        p_masked, weighed, u_moved, recips, ctx_ready, ready_max = m.sem("p_masked"), m.sem("weighed"), m.sem("u_moved"), m.sem("recips"), m.sem("ctx_ready"), m.sem("ready_max")
        ident = g.const("ident")
        block = ctx.enter_context(nc.Block())

        def free(eng, t, name, n=0):
            bank = TAKES[name][n]
            wait(eng, left[bank], uses_before(t, name, bank) + TAKES[name][:n].count(bank))
            return bank

        def read(eng, t, name):
            for bank in set(TAKES[name]):
                eng.wait_ge(left[bank], uses_before(t, name, bank) + TAKES[name].count(bank))

        @block.sync
        def _(sp):
            sp.dma_start(w_qkv[:], dram["a_Wqkv"].rearrange("(k p) n -> p k n", p=P)).then_inc(w_loaded, 16)
            sp.dma_start(w_o[:], dram["a_Wo"].rearrange("(k p) n -> p k n", p=P)).then_inc(w_loaded, 16)
            sp.wait_ge(w_loaded, 32)

        @block.gpsimd
        def _(pool):
            def step(t, s):
                if present(t, 0):
                    for c in range(2):
                        pool.wait_ge(m.veps_ready, t * 2 + c + 1)
                        nc.gpsimd.tensor_tensor(m.rstd[:, c:c + 1], m.veps[:, c:c + 1], g.minus_half[:], ALU.pow).then_inc(m.rstd_ready, 1)
                for v in range(UNITS):
                    if present(t, 1) and v % 3 != 1:
                        pool.wait_ge(p_ready, (t - 1) * UNITS + v + 1)
                        nc.gpsimd.tensor_tensor(pool_pause[:, v % 6:v % 6 + 1], g.minus_half[:], g.minus_half[:], ALU.add)
                        nc.gpsimd.affine_select(out=probs[:, v % 4], in_=probs[:, v % 4], compare_op=ALU.is_ge, fill=0.0, base=0,
                                                pattern=[[0, REP], [1, P]], channel_multiplier=-1).then_inc(p_masked, 1)
                    for name in AFTER.get(v, ()):
                        if name in ("K0", "K1") and present(t, 0):
                            c = int(name[1])
                            pool.wait_ge(parts_ready, t * 2 + c + 1)
                            nc.gpsimd.tensor_tensor(pool_pause[:, 6 + c:7 + c], g.minus_half[:], g.minus_half[:], ALU.add)
                            for n, part in enumerate((high, mid, low)):
                                width = len(range(n, 8, 3))
                                last = nc.gpsimd.tensor_copy(k_stack[:, c, :, n:8:3, :],
                                                             part[:, c, HA:].rearrange("p h (o d) -> p h o d", o=1).broadcast_to([P, GA, width, DA]))
                            last.then_inc(k_stacked, 1)

            run_steps(pool, step)

        @block.tensor
        def _(pe):
            pe.wait_ge(made, 5)
            pe.wait_ge(w_loaded, 32)

            def scores(b, s, v):
                group, (s_blk, t_blk) = v // 3, BLOCKS_OF[v % 3]
                rows, pair = slice(STACK * (group % 2), STACK * (group % 2) + STACK), group // 2
                wait(pe, p_ready, b * UNITS + v - 1)
                nc.tensor.matmul(ps_s[:, v % 2], k_t[rows, s, s_blk, pair], q_t[rows, s, t_blk, pair * REP:(pair + 1) * REP], start=True, stop=False)
                nc.tensor.matmul(ps_s[:, v % 2], minus_group[:, group], max_t[:, s, t_blk], start=False, stop=True).then_inc(s_ready, 1)

            def weigh(b, s, v):
                group, (s_blk, t_blk) = v // 3, BLOCKS_OF[v % 3]
                if v % 3 == 1:
                    pe.wait_ge(p_ready, b * UNITS + v + 1)
                else:
                    pe.wait_ge(p_masked, b * 2 * GA + group * 2 + (v % 3) // 2 + 1)
                if v in (0, UNITS // 2):
                    wait(pe, u_moved, b * 2 + v // (UNITS // 2))
                rows = slice(VROW * (group % 4), VROW * (group % 4) + VROW)
                nc.tensor.matmul(ps_u[rows, t_blk], values[:, s, s_blk, group], probs[:, v % 4].rearrange("p r t -> p (r t)"),
                                 start=(v % 3 != 2), stop=(v % 3 != 1)).then_inc(weighed, 1)

            def maxima(b, s, v):
                group, c = v // 3, min(v % 3, 1)
                rows, pair = slice(STACK * (group % 2), STACK * (group % 2) + STACK), group // 2
                wait(pe, smax_read, b * UNITS + v - 1)
                bank = ps_m[:, v % 2].rearrange("p (r s) -> p r s", s=(c + 1) * P)
                reps = REP // (c + 1)
                for r in range(reps):
                    nc.tensor.matmul(bank[:, r], q_t[rows, s, c, pair * REP + (v % 3 == 2) * reps + r], k_t[rows, s, 0:c + 1, pair],
                                     start=(r == 0), stop=False)
                nc.tensor.matmul(bank[:, :, c * P:(c + 1) * P], ident_b[:],
                                 future_b[:].rearrange("p (o s) -> p o s", o=1).broadcast_to([P, reps, P]),
                                 start=False, stop=True).then_inc(smax_ready, 1)

            def turn_weighted(t, s, name):
                pe.wait_ge(u_moved, (t - LAG[name]) * 2 + int(name[1]) + 1)
                for c in range(2):
                    bank = free(pe, t, name, c)
                    for r in range(REP):
                        last = nc.tensor.transpose(ps_w[:, bank, r * P:(r + 1) * P], weighted[:, int(name[1]), c, r], ident)
                    last.then_inc(ready[name], 1)

            def turn_stacks(t, s, name):
                c = int(name[1])
                pe.wait_ge(q_stacked, t * 2 + c + 1)
                pe.wait_ge(k_stacked, t * 2 + c + 1)
                for part in range(3):
                    bank = free(pe, t, name, part)
                    for n in range(8 if part < 2 else 4):
                        src = (q_stack[:, c, (part * 8 + n) * 2:(part * 8 + n) * 2 + 2] if part < 2
                               else k_stack[:, c, n * 2:n * 2 + 2])
                        last = nc.tensor.transpose(ps_w[:, bank].bitcast(BF16)[:, n * P:(n + 1) * P], src.rearrange("p h r d -> p (h r d)"), ident_b[:])
                    last.then_inc(ready[name], 1)

            def other(t, s, name):
                if name == "X":
                    pe.wait_ge(m.xn_ready, t * 2 + 2)
                    bank = free(pe, t, name)
                    for c in range(2):
                        for k in range(KD):
                            last = nc.tensor.transpose(ps_w[:, bank, (k * 2 + c) * P:(k * 2 + c + 1) * P], m.xn[:, c, k * P:(k + 1) * P], ident)
                    last.then_inc(ready[name], 1)
                elif name in ("Q0", "Q1"):
                    c = int(name[1])
                    read(pe, t, "X")
                    bank = free(pe, t, name)
                    for k in range(KD):
                        last = nc.tensor.matmul(ps_w[:, bank, 0:WQKV], x_t[:, k, c], w_qkv[:, k, :], start=(k == 0), stop=(k == KD - 1))
                    last.then_inc(ready[name], 1)
                elif name in ("S0", "S1"):
                    turn_stacks(t, s, name)
                elif name in ("H0", "H1"):
                    turn_weighted(t, s, name)
                elif name == "C":
                    bank = free(pe, t, name)
                    pe.wait_ge(ctx_ready, (t - 2) * 4 + 4)
                    for c in range(2):
                        for k in range(KD):
                            last = nc.tensor.transpose(ps_w[:, bank, (k * 2 + c) * P:(k * 2 + c + 1) * P],
                                                       ctx_n[:, c].rearrange("p h d -> p (h d)")[:, k * P:(k + 1) * P], ident)
                    last.then_inc(ready[name], 1)
                elif name == "O":
                    read(pe, t, "C")
                    bank = free(pe, t, name)
                    for c in range(2):
                        for k in range(KD):
                            last = nc.tensor.matmul(ps_w[:, bank, c * D:(c + 1) * D], ctx_t[:, k, c], w_o[:, k, :], start=(k == 0), stop=(k == KD - 1))
                    last.then_inc(ready[name], 1)
                elif name == "M":
                    pe.wait_ge(smax_read, t * UNITS + UNITS)
                    bank = free(pe, t, name)
                    for c in range(2):
                        last = nc.tensor.transpose(ps_w[0:HA, bank].bitcast(BF16)[:, c * P:(c + 1) * P], row_max[:, c], ident_b[:])
                    last.then_inc(ready[name], 1)

            def step(t, s):
                if present(t, 1):
                    pe.wait_ge(ready_max, t)
                next_max = 0
                for v in range(UNITS + 2):
                    if present(t, 1) and v < UNITS:
                        scores(t - 1, 1 - s, v)
                    if present(t, 1) and v == UNITS:
                        weigh(t - 1, 1 - s, v - 2)
                    if v == MAX_FROM and present(t, 0):
                        read(pe, t, "S0")
                        read(pe, t, "S1")
                    while present(t, 0) and v >= MAX_FROM and next_max < min(UNITS, 2 * (v - MAX_FROM + 1)):
                        maxima(t, s, next_max)
                        next_max += 1
                    if present(t, 1) and v >= 2 and v != UNITS:
                        weigh(t - 1, 1 - s, v - 2)
                    for name in AFTER.get(v, ()):
                        if name in TAKES and present(t, LAG[name]):
                            other(t, s, name)

            run_steps(pe, step)

        @block.scalar
        def _(act):
            def other(t, s, name):
                if name in ("X", "C"):
                    src = ps_w[:, TAKES[name][0]]
                    act.wait_ge(ready[name], t - LAG[name] + 1)
                    dst = x_t if name == "X" else ctx_t
                    nc.scalar.copy(dst[:].rearrange("p k c t -> p (k c t)"), src).then_inc(left[TAKES[name][0]], 1)
                elif name in ("K0", "K1"):
                    c = int(name[1])
                    act.wait_ge(parts_ready, t * 2 + c + 1)
                    for part, a, z in ((high, 0, 3), (mid, 3, 6), (low, 6, 8)):
                        last = nc.scalar.copy(q_stack[:, c, :, a:z, :], part[:, c, 0:HA].rearrange("p h (o d) -> p h o d", o=1).broadcast_to([P, HA, z - a, DA]))
                    last.then_inc(q_stacked, 1)
                elif name in ("S0", "S1"):
                    c = int(name[1])
                    for part, bank in enumerate(TAKES[name]):
                        act.wait_ge(ready[name], t * 3 + part + 1)
                        dst = q_t[:, s, c, part * 8:part * 8 + 8] if part < 2 else k_t[:, s, c]
                        n = 8 if part < 2 else 4
                        nc.scalar.copy(dst, ps_w[:, bank].bitcast(BF16)[:, 0:n * P].rearrange("p (n t) -> p n t", t=P)).then_inc(left[bank], 1)
                elif name in ("U0", "U1"):
                    half = int(name[1])
                    act.wait_ge(weighed, (t - 1) * UNITS + (half + 1) * UNITS // 2)
                    nc.scalar.copy(weighted[:, half].rearrange("p c r t -> p c (r t)"), ps_u[:]).then_inc(u_moved, 1)

            def step(t, s):
                for v in range(UNITS + 2):
                    if present(t, 1) and v < UNITS:
                        act.wait_ge(s_ready, (t - 1) * UNITS + v + 1)
                        wait(act, weighed, (t - 1) * UNITS + v - 3)
                        nc.scalar.activation(probs[:, v % 4].rearrange("p r t -> p (r t)"), ps_s[:, v % 2], ACT.Exp,
                                             scale=float(DA) ** -0.5).then_inc(p_ready, 1)
                    for name in AFTER.get(v, ()):
                        if present(t, LAG[name]):
                            other(t, s, name)

            run_steps(act, step)

        @block.vector
        def _(dve):
            nc.vector.tensor_copy(ident_b[:], ident).then_inc(made, 1)
            nc.vector.tensor_copy(future_b[:], g.const("future")).then_inc(made, 1)
            nc.vector.tensor_copy(minus_group[:], g.const("minus_group")[0:HA].rearrange("p (g o) -> p g o", o=1).broadcast_to([HA, GA, P])).then_inc(made, 1)
            nc.vector.memset(values[:, :, :, :, DA:DA + 1], 1.0).then_inc(made, 1)
            nc.vector.memset(values[:, :, :, :, DA + 1:], 0.0).then_inc(made, 1)
            norm, rope = Chain(dve, chain_sem, 4), Chain(dve, rope_chain, 10)

            def rotate(t, s, name):
                c = int(name[1])
                dve.wait_ge(ready[name], t + 1)
                src = ps_w[:, TAKES[name][0], 0:NQK * DA].rearrange("p (h d) -> p h d", d=DA)
                cos = g.const("cos_a")[:, c * DA:(c + 1) * DA].rearrange("p (o d) -> p o d", o=1)
                sin = g.const("sin_a")[:, c * DA:(c + 1) * DA].rearrange("p (o d) -> p o d", o=1)
                half = DA // 2
                nc.vector.tensor_tensor(by_cos[:], src, cos.broadcast_to([P, NQK, DA]), ALU.mult)
                nc.vector.tensor_tensor(by_sin[:, :, 0:half], src[:, :, half:], sin[:, :, 0:half].broadcast_to([P, NQK, half]), ALU.mult)
                nc.vector.tensor_tensor(by_sin[:, :, half:], src[:, :, 0:half], sin[:, :, half:].broadcast_to([P, NQK, half]), ALU.mult)
                nc.vector.tensor_copy(values[:, s, c, :, 0:DA], ps_w[:, TAKES[name][0], NQK * DA:WQKV].rearrange("p (h d) -> p h d", d=DA)).then_inc(left[TAKES[name][0]], 1)
                dve.wait_ge(left[TAKES[name][0]], uses_before(t, name, TAKES[name][0]) + 1)
                rope.then(nc.vector.tensor_tensor(qk[:], by_cos[:], by_sin[:], ALU.add))
                rope.then(nc.vector.tensor_copy(high[:, c], qk[:]))
                rope.then(nc.vector.tensor_tensor(rest[:], qk[:], high[:, c], ALU.subtract))
                rope.then(nc.vector.tensor_copy(mid[:, c], rest[:]))
                rope.then(nc.vector.tensor_tensor(low[:, c], rest[:], mid[:, c], ALU.subtract))
                nc.vector.memset(m.pause[:], 0).then_inc(parts_ready, 1)

            def other(t, s, name):
                if name in ("Q0", "Q1"):
                    rotate(t, s, name)
                elif name in ("H0", "H1"):
                    half = int(name[1])
                    for c in range(2):
                        bank = TAKES[name][c]
                        dve.wait_ge(ready[name], (t - LAG[name]) * 2 + c + 1)
                        src = ps_w[:, bank].rearrange("p (r g d) -> p r g d", r=REP, d=VROW)
                        nc.vector.reciprocal(recip[:, c], src[:, :, :, DA:DA + 1]).then_inc(recips, 1)
                        dve.wait_ge(recips, (t - LAG[name]) * 4 + half * 2 + c + 1)
                        dst = ctx_n[:, c, half * (HA // 2):(half + 1) * (HA // 2)].rearrange("p (g r) d -> p r g d", r=REP)
                        nc.vector.tensor_tensor(dst, src[:, :, :, 0:DA], recip[:, c].broadcast_to([P, REP, 4, DA]), ALU.mult).then_inc(left[bank], 1)
                        nc.vector.memset(m.pause[:], 0).then_inc(ctx_ready, 1)
                elif name == "O":
                    dve.wait_ge(ready[name], t - 2 + 1)
                    tiles = g.x[:, bass.ds((t - 2) * 2, 2), :]
                    nc.vector.tensor_tensor(tiles, tiles, ps_w[:, TAKES[name][0]].rearrange("p (c d) -> p c d", c=2), ALU.add).then_inc(left[TAKES[name][0]], 1)
                elif name == "M":
                    dve.wait_ge(ready[name], t + 1)
                    bank = TAKES[name][0]
                    for r in range(REP):
                        last = nc.vector.tensor_scalar(max_t[:, s, :, r], ps_w[0:HA, bank].bitcast(BF16)[:, 0:2 * P].rearrange("p (c t) -> p c t", c=2),
                                                       g.const("row_mod")[0:HA, r:r + 1], None, ALU.mult)
                    last.then_inc(left[bank], 1)
                    nc.vector.memset(m.pause[:], 0).then_inc(ready_max, 1)

            def step(t, s):
                if present(t, 0):
                    norm.at(t)
                    wait(dve, ready["X"], t)
                    for c in range(2):
                        normalise_tile(nc, dve, g, m, t * 2 + c, c, t * 2 + c, norm)
                    rope.at(t)
                next_max = 0
                for v in range(UNITS + 2):
                    while present(t, 0) and v >= MAX_FROM and next_max < min(UNITS, 2 * (v - MAX_FROM + 1)):
                        group, n = next_max // 3, next_max % 3
                        c = min(n, 1)
                        reps = REP // (c + 1)
                        first = group * REP + (n == 2) * reps
                        dve.wait_ge(smax_ready, t * UNITS + next_max + 1)
                        nc.vector.tensor_reduce(row_max[:, c, first:first + reps], ps_m[:, next_max % 2].rearrange("p (r s) -> p r s", s=(c + 1) * P),
                                                AX.X, ALU.max).then_inc(smax_read, 1)
                        next_max += 1
                    for name in AFTER.get(v, ()):
                        if present(t, LAG[name]):
                            other(t, s, name)

            run_steps(dve, step)
            dve.wait_ge(left[1], uses_before(STEPS - 1, "O", 1) + 1)



RMS_EPS_B = float(np.finfo(np.float32).eps)
PAIRS = HB // 2
HEAD_GROUP = 8


def attention_b_weights(nc, g, w, dram):
    with ExitStack() as ctx:
        m = Memory(nc, ctx, "b_weights")
        wqn_t, wk_t = m.sb("wqn_t", [NOPE, HB, QR]), m.sb("wk_t", [NOPE, HB, KVR])
        wv_t, wo, q_norm = m.sb("wv_t", [VD, HB, KVR]), m.sb("wo", [VD, HB, D]), m.sb("q_norm", [QR, 1])
        ps = m.ps("ps", [P, 6, 512])
        loaded, kept, multiplied, moved = m.sem("loaded"), m.sem("kept"), m.sem("multiplied"), m.sem("moved")
        block = ctx.enter_context(nc.Block())

        @block.sync
        def _(sp):
            sp.dma_start(wqn_t[:], dram["b_wqn_t"]).then_inc(loaded, 16)
            sp.dma_start(wk_t[:], dram["b_wk_t"]).then_inc(loaded, 16)
            sp.dma_start(wv_t[:], dram["b_wv_t"]).then_inc(loaded, 16)
            sp.dma_start(wo[:], dram["b_wo"].rearrange("(h v) n -> v h n", v=VD)).then_inc(loaded, 16)
            sp.dma_start(q_norm[:], dram["b_q_a_norm_w"].rearrange("(p a) -> p a", a=1)).then_inc(loaded, 16)
            sp.dma_start(w.wq[:, :, 0:ROPE], dram["b_wqp"]).then_inc(loaded, 16)
            sp.dma_start(w.w_a[:], dram["b_w_a"].rearrange("(k p) n -> p k n", p=P)).then_inc(loaded, 16)
            sp.dma_start(w.kv_norm[:], dram["b_kv_a_norm_w"].rearrange("(a d) -> a d", a=1).broadcast_to([P, KVR])).then_inc(loaded, 16)
            sp.wait_ge(loaded, 128)

        @block.tensor
        def _(pe):
            pe.wait_ge(loaded, 128)
            for h in range(HB):
                nc.tensor.matmul(ps[0:QR, h // 8, (h % 8) * KVR:(h % 8 + 1) * KVR], wqn_t[:, h], wk_t[:, h], start=True, stop=True)
            for h in range(HB):
                half = slice(KVR * (h % 2), KVR * (h % 2) + KVR)
                last = nc.tensor.matmul(ps[half, 2 + h // 4, (h // 2 % 2) * D:(h // 2 % 2 + 1) * D], wv_t[:, h], wo[:, h], start=True, stop=True)
            last.then_inc(multiplied, 1)

        @block.vector
        def _(dve):
            dve.wait_ge(multiplied, 1)
            nc.vector.tensor_copy(w.wvo[:].rearrange("p h n -> p (h n)"), ps[:, 2:6].rearrange("p b n -> p (b n)"))
            nc.vector.tensor_copy(w.wq[:, :, ROPE:], ps[0:QR, 0:2].rearrange("p b n -> p (b n)").rearrange("p (h c) -> p h c", c=KVR)).then_inc(moved, 1)
            dve.wait_ge(moved, 1)
            nc.vector.tensor_scalar(w.wq[:], w.wq[:], q_norm[:, 0:1], None, ALU.mult).then_inc(kept, 1)
            nc.vector.tensor_copy(w.ident_b[:], g.const("ident")).then_inc(kept, 1)
            nc.vector.tensor_copy(w.minus_head[:], g.const("ident")[0:HB, 0:HB].rearrange("p (h o) -> p h o", o=1).broadcast_to([HB, HB, P])).then_inc(kept, 1)
            dve.wait_ge(kept, 3)
            nc.vector.tensor_scalar(w.minus_head[:], w.minus_head[:], -1.0, None, ALU.mult).then_inc(kept, 1)
            nc.vector.memset(w.keys[:, :, DK:], 1.0).then_inc(kept, 1)
            dve.wait_ge(kept, 5)


def attention_b(nc, g, dram):
    NA = QR + KVR + ROPE
    with ExitStack() as ctx:
        m = Memory(nc, ctx, "b")
        norm_buffers(m)
        m.w_a, m.wq, m.wvo = m.sb("w_a", [P, KD, NA]), m.sb("wq", [QR, HB, DK]), m.sb("wvo", [P, PAIRS, D])
        m.kv_norm, m.ident_b, m.minus_head = m.sb("kv_norm", [P, KVR]), m.sb("ident_b", [P, P], BF16), m.sb("minus_head", [HB, HB, P], BF16)
        m.keys = m.sb("keys", [P, 2, DK + 1])
        attention_b_weights(nc, g, m, dram)
        x_t, junk, sums = m.sb("x_t", [P, KD, 2, P]), m.sb("junk", [P, QR]), m.sb("sums", [P, 2, 2])
        means, inverse, q_low = m.sb("means", [P, 2, 2]), m.sb("inverse", [P, 2, 2]), m.sb("q_low", [P, 2, QR])
        by_cos, by_sin = m.sb("by_cos", [P, 2, HEAD_GROUP, ROPE]), m.sb("by_sin", [P, 2, HEAD_GROUP, ROPE])
        k_cos, k_sin = m.sb("k_cos", [P, 2, ROPE]), m.sb("k_sin", [P, 2, ROPE])
        q_low_t, k_t, k_tb = m.sb("q_low_t", [QR, 2, P]), m.sb("k_t", [P, 2, P]), m.sb("k_tb", [P, 2, P], BF16)
        queries, q_t, q_tb = m.sb("queries", [P, 2, HEAD_GROUP, DK]), m.sb("q_t", [P, HB, 2, P]), m.sb("q_tb", [P, HB, 2, P], BF16)
        row_max, max_t = m.sb("row_max", [P, 2, HB], BF16), m.sb("max_t", [HB, 2 * P], BF16)
        probs, recip = m.sb("probs", [P, 2, 2, 2, 2 * P]), m.sb("recip", [P, 2, 2, 2, 1])
        ctx_n, ctx_t = m.sb("ctx_n", [P, 2, 2, 2, KVR]), m.sb("ctx_t", [P, 2, 2, P])
        ps_s, ps_o, ps_c, ps_y = m.ps("ps_s", [P, 2, 2, 512]), m.ps("ps_o", [P, 2, 512]), m.ps("ps_c", [P, 512]), m.ps("ps_y", [P, 512])

        chain_sem, low_chain, rope_sem = m.sem("chain"), m.sem("low_chain"), m.sem("rope")
        x_turned, x_t_ready, low_ready, sums_ready = m.sem("x_turned"), m.sem("x_t_ready"), m.sem("low_ready"), m.sem("sums_ready")
        means_ready, inverse_ready, keys_ready, low_turned = m.sem("means_ready"), m.sem("inverse_ready"), m.sem("keys_ready"), m.sem("low_turned")
        low_t_ready, q_made, q_rotated, q_ready = m.sem("low_t_ready"), m.sem("q_made"), m.sem("q_rotated"), m.sem("q_ready")
        q_turned, q_t_ready, q_tb_ready = m.sem("q_turned"), m.sem("q_t_ready"), m.sem("q_tb_ready")
        smax_ready, smax_read, max_turned, max_t_ready = m.sem("smax_ready"), m.sem("smax_read"), m.sem("max_turned"), m.sem("max_t_ready")
        s_ready, p_ready, pv_done, recips = m.sem("s_ready"), m.sem("p_ready"), m.sem("pv_done"), m.sem("recips")
        ctx_ready, ctx_turned, ctx_moved, y_ready, x_added = m.sem("ctx_ready"), m.sem("ctx_turned"), m.sem("ctx_moved"), m.sem("y_ready"), m.sem("x_added")
        ident = g.const("ident")
        block = ctx.enter_context(nc.Block())

        def skewed(first, second):
            for u in range(5):
                if u < 4:
                    first(u)
                if u:
                    second(u - 1)

        @block.gpsimd
        def _(pool):
            def batch(b, s, lap):
                for c in range(2):
                    pool.wait_ge(m.veps_ready, b * 2 + c + 1)
                    nc.gpsimd.tensor_tensor(m.rstd[:, c:c + 1], m.veps[:, c:c + 1], g.minus_half[:], ALU.pow).then_inc(m.rstd_ready, 1)
                for c in range(2):
                    pool.wait_ge(means_ready, b * 2 + c + 1)
                    nc.gpsimd.tensor_tensor(inverse[:, c], means[:, c], g.minus_half[:].broadcast_to([P, 2]), ALU.pow).then_inc(inverse_ready, 1)

            pipeline(pool, B, [(0, batch)], 1)

        @block.tensor
        def _(pe):
            def batch(b, s, lap):
                pe.wait_ge(m.xn_ready, b * 2 + 2)
                for c in range(2):
                    for k in range(KD):
                        last = nc.tensor.transpose(ps_s[:, 0, 0, (k * 2 + c) * P:(k * 2 + c + 1) * P], m.xn[:, c, k * P:(k + 1) * P], ident)
                last.then_inc(x_turned, 1)
                pe.wait_ge(x_t_ready, b + 1)
                for c in range(2):
                    for k in range(KD):
                        last = nc.tensor.matmul(ps_s[:, 1, c, 0:NA], x_t[:, k, c], m.w_a[:, k, :], start=(k == 0), stop=(k == KD - 1))
                    last.then_inc(low_ready, 1)
                pe.wait_ge(keys_ready, b * 2 + 2)
                for c in range(2):
                    nc.tensor.transpose(ps_s[0:QR, 0, 0, c * P:(c + 1) * P], q_low[:, c], ident)
                    last = nc.tensor.transpose(ps_s[:, 0, 1, c * P:(c + 1) * P], m.keys[:, c, 0:DK], ident)
                last.then_inc(low_turned, 1)
                pe.wait_ge(low_t_ready, b + 1)

                def make(u):
                    c, half = u // 2, u % 2
                    if u >= 2:
                        pe.wait_ge(q_ready, b * 4 + u - 1)
                    for n in range(2):
                        h = half * HEAD_GROUP + n * 4
                        last = nc.tensor.matmul(ps_s[:, u % 2, n], q_low_t[:, c], m.wq[:, h:h + 4, :].rearrange("p h d -> p (h d)"), start=True, stop=True)
                    last.then_inc(q_made, 1)

                def turn(u):
                    pe.wait_ge(q_ready, b * 4 + u + 1)
                    if u >= 1:
                        pe.wait_ge(q_t_ready, b * 4 + u)
                    for n in range(HEAD_GROUP):
                        last = nc.tensor.transpose(ps_o[:, n // 4, (n % 4) * P:(n % 4 + 1) * P], queries[:, u % 2, n], ident)
                    last.then_inc(q_turned, 1)

                skewed(make, turn)
                pe.wait_ge(q_tb_ready, b * 4 + 4)
                for j in range(PAIRS):
                    if j >= 2:
                        pe.wait_ge(smax_read, b * PAIRS + j - 1)
                    for c in range(2):
                        for n in range(2):
                            last = nc.tensor.matmul(ps_s[:, j % 2, c, n * T:(n + 1) * T], q_tb[:, j * 2 + n, c], k_tb[:].rearrange("p c s -> p (c s)"), start=True, stop=True)
                    last.then_inc(smax_ready, 1)
                pe.wait_ge(smax_read, b * PAIRS + PAIRS)
                for c in range(2):
                    last = nc.tensor.transpose(ps_s[0:HB, 0, 0, :].bitcast(BF16)[:, c * P:(c + 1) * P], row_max[:, c], m.ident_b[:])
                last.then_inc(max_turned, 1)
                pe.wait_ge(max_t_ready, b + 1)
                wait(pe, x_added, b)

                def scores(j):
                    if j >= 2:
                        pe.wait_ge(p_ready, b * PAIRS + j - 1)
                    for n in range(2):
                        h = j * 2 + n
                        for s_blk in range(2):
                            nc.tensor.matmul(ps_s[:, j % 2, n, s_blk * T:(s_blk + 1) * T], k_t[:, s_blk], q_t[:, h].rearrange("p c t -> p (c t)"),
                                             start=(s_blk == 0), stop=False)
                        last = nc.tensor.matmul(ps_s[:, j % 2, n].rearrange("p (a t) -> p a t", a=2), m.minus_head[:, h],
                                                max_t[:].rearrange("p (a t) -> p a t", a=1).broadcast_to([HB, 2, T]), start=False, stop=True)
                    last.then_inc(s_ready, 1)

                def weigh(j):
                    pe.wait_ge(p_ready, b * PAIRS + j + 1)
                    if j >= 2:
                        pe.wait_ge(ctx_ready, b * PAIRS + j - 1)
                    for c in range(2):
                        for n in range(2):
                            at = (c * 2 + n) * (KVR + 1)
                            for s_blk in range(2):
                                last = nc.tensor.matmul(ps_o[:, j % 2, at:at + KVR + 1], probs[:, j % 2, n, s_blk, c * P:(c + 1) * P],
                                                        m.keys[:, s_blk, ROPE:], start=(s_blk == 0), stop=(s_blk == 1))
                    last.then_inc(pv_done, 1)

                def turn_ctx(j):
                    pe.wait_ge(ctx_ready, b * PAIRS + j + 1)
                    if j >= 1:
                        pe.wait_ge(ctx_moved, b * PAIRS + j)
                    for c in range(2):
                        last = nc.tensor.transpose(ps_c[:, c * P:(c + 1) * P], ctx_n[:, j % 2, c].rearrange("p n d -> p (n d)"), ident)
                    last.then_inc(ctx_turned, 1)

                def project(j):
                    pe.wait_ge(ctx_moved, b * PAIRS + j + 1)
                    for c in range(2):
                        last = nc.tensor.matmul(ps_y[:, c * D:(c + 1) * D], ctx_t[:, j % 2, c], m.wvo[:, j, :],
                                                start=(j == 0 and c == 0), stop=(j == PAIRS - 1 and c == 1))
                    if j == PAIRS - 1:
                        last.then_inc(y_ready, 1)

                for j in range(PAIRS + 3):
                    for delay, part in enumerate((scores, weigh, turn_ctx, project)):
                        if 0 <= j - delay < PAIRS:
                            part(j - delay)

            pipeline(pe, B, [(0, batch)], 1)

        @block.scalar
        def _(act):
            def batch(b, s, lap):
                act.wait_ge(x_turned, b + 1)
                nc.scalar.copy(x_t[:].rearrange("p k c t -> p (k c t)"), ps_s[:, 0, 0, :]).then_inc(x_t_ready, 1)
                for c in range(2):
                    act.wait_ge(low_ready, b * 2 + c + 1)
                    wait(act, sums_ready, b * 4 + c * 2)
                    nc.scalar.activation(junk[:], ps_s[:, 1, c, 0:QR], ACT.Square, accum_out=sums[:, c, 0:1]).then_inc(sums_ready, 1)
                    act.wait_ge(sums_ready, b * 4 + c * 2 + 1)
                    nc.scalar.activation(junk[:, 0:KVR], ps_s[:, 1, c, QR:QR + KVR], ACT.Square, accum_out=sums[:, c, 1:2]).then_inc(sums_ready, 1)
                act.wait_ge(low_turned, b + 1)
                nc.scalar.copy(q_low_t[:].rearrange("p c t -> p (c t)"), ps_s[0:QR, 0, 0, 0:2 * P])
                nc.scalar.copy(k_t[:].rearrange("p c t -> p (c t)"), ps_s[:, 0, 1, 0:2 * P])
                nc.scalar.copy(k_tb[:].rearrange("p c t -> p (c t)"), ps_s[:, 0, 1, 0:2 * P]).then_inc(low_t_ready, 1)

                def plain(u):
                    act.wait_ge(q_rotated, b * 4 + u + 1)
                    nc.scalar.copy(queries[:, u % 2, :, ROPE:], ps_s[:, u % 2].rearrange("p b n -> p (b n)").rearrange("p (h d) -> p h d", d=DK)[:, :, ROPE:]).then_inc(q_ready, 1)

                def move(u):
                    c, half = u // 2, u % 2
                    act.wait_ge(q_turned, b * 4 + u + 1)
                    nc.scalar.copy(q_t[:, half * HEAD_GROUP:(half + 1) * HEAD_GROUP, c], ps_o[:].rearrange("p b n -> p (b n)").rearrange("p (h t) -> p h t", t=P)).then_inc(q_t_ready, 1)

                skewed(plain, move)

                def exponential(j):
                    act.wait_ge(s_ready, b * PAIRS + j + 1)
                    wait(act, pv_done, b * PAIRS + j - 1)
                    nc.scalar.activation(probs[:, j % 2].rearrange("p n a t -> p n (a t)"), ps_s[:, j % 2], ACT.Exp,
                                         scale=float(DK) ** -0.5).then_inc(p_ready, 1)

                def move_ctx(j):
                    act.wait_ge(ctx_turned, b * PAIRS + j + 1)
                    nc.scalar.copy(ctx_t[:, j % 2].rearrange("p c t -> p (c t)"), ps_c[:, 0:2 * P]).then_inc(ctx_moved, 1)

                for j in range(PAIRS + 2):
                    if j < PAIRS:
                        exponential(j)
                    if j >= 2:
                        move_ctx(j - 2)

            pipeline(act, B, [(0, batch)], 1)

        @block.vector
        def _(dve):
            norm, low = Chain(dve, chain_sem, 4), Chain(dve, low_chain, 2)

            def batch(b, s, lap):
                norm.at(b)
                wait(dve, x_turned, b)
                for c in range(2):
                    normalise_tile(nc, dve, g, m, b * 2 + c, c, b * 2 + c, norm)
                low.at(b)
                cos, sin = (g.const(name).rearrange("p (c o d) -> p c o d", c=2, o=1) for name in ("cos_b", "sin_b"))
                half = ROPE // 2
                for c in range(2):
                    dve.wait_ge(sums_ready, b * 4 + c * 2 + 2)
                    nc.vector.tensor_scalar(means[:, c, 0:1], sums[:, c, 0:1], 1.0 / QR, RMS_EPS_B, ALU.mult, ALU.add)
                    nc.vector.tensor_scalar(means[:, c, 1:2], sums[:, c, 1:2], 1.0 / KVR, RMS_EPS_B, ALU.mult, ALU.add).then_inc(means_ready, 1)
                    src = ps_s[:, 1, c, QR + KVR:NA]
                    nc.vector.tensor_tensor(k_cos[:, c], src, cos[:, c, 0], ALU.mult)
                    nc.vector.tensor_tensor(k_sin[:, c, 0:half], src[:, half:], sin[:, c, 0, 0:half], ALU.mult)
                    low.then(nc.vector.tensor_tensor(k_sin[:, c, half:], src[:, 0:half], sin[:, c, 0, half:], ALU.mult))
                    nc.vector.tensor_tensor(m.keys[:, c, 0:ROPE], k_cos[:, c], k_sin[:, c], ALU.add)
                    dve.wait_ge(inverse_ready, b * 2 + c + 1)
                    nc.vector.tensor_scalar(q_low[:, c], ps_s[:, 1, c, 0:QR], inverse[:, c, 0:1], None, ALU.mult)
                    nc.vector.scalar_tensor_tensor(out=m.keys[:, c, ROPE:DK], in0=ps_s[:, 1, c, QR:QR + KVR], scalar=inverse[:, c, 1:2],
                                                   in1=m.kv_norm[:], op0=ALU.mult, op1=ALU.mult).then_inc(keys_ready, 1)

                def rotate(u):
                    c = u // 2
                    dve.wait_ge(q_made, b * 4 + u + 1)
                    wait(dve, q_turned, b * 4 + u - 1)
                    src = ps_s[:, u % 2].rearrange("p b n -> p (b n)").rearrange("p (h d) -> p h d", d=DK)
                    nc.vector.tensor_tensor(by_cos[:, u % 2], src[:, :, 0:ROPE], cos[:, c].broadcast_to([P, HEAD_GROUP, ROPE]), ALU.mult)
                    nc.vector.tensor_tensor(by_sin[:, u % 2, :, 0:half], src[:, :, half:ROPE], sin[:, c, :, 0:half].broadcast_to([P, HEAD_GROUP, half]), ALU.mult)
                    nc.vector.tensor_tensor(by_sin[:, u % 2, :, half:], src[:, :, 0:half], sin[:, c, :, half:].broadcast_to([P, HEAD_GROUP, half]), ALU.mult).then_inc(rope_sem, 1)
                    dve.wait_ge(rope_sem, b * 4 + u + 1)
                    nc.vector.tensor_tensor(queries[:, u % 2, :, 0:ROPE], by_cos[:, u % 2], by_sin[:, u % 2], ALU.add).then_inc(q_rotated, 1)

                def narrow(u):
                    c, group = u // 2, u % 2
                    dve.wait_ge(q_t_ready, b * 4 + u + 1)
                    heads = slice(group * HEAD_GROUP, (group + 1) * HEAD_GROUP)
                    nc.vector.tensor_copy(q_tb[:, heads, c], q_t[:, heads, c]).then_inc(q_tb_ready, 1)

                skewed(rotate, narrow)
                for j in range(PAIRS):
                    dve.wait_ge(smax_ready, b * PAIRS + j + 1)
                    nc.vector.tensor_reduce(row_max[:, :, j * 2:j * 2 + 2], ps_s[:, j % 2].rearrange("p c (n s) -> p c n s", n=2), AX.X, ALU.max).then_inc(smax_read, 1)
                dve.wait_ge(max_turned, b + 1)
                nc.vector.tensor_copy(max_t[:], ps_s[0:HB, 0, 0, :].bitcast(BF16)[:, 0:2 * P]).then_inc(max_t_ready, 1)
                for j in range(PAIRS):
                    dve.wait_ge(pv_done, b * PAIRS + j + 1)
                    out = ps_o[:, j % 2, 0:4 * (KVR + 1)].rearrange("p (c n d) -> p c n d", c=2, n=2)
                    nc.vector.reciprocal(recip[:, j % 2], out[:, :, :, KVR:]).then_inc(recips, 1)
                    dve.wait_ge(recips, b * PAIRS + j + 1)
                    wait(dve, ctx_turned, b * PAIRS + j - 1)
                    nc.vector.tensor_tensor(ctx_n[:, j % 2], out[:, :, :, 0:KVR],
                                            recip[:, j % 2].broadcast_to([P, 2, 2, KVR]),
                                            ALU.mult).then_inc(ctx_ready, 1)
                dve.wait_ge(y_ready, b + 1)
                nc.vector.tensor_tensor(g.x[:, bass.ds(b * 2, 2), :], g.x[:, bass.ds(b * 2, 2), :], ps_y[:].rearrange("p (c d) -> p c d", c=2), ALU.add).then_inc(x_added, 1)

            pipeline(dve, B, [(0, batch)], 1)
            dve.wait_ge(x_added, B)



def ffn_router(nc, g, tag):
    with ExitStack() as ctx:
        m = Memory(nc, ctx, tag + "_router")
        stats, mv = m.sb("stats", [P, 2, 6]), m.sb("mv", [P, 2, 2])
        rstd, ssq, rrms = m.sb("rstd", [P, 2]), m.sb("ssq", [P, 2]), m.sb("rrms", [P, 2])
        veps, meps, pause = m.sb("veps", [P, 2]), m.sb("meps", [P, 2]), m.sb("pause", [P, 1], U32)
        veps_ready, rstd_ready, meps_ready = m.sem("veps_ready"), m.sem("rstd_ready"), m.sem("meps_ready")
        h, junk, xin = m.sb("h", [P, 2, D]), m.sb("junk", [P, D]), m.sb("xin", [P, 2, D])
        xin_t, act_t = m.sb("xin_t", [P, 2, KD, P]), m.sb("act_t", [P, 2, P])
        silu, act = m.sb("silu", [P, 2, INNER]), m.sb("act", [P, 2, INNER])
        logits, top8, idx8 = m.sb("logits", [P, 2, E]), m.sb("top8", [P, 2, 8]), m.sb("idx8", [P, 2, 8], U32)
        ps_t, ps_g, ps_o = m.ps("ps_t", [P, 2, 512]), m.ps("ps_g", [P, 2, 512]), m.ps("ps_o", [P, 2, 512])
        norm_chain, route_chain = m.sem("norm_chain"), m.sem("route_chain")
        h_ready, ssq_ready, xin_ready, xin_kept = m.sem("h_ready"), m.sem("ssq_ready"), m.sem("xin_ready"), m.sem("xin_kept")
        turned, xin_t_ready, gates_ready, silu_ready = m.sem("turned"), m.sem("xin_t_ready"), m.sem("gates_ready"), m.sem("silu_ready")
        act_ready, act_turned, act_t_ready, down_ready = m.sem("act_ready"), m.sem("act_turned"), m.sem("act_t_ready"), m.sem("down_ready")
        logits_read, rrms_ready, x_added = m.sem("logits_read"), m.sem("rrms_ready"), m.sem("x_added")
        ident = g.const("ident")
        block = ctx.enter_context(nc.Block())

        @block.vector
        def _(dve):
            norm, route = Chain(dve, norm_chain, 3), Chain(dve, route_chain, 3)

            def normalise(i, s, lap):
                norm.at(i)
                norm.then(nc.vector.bn_stats(stats[:, s], g.x[:, i, :]))
                nc.vector.memset(pause[:], 0)
                norm.then(nc.vector.bn_aggr(mv[:, s], stats[:, s]))
                nc.vector.tensor_scalar(veps[:, s:s + 1], mv[:, s, 1:2], LN_EPS, None, ALU.add).then_inc(veps_ready, 1)
                dve.wait_ge(rstd_ready, i + 1)
                nc.vector.tensor_scalar(h[:, s], g.x[:, i, :], mv[:, s, 0:1], rstd[:, s:s + 1],
                                        ALU.subtract, ALU.mult).then_inc(h_ready, 1)
                dve.wait_ge(h_ready, i + 1)
                norm.then(nc.vector.tensor_tensor(g.x[:, i, :], g.x[:, i, :], h[:, s], ALU.add))
                dve.wait_ge(ssq_ready, i + 1)
                nc.vector.tensor_scalar(meps[:, s:s + 1], ssq[:, s:s + 1], 1.0 / D, RMS_EPS, ALU.mult, ALU.add).then_inc(meps_ready, 1)
                dve.wait_ge(rrms_ready, i + 1)
                wait(dve, turned, i - 1)
                wait(dve, xin_kept, i - 1)
                nc.vector.scalar_tensor_tensor(out=xin[:, s], in0=h[:, s], scalar=rrms[:, s:s + 1], in1=g.norm_w[:],
                                               op0=ALU.mult, op1=ALU.mult).then_inc(xin_ready, 1)

            def route_tile(i, s, lap):
                dve.wait_ge(gates_ready, i + 1)
                route.at(i)
                nc.vector.tensor_copy(logits[:, s], ps_g[:, s, 0:E]).then_inc(logits_read, 1)
                dve.wait_ge(silu_ready, i + 1)
                wait(dve, act_turned, i - 1)
                nc.vector.tensor_tensor(act[:, s], silu[:, s], ps_g[:, s, E + INNER:GATES], ALU.mult).then_inc(act_ready, 1)
                dve.wait_ge(logits_read, i + 1)
                nc.vector.memset(pause[:], 0)
                route.then(nc.vector.max(top8[:, s], logits[:, s]))
                nc.vector.memset(pause[:], 0)
                route.then(nc.vector.max_index(idx8[:, s], top8[:, s], logits[:, s]))
                nc.vector.tensor_copy(g.top[:, i, :], top8[:, s, 0:TOPK])
                route.then(nc.vector.tensor_copy(g.chosen[:, i, :], idx8[:, s, 0:TOPK]))

            def add_shared(i, s, lap):
                dve.wait_ge(down_ready, i + 1)
                nc.vector.tensor_tensor(g.x[:, i, :], g.x[:, i, :], ps_o[:, s, 0:D], ALU.add).then_inc(x_added, 1)

            pipeline(dve, TILES, [(0, normalise), (1, route_tile), (2, add_shared)], 2)
            dve.wait_ge(x_added, TILES)

        @block.gpsimd
        def _(pool):
            def keep(i, s, lap):
                pool.wait_ge(veps_ready, i + 1)
                nc.gpsimd.tensor_tensor(rstd[:, s:s + 1], veps[:, s:s + 1], g.minus_half[:], ALU.pow).then_inc(rstd_ready, 1)
                pool.wait_ge(meps_ready, i + 1)
                nc.gpsimd.tensor_tensor(rrms[:, s:s + 1], meps[:, s:s + 1], g.minus_half[:], ALU.pow).then_inc(rrms_ready, 1)
                pool.wait_ge(xin_ready, i + 1)
                nc.gpsimd.tensor_copy(g.xin[:, i, :], xin[:, s]).then_inc(xin_kept, 1)

            pipeline(pool, TILES, [(0, keep)], 2)
            pool.wait_ge(xin_kept, TILES)

        @block.scalar
        def _(act_e):
            def squares(i, s, lap):
                act_e.wait_ge(h_ready, i + 1)
                wait(act_e, ssq_ready, i)
                nc.scalar.activation(junk[:], h[:, s], ACT.Square, accum_out=ssq[:, s:s + 1]).then_inc(ssq_ready, 1)

            def move_xin(i, s, lap):
                act_e.wait_ge(turned, i + 1)
                wait(act_e, gates_ready, i - 1)
                nc.scalar.copy(xin_t[:, s], ps_t[:, s, 0:D].rearrange("p (k t) -> p k t", k=KD)).then_inc(xin_t_ready, 1)

            def gate_silu(i, s, lap):
                act_e.wait_ge(logits_read, i + 1)
                wait(act_e, act_ready, i - 1)
                nc.scalar.activation(silu[:, s], ps_g[:, s, E:E + INNER], ACT.Silu).then_inc(silu_ready, 1)

            def move_act(i, s, lap):
                act_e.wait_ge(act_turned, i + 1)
                wait(act_e, down_ready, i - 1)
                nc.scalar.copy(act_t[:, s], ps_o[:, s, D:D + P]).then_inc(act_t_ready, 1)

            pipeline(act_e, TILES, [(0, squares), (0, move_xin), (1, gate_silu), (1, move_act)], 2)

        @block.tensor
        def _(pe):
            def turn(i, s, lap):
                pe.wait_ge(xin_ready, i + 1)
                wait(pe, xin_t_ready, i - 1)
                for k in range(KD):
                    last = nc.tensor.transpose(ps_t[:, s, k * P:(k + 1) * P], xin[:, s, k * P:(k + 1) * P], ident)
                last.then_inc(turned, 1)

            def gates(i, s, lap):
                pe.wait_ge(xin_t_ready, i + 1)
                wait(pe, act_ready, i - 1)
                wait(pe, logits_read, i - 1)
                for k in range(KD):
                    last = nc.tensor.matmul(ps_g[:, s, 0:GATES], xin_t[:, s, k], g.w_gates[:, k, :], start=(k == 0), stop=(k == KD - 1))
                last.then_inc(gates_ready, 1)

            def down(i, s, lap):
                pe.wait_ge(act_ready, i + 1)
                wait(pe, x_added, i - 1)
                nc.tensor.transpose(ps_o[:, s, D:D + P], act[:, s], ident).then_inc(act_turned, 1)
                pe.wait_ge(act_t_ready, i + 1)
                nc.tensor.matmul(ps_o[:, s, 0:D], act_t[:, s], g.w_down[:], start=True, stop=True).then_inc(down_ready, 1)

            pipeline(pe, TILES, [(0, turn), (0, gates), (1, down)], 2)



def ffn_route(nc, g, tag):
    with ExitStack() as ctx:
        m = Memory(nc, ctx, tag + "_route")
        hot, prod = m.sb("hot", [P, TOPK, TILES, E]), m.sb("prod", [P, TILES, E])
        sums = [m.sb(f"sum{i}", [P, TILES, E]) for i in range(2)]
        scan = [m.sb(f"scan{i}", [P, TILES, E]) for i in range(2)]
        count, nblocks = m.sb("count", [P, E]), [m.sb(f"nblocks{i}", [P, E]) for i in range(2)]
        ends = [m.sb(f"ends{i}", [P, E]) for i in range(2)]
        base, slot, over = m.sb("base", [P, E]), m.sb("slot", [P, TILES, E]), m.sb("over", [P, TILES, E])
        passed, owner, slots = m.sb("passed", [P, E]), m.sb("owner", [P, 1]), m.sb("slots", [P, TILES, TOPK])
        kept, off, total = m.sb("kept", [P, TILES, TOPK]), m.sb("off", [P, TILES, TOPK]), m.sb("total", [P, TILES])
        ps_pos, ps_cnt = m.ps("ps_pos", [P, 512]), m.ps("ps_cnt", [P, 512])
        chain, scanned, counted, owned, turned = m.sem("chain"), m.sem("scanned"), m.sem("counted"), m.sem("owned"), m.sem("turned")
        diffs, exps = m.sem("diffs"), m.sem("exps")
        block = ctx.enter_context(nc.Block())

        @block.tensor
        def _(pe):
            pe.wait_ge(scanned, 1)
            nc.tensor.matmul(ps_pos[:], g.const("before"), sums[0][:].rearrange("p a e -> p (a e)"), start=True, stop=False)
            nc.tensor.matmul(ps_pos[:, E:], g.ones[:], scan[0][:, 0:TILES - 1].rearrange("p a e -> p (a e)"), start=False, stop=True)
            nc.tensor.matmul(ps_cnt[:, 0:E], g.ones[:], scan[0][:, TILES - 1], start=True, stop=True).then_inc(counted, 1)
            pe.wait_ge(owned, 1)
            nc.tensor.matmul(ps_cnt[0:1, P:2 * P], owner[:], g.const("ident"), start=True, stop=True).then_inc(turned, 1)

        @block.scalar
        def _(act):
            act.wait_ge(diffs, 1)
            nc.scalar.activation(off[:], off[:], ACT.Exp).then_inc(exps, 1)

        @block.vector
        def _(dve):
            link = Chain(dve, chain, 0).then
            v = nc.vector
            link(v.tensor_tensor(off[:], g.top[:], g.top[:, :, 0:1].broadcast_to([P, TILES, TOPK]), ALU.subtract))
            v.tensor_copy(passed[:, 0:1], g.consts[:, 0:1]).then_inc(diffs, 1)
            experts = g.const("experts").rearrange("p (a e) -> p a e", a=1).broadcast_to([P, TILES, E])
            for k in range(TOPK):
                link(v.tensor_tensor(hot[:, k], experts, g.chosen[:, :, k:k + 1].broadcast_to([P, TILES, E]), ALU.is_equal))
            link(v.tensor_tensor(sums[0][:], hot[:, 0], hot[:, 1], ALU.add))
            link(v.tensor_tensor(sums[1][:], sums[0][:], hot[:, 2], ALU.add))
            link(v.tensor_tensor(sums[0][:], sums[1][:], hot[:, 3], ALU.add))
            src = sums[0]
            for n, step in enumerate((1, 2, 4, 8)):
                dst = scan[(n + 1) % 2]
                link(v.tensor_copy(dst[:, 0:step], src[:, 0:step]))
                link(v.tensor_tensor(dst[:, step:], src[:, step:], src[:, 0:TILES - step], ALU.add))
                src = dst
            v.tensor_copy(passed[:, 0:1], g.consts[:, 0:1]).then_inc(scanned, 1)
            dve.wait_ge(exps, 1)
            link(v.tensor_reduce(total[:], off[:], AX.X, ALU.add))
            link(v.reciprocal(total[:], total[:]))
            link(v.tensor_tensor(g.weight[:], off[:], total[:].rearrange("p (a o) -> p a o", o=1).broadcast_to([P, TILES, TOPK]), ALU.mult))
            dve.wait_ge(counted, 1)
            link(v.tensor_copy(count[:], ps_cnt[:, 0:E]))
            link(v.tensor_scalar(nblocks[0][:], count[:], 0.0, None, ALU.is_gt))
            for n, at in enumerate(range(P, CAP, P)):
                link(v.scalar_tensor_tensor(out=nblocks[(n + 1) % 2][:], in0=count[:], scalar=float(at), in1=nblocks[n % 2][:],
                                            op0=ALU.is_gt, op1=ALU.add))
            nb = nblocks[(CAP // P - 1) % 2]
            src, step, n = nb, 1, 0
            while step < E:
                dst = ends[n % 2]
                link(v.tensor_copy(dst[:, 0:step], src[:, 0:step]))
                link(v.tensor_tensor(dst[:, step:], src[:, step:], src[:, 0:E - step], ALU.add))
                src, step, n = dst, 2 * step, n + 1
            link(v.tensor_scalar(passed[:], src[:], g.const("blocks"), None, ALU.is_le))
            link(v.tensor_reduce(owner[:], passed[:], AX.X, ALU.add))
            link(v.tensor_scalar(owner[:], owner[:], float(E - 1), None, ALU.min))
            v.tensor_copy(passed[:, 0:1], g.consts[:, 0:1]).then_inc(owned, 1)
            link(v.tensor_tensor(base[:], src[:], nb[:], ALU.subtract))
            link(v.tensor_scalar(base[:], base[:], float(P), None, ALU.mult))
            pos = ps_pos[:].rearrange("p (a e) -> p a e", e=E)
            link(v.tensor_scalar(over[:], pos, float(CAP), float(DROPPED), ALU.is_ge, ALU.mult))
            link(v.scalar_tensor_tensor(out=slot[:], in0=pos, scalar=float(CAP - 1),
                                        in1=base[:].rearrange("p (a e) -> p a e", a=1).broadcast_to([P, TILES, E]),
                                        op0=ALU.min, op1=ALU.add))
            link(v.tensor_tensor(slot[:], slot[:], over[:], ALU.add))
            for k in range(TOPK):
                link(v.tensor_tensor(prod[:], hot[:, k], slot[:], ALU.mult))
                link(v.tensor_reduce(slots[:, :, k], prod[:], AX.X, ALU.add))
            link(v.tensor_copy(g.slot_in[:], slots[:]))
            link(v.tensor_scalar(kept[:], slots[:], float(DROPPED), float(-DROPPED), ALU.is_ge, ALU.mult))
            link(v.tensor_tensor(kept[:], kept[:], slots[:], ALU.add))
            link(v.tensor_copy(g.slot_out[:], kept[:]))
            dve.wait_ge(turned, 1)
            link(v.tensor_copy(g.owner[:], ps_cnt[0:1, P:2 * P]))


def ffn_dispatch(nc, g, tag):
    with ExitStack() as ctx:
        m = Memory(nc, ctx, tag + "_dispatch")
        sent = m.sem("sent")
        block = ctx.enter_context(nc.Block())

        @block.gpsimd
        def _(pool):
            for i in range(TILES):
                for k in range(TOPK):
                    nc.gpsimd.indirect_dma_start(
                        out=g.slots_in, out_offset=bass.IndirectOffsetOnAxis(ap=g.slot_in[:, i, k:k + 1], axis=0),
                        in_=g.xin[:, i, :], in_offset=None, bounds_check=SLOTS - 1, oob_is_err=False).then_inc(sent, 16)
            pool.wait_ge(sent, 16 * TILES * TOPK)


def ffn_experts(nc, g, tag):
    with ExitStack() as ctx:
        m = Memory(nc, ctx, tag + "_experts")
        rows, rows_t = m.sb("rows", [P, RING, D]), m.sb("rows_t", [P, 4, KD, P])
        silu = m.sb("silu", [P, 4, INNER])
        act, act_t, res = m.sb("act", [P, 4, INNER]), m.sb("act_t", [P, 4, P]), m.sb("res", [P, RING, D])
        ps_t, ps_g, ps_o = m.ps("ps_t", [P, 2, 512]), m.ps("ps_g", [P, 2, 512]), m.ps("ps_o", [P, 2, 512])
        loads = [m.sem(f"loaded{r}") for r in range(RING)]
        stores = [m.sem(f"stored{r}") for r in range(RING)]
        turned, rows_t_ready, gu_ready = m.sem("turned"), m.sem("rows_t_ready"), m.sem("gu_ready")
        silu_ready, act_ready, act_turned, act_t_ready = m.sem("silu_ready"), m.sem("act_ready"), m.sem("act_turned"), m.sem("act_t_ready")
        out_ready, res_ready = m.sem("out_ready"), m.sem("res_ready")
        ident = g.const("ident")
        block = ctx.enter_context(nc.Block())

        @block.sync
        def _(sp):
            def load(j, s, lap):
                wait(sp, turned, j - RING + 1)
                sp.dma_start(rows[:, s], g.slots_in[bass.ts(j, P), :]).then_inc(loads[s], 16)

            def store(j, s, lap):
                sp.wait_ge(res_ready, j + 1)
                sp.dma_start(g.slots_out[bass.ts(j, P), :], res[:, s]).then_inc(stores[s], 16)

            pipeline(sp, BLOCKS, [(5, store), (0, load)], RING)
            for s in range(RING):
                sp.wait_ge(stores[s], 16 * (BLOCKS // RING))

        @block.tensor
        def _(pe):
            def turn(j, s, lap):
                pe.wait_ge(loads[s], lap * 16 + 16)
                wait(pe, rows_t_ready, j - 1)
                for k in range(KD):
                    last = nc.tensor.transpose(ps_t[:, s % 2, k * P:(k + 1) * P], rows[:, s, k * P:(k + 1) * P], ident)
                last.then_inc(turned, 1)

            def gate_up(j, s, lap):
                e = pe.value_load(g.owner[0:1, bass.ds(j, 1)], min_val=0, max_val=E - 1)
                pe.wait_ge(rows_t_ready, j + 1)
                wait(pe, act_ready, j - 1)
                for k in range(KD):
                    last = nc.tensor.matmul(ps_g[:, s % 2, 0:2 * INNER], rows_t[:, s % 4, k],
                                            g.w13[:, bass.ds(e, 1), k, :].rearrange("p o f -> p (o f)"), start=(k == 0), stop=(k == KD - 1))
                last.then_inc(gu_ready, 1)

            def turn_act(j, s, lap):
                pe.wait_ge(act_ready, j + 1)
                wait(pe, res_ready, j - 1)
                nc.tensor.transpose(ps_o[:, s % 2, D:D + P], act[:, s % 4], ident).then_inc(act_turned, 1)

            def down(j, s, lap):
                e = pe.value_load(g.owner[0:1, bass.ds(j, 1)], min_val=0, max_val=E - 1)
                pe.wait_ge(act_t_ready, j + 1)
                nc.tensor.matmul(ps_o[:, s % 2, 0:D], act_t[:, s % 4], g.w2[:, bass.ds(e, 1), :].rearrange("p o f -> p (o f)"),
                                 start=True, stop=True).then_inc(out_ready, 1)

            pipeline(pe, BLOCKS, [(0, turn), (1, gate_up), (2, turn_act), (3, down)], RING)

        @block.scalar
        def _(act_e):
            def move_rows(j, s, lap):
                act_e.wait_ge(turned, j + 1)
                wait(act_e, gu_ready, j - 3)
                nc.scalar.copy(rows_t[:, s % 4], ps_t[:, s % 2, 0:D].rearrange("p (k t) -> p k t", k=KD)).then_inc(rows_t_ready, 1)

            def gate_silu(j, s, lap):
                act_e.wait_ge(gu_ready, j + 1)
                wait(act_e, act_ready, j - 3)
                nc.scalar.activation(silu[:, s % 4], ps_g[:, s % 2, 0:INNER], ACT.Silu).then_inc(silu_ready, 1)

            def move_act(j, s, lap):
                act_e.wait_ge(act_turned, j + 1)
                wait(act_e, out_ready, j - 3)
                nc.scalar.copy(act_t[:, s % 4], ps_o[:, s % 2, D:D + P]).then_inc(act_t_ready, 1)

            pipeline(act_e, BLOCKS, [(0, move_rows), (1, gate_silu), (2, move_act)], RING)

        @block.vector
        def _(dve):
            def activate(j, s, lap):
                dve.wait_ge(silu_ready, j + 1)
                wait(dve, act_turned, j - 3)
                nc.vector.tensor_tensor(act[:, s % 4], silu[:, s % 4], ps_g[:, s % 2, INNER:2 * INNER], ALU.mult).then_inc(act_ready, 1)

            def move_out(j, s, lap):
                dve.wait_ge(out_ready, j + 1)
                wait(dve, stores[s], lap * 16)
                nc.vector.tensor_copy(res[:, s], ps_o[:, s % 2, 0:D]).then_inc(res_ready, 1)

            pipeline(dve, BLOCKS, [(1, activate), (3, move_out)], RING)


def ffn_combine(nc, g, tag):
    with ExitStack() as ctx:
        m = Memory(nc, ctx, tag + "_combine")
        DEEP = 8
        got = m.sb("got", [P, DEEP, D])
        gathered = [m.sem(f"gathered{r}") for r in range(DEEP)]
        added = m.sem("added")
        block = ctx.enter_context(nc.Block())

        @block.gpsimd
        def _(pool):
            for n in range(TILES * TOPK):
                wait(pool, added, n - DEEP + 1)
                nc.gpsimd.indirect_dma_start(
                    out=got[:, n % DEEP], out_offset=None, in_=g.slots_out,
                    in_offset=bass.IndirectOffsetOnAxis(ap=g.slot_out[:, n // TOPK, n % TOPK:n % TOPK + 1], axis=0),
                    bounds_check=SLOTS - 1, oob_is_err=False).then_inc(gathered[n % DEEP], 16)

        @block.vector
        def _(dve):
            for n in range(TILES * TOPK):
                i, k = n // TOPK, n % TOPK
                dve.wait_ge(gathered[n % DEEP], 16 * (n // DEEP + 1))
                wait(dve, added, n)
                nc.vector.scalar_tensor_tensor(out=g.x[:, i, :], in0=got[:, n % DEEP], scalar=g.weight[:, i, k:k + 1],
                                               in1=g.x[:, i, :], op0=ALU.mult, op1=ALU.add).then_inc(added, 1)
            dve.wait_ge(added, TILES * TOPK)


def ffn(nc, g, tag):
    with nc.sbuf_tensor(f"{tag}_xin", [P, TILES, D], F32) as g.xin:
        ffn_router(nc, g, tag)
        ffn_route(nc, g, tag)
        ffn_dispatch(nc, g, tag)
        ffn_experts(nc, g, tag)
        ffn_combine(nc, g, tag)


def store_all(nc, g, out):
    with ExitStack() as ctx:
        stored = Memory(nc, ctx, "store").sem("stored")
        block = ctx.enter_context(nc.Block())

        @block.sync
        def _(sp):
            sp.dma_start(out.rearrange("b (h p) d -> p (b h) d", p=P), g.x[:]).then_inc(stored, 16)
            sp.wait_ge(stored, 16)


class Globals:

    def __init__(self, nc, ctx):
        m = Memory(nc, ctx, "g")
        self.consts = m.sb("consts", [P, CONST_COLS])
        self.ones, self.minus_half = m.sb("ones", [P, P]), m.sb("minus_half", [P, 1])
        self.x = m.sb("x", [P, TILES, D])
        self.w_gates, self.w_down = m.sb("w_gates", [P, KD, GATES]), m.sb("w_down", [P, D])
        self.norm_w = m.sb("norm_w", [P, D])
        self.w13, self.w2 = m.sb("w13", [P, E, KD, 2 * INNER]), m.sb("w2", [P, E, D])
        self.top, self.chosen = m.sb("top", [P, TILES, TOPK]), m.sb("chosen", [P, TILES, TOPK])
        self.weight = m.sb("weight", [P, TILES, TOPK])
        self.slot_in, self.slot_out = m.sb("slot_in", [P, TILES, TOPK], U32), m.sb("slot_out", [P, TILES, TOPK], U32)
        self.owner = m.sb("owner", [1, P], I32)
        self.slots_in = nc.dram_tensor("slots_in", [SLOTS, D], F32, kind="Internal").ap()
        self.slots_out = nc.dram_tensor("slots_out", [SLOTS, D], F32, kind="Internal").ap()

    def const(self, name):
        a, b = CONST[name]
        return self.consts[:, a:b]


def build(nc, dram, out):
    Memory.sems.clear()
    with ExitStack() as ctx:
        g = Globals(nc, ctx)
        load_all(nc, g, dram)
        if "a" in STAGES:
            attention_a(nc, g, dram)
        if "f" in STAGES:
            ffn(nc, g, "f1")
        zero_semaphores(nc)
        if "b" in STAGES:
            attention_b(nc, g, dram)
        if "F" in STAGES:
            ffn(nc, g, "f2")
        store_all(nc, g, out)


def kernel(**inputs):
    import concourse.bacc as bacc
    from concourse.bass_utils import run_bass_kernel_spmd

    nc = bacc.Bacc("TRN2", target_bir_lowering=False, num_devices=1)
    laid = {
        "x": inputs["L0_attn_a_x"], "consts": constants(),
        "gate_t": np.asarray(inputs["L0_ffn_gate_w"]).T,
    }
    for name in inputs:
        if name not in ("L0_attn_a_x", "L0_ffn_gate_w"):
            laid[name.replace("L0_ffn_", "").replace("L0_attn_a_", "a_").replace("L0_attn_b_", "b_")] = np.asarray(inputs[name])
    wq = laid.pop("a_Wq").reshape(D, GA // 2, 2, REP, DA).transpose(0, 1, 3, 2, 4).reshape(D, HA * DA)
    laid["a_Wqkv"] = np.concatenate([wq, laid.pop("a_Wk"), laid.pop("a_Wv")], 1)
    wq_b = laid.pop("b_wq_b").reshape(QR, HB, DK)
    laid["b_wqn_t"], laid["b_wqp"] = wq_b[:, :, :NOPE].transpose(2, 1, 0), wq_b[:, :, NOPE:]
    wkv_b = laid.pop("b_wkv_b").reshape(KVR, HB, NOPE + VD)
    laid["b_wk_t"], laid["b_wv_t"] = wkv_b[:, :, :NOPE].transpose(2, 1, 0), wkv_b[:, :, NOPE:].transpose(2, 1, 0)
    laid["b_w_a"] = np.concatenate([laid.pop("b_wq_a"), laid.pop("b_wkv_a")], 1)
    arrays, dram = {}, {}
    for name, value in laid.items():
        value = np.ascontiguousarray(value)
        arrays[f"in_{name}"] = value
        dram[name] = nc.dram_tensor(f"in_{name}", value.shape, mybir.dt.from_np(value.dtype), kind="ExternalInput").ap()
    out = nc.dram_tensor("out_x", (B, T, D), F32, kind="ExternalOutput").ap()
    build(nc, dram, out)
    return run_bass_kernel_spmd(nc, [arrays], core_ids=[0]).results[0]["out_x"]
```

```python
from contextlib import ExitStack

import numpy as np

import concourse.bass as bass
from concourse import mybir

ALU = mybir.AluOpType
ACT = mybir.ActivationFunctionType
AX = mybir.AxisListType
F32 = mybir.dt.float32
BF16 = mybir.dt.bfloat16
U32 = mybir.dt.uint32
I32 = mybir.dt.int32

P = 128
B, T, D = 8, 256, 256
NTOK = B * T
TILES = NTOK // P
KD = D // P
LN_EPS = 1e-5

E, TOPK, INNER = 32, 4, 128
CAP = 2 * NTOK * TOPK // E
RMS_EPS = 1e-6
RING = 8
BLOCKS = -(-((NTOK * TOPK + E * (P - 1)) // P) // RING) * RING
SLOTS = E * CAP + P
TABLE_PAD = 4 + RING // 2
GATES = E + 2 * INNER

HA, GA, DA = 32, 8, 8
REP = HA // GA
STACK = 64
HB, DK, ROPE, NOPE, VD, KVR, QR = 16, 128, 64, 64, 128, 64, 96

CLEAR_BLOCKS = 16
CLEARS = -(-SLOTS // (P * CLEAR_BLOCKS))

NEG = -1e30
DROPPED = 1 << 16

_WIDTHS = [("ident", P), ("before", P), ("future", P), ("cos_a", 2 * DA), ("sin_a", 2 * DA),
           ("cos_b", 2 * ROPE), ("sin_b", 2 * ROPE), ("first_slots", E), ("blocks", 1), ("row_mod", REP), ("minus_group", GA)]
CONST = {}
_at = 0
for _name, _w in _WIDTHS:
    CONST[_name] = (_at, _at + _w)
    _at += _w
CONST_COLS = _at


def constants():
    c = np.zeros((P, CONST_COLS), np.float32)

    def put(name, value):
        a, b = CONST[name]
        c[:, a:b] = value

    p = np.arange(P)
    put("ident", np.eye(P))
    put("before", p[:, None] < p[None, :])
    put("future", np.where(p[None, :] > p[:, None], NEG, 0.0))
    for name, dim in (("a", DA), ("b", ROPE)):
        theta = (np.float32(1.0) / np.float32(10000.0) ** (np.arange(0, dim, 2, dtype=np.float32) / np.float32(dim))).astype(np.float32)
        angle = np.outer(np.arange(T, dtype=np.float32), theta).astype(np.float32)
        cos, sin = np.cos(angle), np.sin(angle)
        both = np.concatenate([cos, cos], 1).reshape(2, P, dim).transpose(1, 0, 2)
        sign = np.concatenate([-sin, sin], 1).reshape(2, P, dim).transpose(1, 0, 2)
        put("cos_" + name, both.reshape(P, 2 * dim))
        put("sin_" + name, sign.reshape(P, 2 * dim))
    put("first_slots", CAP * np.arange(E)[None, :])
    put("blocks", p[:, None])
    put("row_mod", (p[:, None] % REP) == np.arange(REP)[None, :])
    put("minus_group", -1.0 * ((p[:, None] // REP) == np.arange(GA)[None, :]))
    return c


def wait(eng, sem, value):
    if not (isinstance(value, int) and value <= 0):
        eng.wait_ge(sem, value)


class Chain:

    def __init__(self, eng, sem, per):
        self.eng, self.sem, self.per, self.k, self.i = eng, sem, per, 0, 0

    def at(self, i):
        assert self.k in (0, self.per), (self.k, self.per)
        self.i, self.k = i, 0

    def then(self, ins):
        self.k += 1
        ins.then_inc(self.sem, 1)
        self.eng.wait_ge(self.sem, self.i * self.per + self.k)


def pipeline(eng, n, stages, ring, at_lap=None):
    depth = max(d for d, _ in stages)

    def emit(t):
        if at_lap and t % ring == 0:
            at_lap(t // ring)
        for d, body in stages:
            if 0 <= t - d < n:
                body(t - d, (t - d) % ring, (t - d) // ring)

    first = -(-(depth + ring) // ring)
    last = n // ring
    for t in range(min(first, last) * ring):
        emit(t)
    if last > first:
        with eng.Fori(first, last) as lap:
            if at_lap:
                at_lap(lap)
            for u in range(ring):
                for d, body in stages:
                    off = u - d
                    body(lap * ring + off, off % ring, lap + off // ring)
    for t in range(max(first, last) * ring, n + depth):
        emit(t)


class Memory:

    sems = []

    def __init__(self, nc, ctx, tag):
        self.nc, self.ctx, self.tag = nc, ctx, tag

    def sb(self, name, shape, dt=F32):
        return self.ctx.enter_context(self.nc.sbuf_tensor(f"{self.tag}_{name}", shape, dt))

    def ps(self, name, shape, dt=F32):
        return self.ctx.enter_context(self.nc.psum_tensor(f"{self.tag}_{name}", shape, dt))

    def sem(self, name):
        Memory.sems.append(self.nc.alloc_semaphore(name=f"{self.tag}_{name}"))
        return Memory.sems[-1]


def zero_semaphores(nc):
    nc.clear_and_free_semaphores(Memory.sems)
    Memory.sems.clear()
    nc.all_engine_barrier()



def load_all(nc, g, dram):
    with ExitStack() as ctx:
        m = Memory(nc, ctx, "load")
        loaded, made = m.sem("loaded"), m.sem("made")
        block = ctx.enter_context(nc.Block())

        @block.sync
        def _(sp):
            sp.dma_start(g.consts[:], dram["consts"]).then_inc(loaded, 16)
            sp.dma_start(g.x[:, 0:2], dram["x"][0].rearrange("(h p) d -> p h d", p=P)).then_inc(loaded, 16)
            sp.wait_ge(loaded, 32)

        @block.vector
        def _(dve):
            nc.vector.memset(g.ones[:], 1.0).then_inc(made, 1)
            nc.vector.memset(g.minus_half[:], -0.5).then_inc(made, 1)
            nc.vector.memset(g.owner[:], 0).then_inc(made, 1)
            nc.vector.memset(g.place[:], 0).then_inc(made, 1)
            dve.wait_ge(made, 4)


def load_weights(sp, g, zeros, dram):
    for dst, src in ((g.w_gates[:, :, 0:E], dram["gate_t"]), (g.w_gates[:, :, E:E + INNER], dram["shared_gate_w"]),
                     (g.w_gates[:, :, E + INNER:GATES], dram["shared_up_w"])):
        sp.dma_start(dst, src.rearrange("(k p) e -> p k e", p=P)).then_inc(g.weights_loaded, 16)
    sp.dma_start(g.w_down[:], dram["shared_down_w"]).then_inc(g.weights_loaded, 16)
    sp.dma_start(g.norm_w[:], dram["norm_w"].rearrange("(a d) -> a d", a=1).broadcast_to([P, D])).then_inc(g.weights_loaded, 16)
    for e in range(0, E, 8):
        sp.dma_start(g.w13[:, e:e + 8], dram["w13"][e:e + 8].rearrange("e (k p) f -> p e k f", p=P)).then_inc(g.weights_loaded, 16)
        sp.dma_start(g.w2[:, e:e + 8], dram["w2"][e:e + 8].rearrange("e i h -> i e h")).then_inc(g.weights_loaded, 16)
    for n in range(CLEARS):
        blocks = min(CLEAR_BLOCKS, SLOTS // P - n * CLEAR_BLOCKS)
        at = n * CLEAR_BLOCKS * P
        sp.dma_start(g.slots_in[at:at + blocks * P].rearrange("(r p) d -> p r d", p=P),
                     zeros[:].rearrange("p (o d) -> p o d", o=1).broadcast_to([P, blocks, D])).then_inc(g.cleared, 16)



def normalise_tile(nc, dve, g, m, i, c, count, chain):
    chain.then(nc.vector.bn_stats(m.stats[:, c], g.x[:, i, :]))
    nc.vector.memset(m.pause[:], 0)
    chain.then(nc.vector.bn_aggr(m.mv[:, c], m.stats[:, c]))
    nc.vector.tensor_scalar(m.veps[:, c:c + 1], m.mv[:, c, 1:2], LN_EPS, None, ALU.add).then_inc(m.veps_ready, 1)
    dve.wait_ge(m.rstd_ready, count + 1)
    nc.vector.tensor_scalar(m.xn[:, c], g.x[:, i, :], m.mv[:, c, 0:1], m.rstd[:, c:c + 1],
                            ALU.subtract, ALU.mult).then_inc(m.xn_ready, 1)


def norm_buffers(m):
    m.stats, m.mv, m.xn = m.sb("stats", [P, 2, 6]), m.sb("mv", [P, 2, 2]), m.sb("xn", [P, 2, D])
    m.veps, m.rstd, m.pause = m.sb("veps", [P, 2]), m.sb("rstd", [P, 2]), m.sb("pause", [P, 1], U32)
    m.veps_ready, m.rstd_ready, m.xn_ready = m.sem("veps_ready"), m.sem("rstd_ready"), m.sem("xn_ready")


def attention_a(nc, g, dram):
    WQKV = D + 2 * GA * DA
    NQK = HA + GA
    UNITS = 3 * GA
    BLOCKS_OF = ((0, 0), (0, 1), (1, 1))
    VROW = 32
    AFTER = {0: ["Q1"], 4: ["K0"], 5: ["H1"], 6: ["K1"], 7: ["C"], 8: ["Sa0"], 9: ["O", "Sb0", "N"], 10: ["Sc0", "Sa1"],
             11: ["Sb1", "Sc1"], 14: ["U0"], 17: ["H0"], 23: ["X"], 24: ["M", "Q0", "U1"]}
    MAX_FROM = 12
    TAKES = {"X": (0,), "Q0": (0,), "Q1": (1,), "H1": (0, 1), "C": (0,), "Sa0": (1,), "O": (0,), "Sb0": (1,), "Sc0": (0,),
             "Sa1": (1,), "Sb1": (0,), "Sc1": (1,), "H0": (0, 1), "M": (1,)}
    LAG = {"X": -1, "Q0": -1, "Q1": 0, "K0": 0, "K1": 0, "Sa0": 0, "Sb0": 0, "Sc0": 0, "Sa1": 0, "Sb1": 0, "Sc1": 0, "M": 0, "U0": 1, "U1": 1, "H0": 1, "H1": 2, "C": 2, "O": 2,
           "N": -1}
    STEPS = B + 2
    order = [name for v in sorted(AFTER) for name in AFTER[v] if name in TAKES]

    def present(t, lag):
        return not isinstance(t, int) or 0 <= t - lag < B

    def uses_before(t, name, bank):
        def in_step(step, names):
            return sum(TAKES[n].count(bank) for n in names if present(step, LAG[n]))
        ahead = order[:order.index(name)]
        if isinstance(t, int):
            return sum(in_step(u, order) for u in range(-1, t)) + in_step(t, ahead)
        full = in_step(None, order)
        return (t - 2) * full + (in_step(-1, order) + in_step(0, order) + in_step(1, order) + in_step(None, ahead))

    def run_steps(eng, body):
        for t in range(-1, 2):
            body(t, t % 2)
        with eng.Fori(1, B // 2 - 1) as lap:
            for s in range(2):
                body(lap * 2 + s, s)
        for t in range(B - 2, B + 2):
            body(t, t % 2)

    with ExitStack() as ctx:
        m = Memory(nc, ctx, "a")
        norm_buffers(m)
        w_qkv, w_o, zeros = m.sb("w_qkv", [P, KD, WQKV]), m.sb("w_o", [P, KD, D]), m.sb("zeros", [P, D])
        pool_pause = m.sb("pool_pause", [P, 8])
        ident_b, future_b = m.sb("ident_b", [P, P], BF16), m.sb("future_b", [P, P], BF16)
        minus_group = m.sb("minus_group", [HA, GA, P], BF16)
        x_t, ctx_n, ctx_t = m.sb("x_t", [P, KD, 2, P]), m.sb("ctx_n", [P, 2, HA, DA]), m.sb("ctx_t", [P, KD, 2, P])
        by_cos, by_sin, qk = m.sb("by_cos", [P, NQK, DA]), m.sb("by_sin", [P, NQK, DA]), m.sb("qk", [P, NQK, DA])
        rest = m.sb("rest", [P, NQK, DA])
        high, mid, low = (m.sb(name, [P, 2, NQK, DA], BF16) for name in ("high", "mid", "low"))
        q_stack, k_stack = m.sb("q_stack", [P, 2, HA, 8, DA], BF16), m.sb("k_stack", [P, 2, GA, 8, DA], BF16)
        values = m.sb("values", [P, 2, 2, GA, VROW])
        q_t, k_t = m.sb("q_t", [P, 2, 2, HA // 2, P], BF16), m.sb("k_t", [P, 2, 2, GA // 2, P], BF16)
        max_t = m.sb("max_t", [HA, 2, 2, REP, P], BF16)
        row_max, probs = m.sb("row_max", [P, 2, HA], BF16), m.sb("probs", [P, 4, REP, P])
        weighted, recip = m.sb("weighted", [P, 2, 2, REP, P]), m.sb("recip", [P, 2, REP, 4, 1])
        ps_s, ps_m, ps_u, ps_w = (m.ps(name, [P, 2, 512]) for name in ("ps_s", "ps_m", "ps_u", "ps_w"))

        zeros_made, w_loaded, x_loaded, made, chain_sem, rope_chain = m.sem("zeros_made"), m.sem("w_loaded"), m.sem("x_loaded"), m.sem("made"), m.sem("chain"), m.sem("rope_chain")
        ready = {name: m.sem(f"{name}_ready") for name in TAKES}
        left = [m.sem("left_w0"), m.sem("left_w1")]
        parts_ready, q_stacked, k_stacked = m.sem("parts_ready"), m.sem("q_stacked"), m.sem("k_stacked")
        smax_ready, smax_read, s_ready, p_ready = m.sem("smax_ready"), m.sem("smax_read"), m.sem("s_ready"), m.sem("p_ready")
        p_masked, weighed, u_moved, recips, ctx_ready, ready_max = m.sem("p_masked"), m.sem("weighed"), m.sem("u_moved"), m.sem("recips"), m.sem("ctx_ready"), m.sem("ready_max")
        ident = g.const("ident")
        block = ctx.enter_context(nc.Block())

        def free(eng, t, name, n=0):
            bank = TAKES[name][n]
            wait(eng, left[bank], uses_before(t, name, bank) + TAKES[name][:n].count(bank))
            return bank

        def read(eng, t, name):
            for bank in set(TAKES[name]):
                eng.wait_ge(left[bank], uses_before(t, name, bank) + TAKES[name].count(bank))

        @block.sync
        def _(sp):
            sp.dma_start(w_qkv[:], dram["a_Wqkv"].rearrange("(k p) n -> p k n", p=P)).then_inc(w_loaded, 16)
            sp.dma_start(w_o[:], dram["a_Wo"].rearrange("(k p) n -> p k n", p=P)).then_inc(w_loaded, 16)
            sp.dma_start(g.x[:, 2:], dram["x"][1:].rearrange("b (h p) d -> p (b h) d", p=P)).then_inc(x_loaded, 16)
            sp.wait_ge(zeros_made, 1)
            load_weights(sp, g, zeros, dram)
            sp.wait_ge(w_loaded, 32)
            sp.wait_ge(g.cleared, 16 * CLEARS)

        @block.gpsimd
        def _(pool):
            def roots(b):
                for c in range(2):
                    pool.wait_ge(m.veps_ready, b * 2 + c + 1)
                    nc.gpsimd.tensor_tensor(m.rstd[:, c:c + 1], m.veps[:, c:c + 1], g.minus_half[:], ALU.pow).then_inc(m.rstd_ready, 1)

            def step(t, s):
                for v in range(UNITS):
                    if present(t, 1) and v % 3 != 1:
                        pool.wait_ge(p_ready, (t - 1) * UNITS + v + 1)
                        nc.gpsimd.tensor_tensor(pool_pause[:, v % 6:v % 6 + 1], g.minus_half[:], g.minus_half[:], ALU.add)
                        nc.gpsimd.affine_select(out=probs[:, v % 4], in_=probs[:, v % 4], compare_op=ALU.is_ge, fill=0.0, base=0,
                                                pattern=[[0, REP], [1, P]], channel_multiplier=-1).then_inc(p_masked, 1)
                    for name in AFTER.get(v, ()):
                        if name in ("K0", "K1") and present(t, 0):
                            c = int(name[1])
                            pool.wait_ge(parts_ready, t * 2 + c + 1)
                            nc.gpsimd.tensor_tensor(pool_pause[:, 6 + c:7 + c], g.minus_half[:], g.minus_half[:], ALU.add)
                            for n, part in enumerate((high, mid, low)):
                                width = len(range(n, 8, 3))
                                last = nc.gpsimd.tensor_copy(k_stack[:, c, :, n:8:3, :],
                                                             part[:, c, HA:].rearrange("p h (o d) -> p h o d", o=1).broadcast_to([P, GA, width, DA]))
                            last.then_inc(k_stacked, 1)
                        if name == "N" and present(t, -1):
                            roots(t + 1)

            run_steps(pool, step)

        @block.tensor
        def _(pe):
            pe.wait_ge(made, 5)
            pe.wait_ge(w_loaded, 32)

            def scores(b, s, v):
                group, (s_blk, t_blk) = v // 3, BLOCKS_OF[v % 3]
                rows, pair = slice(STACK * (group % 2), STACK * (group % 2) + STACK), group // 2
                wait(pe, p_ready, b * UNITS + v - 1)
                nc.tensor.matmul(ps_s[:, v % 2], k_t[rows, s, s_blk, pair], q_t[rows, s, t_blk, pair * REP:(pair + 1) * REP], start=True, stop=False)
                if v == 0:
                    pe.wait_ge(ready_max, b + 1)
                nc.tensor.matmul(ps_s[:, v % 2], minus_group[:, group], max_t[:, s, t_blk], start=False, stop=True).then_inc(s_ready, 1)

            def weigh(b, s, v):
                group, (s_blk, t_blk) = v // 3, BLOCKS_OF[v % 3]
                if v % 3 == 1:
                    pe.wait_ge(p_ready, b * UNITS + v + 1)
                else:
                    pe.wait_ge(p_masked, b * 2 * GA + group * 2 + (v % 3) // 2 + 1)
                if v in (0, UNITS // 2):
                    wait(pe, u_moved, b * 2 + v // (UNITS // 2))
                rows = slice(VROW * (group % 4), VROW * (group % 4) + VROW)
                nc.tensor.matmul(ps_u[rows, t_blk], values[:, s, s_blk, group], probs[:, v % 4].rearrange("p r t -> p (r t)"),
                                 start=(v % 3 != 2), stop=(v % 3 != 1)).then_inc(weighed, 1)

            def maxima(b, s, v):
                group, c = v // 3, min(v % 3, 1)
                rows, pair = slice(STACK * (group % 2), STACK * (group % 2) + STACK), group // 2
                wait(pe, smax_read, b * UNITS + v - 1)
                bank = ps_m[:, v % 2].rearrange("p (r s) -> p r s", s=(c + 1) * P)
                reps = REP // (c + 1)
                for r in range(reps):
                    nc.tensor.matmul(bank[:, r], q_t[rows, s, c, pair * REP + (v % 3 == 2) * reps + r], k_t[rows, s, 0:c + 1, pair],
                                     start=(r == 0), stop=False)
                nc.tensor.matmul(bank[:, :, c * P:(c + 1) * P], ident_b[:],
                                 future_b[:].rearrange("p (o s) -> p o s", o=1).broadcast_to([P, reps, P]),
                                 start=False, stop=True).then_inc(smax_ready, 1)

            def turn_weighted(t, s, name):
                pe.wait_ge(u_moved, (t - LAG[name]) * 2 + int(name[1]) + 1)
                for c in range(2):
                    bank = free(pe, t, name, c)
                    for r in range(REP):
                        last = nc.tensor.transpose(ps_w[:, bank, r * P:(r + 1) * P], weighted[:, int(name[1]), c, r], ident)
                    last.then_inc(ready[name], 1)

            def turn_stacks(t, s, name):
                part, c = "abc".index(name[1]), int(name[2])
                if part == 0:
                    pe.wait_ge(q_stacked, t * 2 + c + 1)
                if part == 2:
                    pe.wait_ge(k_stacked, t * 2 + c + 1)
                bank = free(pe, t, name)
                for n in range(8 if part < 2 else 4):
                    src = (q_stack[:, c, (part * 8 + n) * 2:(part * 8 + n) * 2 + 2] if part < 2
                           else k_stack[:, c, n * 2:n * 2 + 2])
                    last = nc.tensor.transpose(ps_w[:, bank].bitcast(BF16)[:, n * P:(n + 1) * P], src.rearrange("p h r d -> p (h r d)"), ident_b[:])
                last.then_inc(ready[name], 1)

            def other(t, s, name):
                if name == "X":
                    pe.wait_ge(m.xn_ready, (t + 1) * 2 + 2)
                    bank = free(pe, t, name)
                    for c in range(2):
                        for k in range(KD):
                            last = nc.tensor.transpose(ps_w[:, bank, (k * 2 + c) * P:(k * 2 + c + 1) * P], m.xn[:, c, k * P:(k + 1) * P], ident)
                    last.then_inc(ready[name], 1)
                elif name in ("Q0", "Q1"):
                    c = int(name[1])
                    if c == 0:
                        read(pe, t, "X")
                    bank = free(pe, t, name)
                    for k in range(KD):
                        last = nc.tensor.matmul(ps_w[:, bank, 0:WQKV], x_t[:, k, c], w_qkv[:, k, :], start=(k == 0), stop=(k == KD - 1))
                    last.then_inc(ready[name], 1)
                elif name[0] == "S":
                    turn_stacks(t, s, name)
                elif name in ("H0", "H1"):
                    turn_weighted(t, s, name)
                elif name == "C":
                    bank = free(pe, t, name)
                    pe.wait_ge(ctx_ready, (t - 2) * 4 + 4)
                    for c in range(2):
                        for k in range(KD):
                            last = nc.tensor.transpose(ps_w[:, bank, (k * 2 + c) * P:(k * 2 + c + 1) * P],
                                                       ctx_n[:, c].rearrange("p h d -> p (h d)")[:, k * P:(k + 1) * P], ident)
                    last.then_inc(ready[name], 1)
                elif name == "O":
                    read(pe, t, "C")
                    bank = free(pe, t, name)
                    for c in range(2):
                        for k in range(KD):
                            last = nc.tensor.matmul(ps_w[:, bank, c * D:(c + 1) * D], ctx_t[:, k, c], w_o[:, k, :], start=(k == 0), stop=(k == KD - 1))
                    last.then_inc(ready[name], 1)
                elif name == "M":
                    pe.wait_ge(smax_read, t * UNITS + UNITS)
                    bank = free(pe, t, name)
                    for c in range(2):
                        last = nc.tensor.transpose(ps_w[0:HA, bank].bitcast(BF16)[:, c * P:(c + 1) * P], row_max[:, c], ident_b[:])
                    last.then_inc(ready[name], 1)

            def step(t, s):
                next_max = 0
                for v in range(UNITS + 2):
                    if present(t, 1) and v < UNITS:
                        scores(t - 1, 1 - s, v)
                    if present(t, 1) and v == UNITS:
                        weigh(t - 1, 1 - s, v - 2)
                    if v == MAX_FROM and present(t, 0):
                        read(pe, t, "Sb1")
                        read(pe, t, "Sc1")
                    while present(t, 0) and v >= MAX_FROM and next_max < min(UNITS, 2 * (v - MAX_FROM + 1)):
                        maxima(t, s, next_max)
                        next_max += 1
                    if present(t, 1) and v >= 2 and v != UNITS:
                        weigh(t - 1, 1 - s, v - 2)
                    for name in AFTER.get(v, ()):
                        if name in TAKES and present(t, LAG[name]):
                            other(t, s, name)

            run_steps(pe, step)

        @block.scalar
        def _(act):
            def other(t, s, name):
                if name in ("X", "C"):
                    src = ps_w[:, TAKES[name][0]]
                    act.wait_ge(ready[name], t - LAG[name] + 1)
                    dst = x_t if name == "X" else ctx_t
                    nc.scalar.copy(dst[:].rearrange("p k c t -> p (k c t)"), src).then_inc(left[TAKES[name][0]], 1)
                elif name in ("K0", "K1"):
                    c = int(name[1])
                    act.wait_ge(parts_ready, t * 2 + c + 1)
                    for part, a, z in ((high, 0, 3), (mid, 3, 6), (low, 6, 8)):
                        last = nc.scalar.copy(q_stack[:, c, :, a:z, :], part[:, c, 0:HA].rearrange("p h (o d) -> p h o d", o=1).broadcast_to([P, HA, z - a, DA]))
                    last.then_inc(q_stacked, 1)
                elif name[0] == "S":
                    part, c, bank = "abc".index(name[1]), int(name[2]), TAKES[name][0]
                    act.wait_ge(ready[name], t + 1)
                    dst = q_t[:, s, c, part * 8:part * 8 + 8] if part < 2 else k_t[:, s, c]
                    n = 8 if part < 2 else 4
                    nc.scalar.copy(dst, ps_w[:, bank].bitcast(BF16)[:, 0:n * P].rearrange("p (n t) -> p n t", t=P)).then_inc(left[bank], 1)
                elif name in ("U0", "U1"):
                    half = int(name[1])
                    act.wait_ge(weighed, (t - 1) * UNITS + (half + 1) * UNITS // 2)
                    nc.scalar.copy(weighted[:, half].rearrange("p c r t -> p c (r t)"), ps_u[:]).then_inc(u_moved, 1)

            def step(t, s):
                for v in range(UNITS + 2):
                    if present(t, 1) and v < UNITS:
                        act.wait_ge(s_ready, (t - 1) * UNITS + v + 1)
                        wait(act, weighed, (t - 1) * UNITS + v - 3)
                        nc.scalar.activation(probs[:, v % 4].rearrange("p r t -> p (r t)"), ps_s[:, v % 2], ACT.Exp,
                                             scale=float(DA) ** -0.5).then_inc(p_ready, 1)
                    for name in AFTER.get(v, ()):
                        if present(t, LAG[name]):
                            other(t, s, name)

            run_steps(act, step)

        @block.vector
        def _(dve):
            nc.vector.memset(zeros[:], 0.0).then_inc(zeros_made, 1)
            nc.vector.tensor_copy(ident_b[:], ident).then_inc(made, 1)
            nc.vector.tensor_copy(future_b[:], g.const("future")).then_inc(made, 1)
            nc.vector.tensor_copy(minus_group[:], g.const("minus_group")[0:HA].rearrange("p (g o) -> p g o", o=1).broadcast_to([HA, GA, P])).then_inc(made, 1)
            nc.vector.memset(values[:, :, :, :, DA:DA + 1], 1.0).then_inc(made, 1)
            nc.vector.memset(values[:, :, :, :, DA + 1:], 0.0).then_inc(made, 1)
            norm, rope = Chain(dve, chain_sem, 4), Chain(dve, rope_chain, 10)

            def rotate(t, s, name):
                c, b = int(name[1]), t - LAG[name]
                if c == 0:
                    rope.at(b)
                    s = 1 - s
                rope.i = b
                dve.wait_ge(ready[name], b + 1)
                src = ps_w[:, TAKES[name][0], 0:NQK * DA].rearrange("p (h d) -> p h d", d=DA)
                cos = g.const("cos_a")[:, c * DA:(c + 1) * DA].rearrange("p (o d) -> p o d", o=1)
                sin = g.const("sin_a")[:, c * DA:(c + 1) * DA].rearrange("p (o d) -> p o d", o=1)
                half = DA // 2
                nc.vector.tensor_tensor(by_cos[:], src, cos.broadcast_to([P, NQK, DA]), ALU.mult)
                nc.vector.tensor_tensor(by_sin[:, :, 0:half], src[:, :, half:], sin[:, :, 0:half].broadcast_to([P, NQK, half]), ALU.mult)
                nc.vector.tensor_tensor(by_sin[:, :, half:], src[:, :, 0:half], sin[:, :, half:].broadcast_to([P, NQK, half]), ALU.mult)
                nc.vector.tensor_copy(values[:, s, c, :, 0:DA], ps_w[:, TAKES[name][0], NQK * DA:WQKV].rearrange("p (h d) -> p h d", d=DA)).then_inc(left[TAKES[name][0]], 1)
                dve.wait_ge(left[TAKES[name][0]], uses_before(t, name, TAKES[name][0]) + 1)
                rope.then(nc.vector.tensor_tensor(qk[:], by_cos[:], by_sin[:], ALU.add))
                rope.then(nc.vector.tensor_copy(high[:, c], qk[:]))
                rope.then(nc.vector.tensor_tensor(rest[:], qk[:], high[:, c], ALU.subtract))
                rope.then(nc.vector.tensor_copy(mid[:, c], rest[:]))
                rope.then(nc.vector.tensor_tensor(low[:, c], rest[:], mid[:, c], ALU.subtract))
                nc.vector.memset(m.pause[:], 0).then_inc(parts_ready, 1)

            def other(t, s, name):
                if name in ("Q0", "Q1"):
                    rotate(t, s, name)
                elif name == "N":
                    normalise(t + 1)
                elif name in ("H0", "H1"):
                    half = int(name[1])
                    for c in range(2):
                        bank = TAKES[name][c]
                        dve.wait_ge(ready[name], (t - LAG[name]) * 2 + c + 1)
                        src = ps_w[:, bank].rearrange("p (r g d) -> p r g d", r=REP, d=VROW)
                        nc.vector.reciprocal(recip[:, c], src[:, :, :, DA:DA + 1]).then_inc(recips, 1)
                        dve.wait_ge(recips, (t - LAG[name]) * 4 + half * 2 + c + 1)
                        dst = ctx_n[:, c, half * (HA // 2):(half + 1) * (HA // 2)].rearrange("p (g r) d -> p r g d", r=REP)
                        nc.vector.tensor_tensor(dst, src[:, :, :, 0:DA], recip[:, c].broadcast_to([P, REP, 4, DA]), ALU.mult).then_inc(left[bank], 1)
                        nc.vector.memset(m.pause[:], 0).then_inc(ctx_ready, 1)
                elif name == "O":
                    dve.wait_ge(ready[name], t - 2 + 1)
                    tiles = g.x[:, bass.ds((t - 2) * 2, 2), :]
                    nc.vector.tensor_tensor(tiles, tiles, ps_w[:, TAKES[name][0]].rearrange("p (c d) -> p c d", c=2), ALU.add).then_inc(left[TAKES[name][0]], 1)
                elif name == "M":
                    dve.wait_ge(ready[name], t + 1)
                    bank = TAKES[name][0]
                    for r in range(REP):
                        last = nc.vector.tensor_scalar(max_t[:, s, :, r], ps_w[0:HA, bank].bitcast(BF16)[:, 0:2 * P].rearrange("p (c t) -> p c t", c=2),
                                                       g.const("row_mod")[0:HA, r:r + 1], None, ALU.mult)
                    last.then_inc(left[bank], 1)
                    nc.vector.memset(m.pause[:], 0).then_inc(ready_max, 1)

            def normalise(b):
                if isinstance(b, int) and b == 1:
                    dve.wait_ge(x_loaded, 16)
                norm.at(b)
                wait(dve, ready["X"], b)
                for c in range(2):
                    normalise_tile(nc, dve, g, m, b * 2 + c, c, b * 2 + c, norm)

            def step(t, s):
                next_max = 0
                for v in range(UNITS + 2):
                    while present(t, 0) and v >= MAX_FROM and next_max < min(UNITS, 2 * (v - MAX_FROM + 1)):
                        group, n = next_max // 3, next_max % 3
                        c = min(n, 1)
                        reps = REP // (c + 1)
                        first = group * REP + (n == 2) * reps
                        dve.wait_ge(smax_ready, t * UNITS + next_max + 1)
                        nc.vector.tensor_reduce(row_max[:, c, first:first + reps], ps_m[:, next_max % 2].rearrange("p (r s) -> p r s", s=(c + 1) * P),
                                                AX.X, ALU.max).then_inc(smax_read, 1)
                        next_max += 1
                    for name in AFTER.get(v, ()):
                        if present(t, LAG[name]):
                            other(t, s, name)

            run_steps(dve, step)
            dve.wait_ge(left[TAKES["O"][0]], uses_before(STEPS - 1, "O", TAKES["O"][0]) + 1)



RMS_EPS_B = float(np.finfo(np.float32).eps)
PAIRS = HB // 2
EARLY = 3


def attention_b_weights(nc, g, w, dram):
    with ExitStack() as ctx:
        m = Memory(nc, ctx, "b_weights")
        wqn_t, wk_t = m.sb("wqn_t", [NOPE, HB, QR]), m.sb("wk_t", [NOPE, HB, KVR])
        wv_t, wo, q_norm = m.sb("wv_t", [VD, HB, KVR]), m.sb("wo", [VD, HB, D]), m.sb("q_norm", [QR, 1])
        ps = m.ps("ps", [P, 6, 512])
        q_loaded, v_loaded, loaded = m.sem("q_loaded"), [m.sem(f"v_loaded{n}") for n in range(2)], m.sem("loaded")
        kept, multiplied, moved = m.sem("kept"), m.sem("multiplied"), m.sem("moved")
        combine = Combine(nc, g, m, 0, 2)
        block = ctx.enter_context(nc.Block())

        @block.sync
        def _(sp):
            sp.dma_start(wqn_t[:], dram["b_wqn_t"]).then_inc(q_loaded, 16)
            sp.dma_start(wk_t[:], dram["b_wk_t"]).then_inc(q_loaded, 16)
            for n in range(2):
                heads = slice(n * HB // 2, (n + 1) * HB // 2)
                sp.dma_start(wv_t[:, heads], dram["b_wv_t"][:, heads]).then_inc(v_loaded[n], 16)
                sp.dma_start(wo[:, heads], dram["b_wo"].rearrange("(h v) n -> v h n", v=VD)[:, heads]).then_inc(v_loaded[n], 16)
            sp.dma_start(q_norm[:], dram["b_q_a_norm_w"].rearrange("(p a) -> p a", a=1)).then_inc(loaded, 16)
            sp.dma_start(w.wq[:, :, 0:ROPE], dram["b_wqp"]).then_inc(loaded, 16)
            sp.dma_start(w.w_a[:], dram["b_w_a"].rearrange("(k p) n -> p k n", p=P)).then_inc(loaded, 16)
            sp.dma_start(w.kv_norm[:], dram["b_kv_a_norm_w"].rearrange("(a d) -> a d", a=1).broadcast_to([P, KVR])).then_inc(loaded, 16)
            sp.wait_ge(loaded, 64)

        @block.gpsimd
        def _(pool):
            for i in range(2 * EARLY):
                combine.gather(pool, i, g.slot_out[:, i])

        @block.tensor
        def _(pe):
            pe.wait_ge(q_loaded, 32)
            for h in range(HB):
                nc.tensor.matmul(ps[0:QR, h // 8, (h % 8) * KVR:(h % 8 + 1) * KVR], wqn_t[:, h], wk_t[:, h], start=True, stop=True)
            for h in range(HB):
                if h % (HB // 2) == 0:
                    pe.wait_ge(v_loaded[h // (HB // 2)], 32)
                half = slice(KVR * (h % 2), KVR * (h % 2) + KVR)
                last = nc.tensor.matmul(ps[half, 2 + h // 4, (h // 2 % 2) * D:(h // 2 % 2 + 1) * D], wv_t[:, h], wo[:, h], start=True, stop=True)
            last.then_inc(multiplied, 1)

        @block.scalar
        def _(act):
            nc.scalar.copy(w.ident_b[:], g.const("ident"))
            nc.scalar.activation(w.minus_head[:], g.const("ident")[0:HB, 0:HB].rearrange("p (h o) -> p h o", o=1).broadcast_to([HB, HB, P]),
                                 ACT.Copy, scale=-1.0)
            act.wait_ge(multiplied, 1)
            nc.scalar.copy(w.wvo[:].rearrange("p h n -> p (h n)"), ps[:, 2:6].rearrange("p b n -> p (b n)")).then_inc(moved, 1)
            act.wait_ge(moved, 1)

        @block.vector
        def _(dve):
            nc.vector.memset(w.keys[:, :, :, DK:], 1.0).then_inc(kept, 1)
            for i in range(2 * EARLY):
                combine.add(dve, i, g.weight[:, i])
            dve.wait_ge(loaded, 64)
            nc.vector.tensor_scalar(w.wq[:, :, 0:ROPE], w.wq[:, :, 0:ROPE], q_norm[:, 0:1], None, ALU.mult).then_inc(kept, 1)
            dve.wait_ge(multiplied, 1)
            nc.vector.tensor_scalar(w.wq[:, :, ROPE:], ps[0:QR, 0:2].rearrange("p b n -> p (b n)").rearrange("p (h c) -> p h c", c=KVR),
                                    q_norm[:, 0:1], None, ALU.mult).then_inc(kept, 1)
            dve.wait_ge(kept, 3)
            dve.wait_ge(combine.added, 2 * EARLY * TOPK)


def attention_b(nc, g, dram):
    NA = QR + KVR + ROPE
    QUAD = 4
    UNITS = 2 * HB // QUAD
    PREPARE = {1: "T", 2: "M0 M1", 3: "M2", 4: "R0 M3", 5: "R1 M4", 6: "R2 M5", 7: "R3 M6 S0 S1", 8: "R4 M7 S2 S3",
               9: "R5 S4 S5", 10: "R6 S6 S7", 11: "R7 S8 S9", 12: "S10 S11", 13: "S12 S13", 14: "X S14 S15", 15: "L0 L1 Z"}
    PREPARE = {v: [(n[0], int(n[1:] or 0)) for n in PREPARE.get(v, "").split()] for v in range(HB)}
    COUNT = {"X": 1, "L": 2, "T": 1, "M": UNITS, "R": UNITS, "S": HB, "Z": 1, "C": PAIRS}
    WORK_BANKS = 3
    BACK = {"X": -1, "L": -1}

    def pair_turned(v):
        return ((v - 3) // 2 % PAIRS, 1 if v >= 3 else 2) if v % 2 else None

    order = []
    for v in range(HB):
        if v % 2:
            order.append(("C",) + pair_turned(v))
        order += [name + (BACK.get(name[0], 0),) for name in PREPARE[v]]
    bank_of = {name[:2]: n % WORK_BANKS for n, name in enumerate(order)}

    def present(t, lag):
        return not isinstance(t, int) or 0 <= t - lag < B

    def taken_before(t, name):
        bank = bank_of[name]
        same = [n for n in order if bank_of[n[:2]] == bank]
        ahead = same[:[n[:2] for n in same].index(name)]
        if isinstance(t, int):
            return sum(present(u, n[2]) for u in range(-1, t) for n in same) + sum(present(t, n[2]) for n in ahead)
        return (t - 2) * len(same) + sum(present(u, n[2]) for u in range(-1, 2) for n in same) + len(ahead)

    with ExitStack() as ctx:
        m = Memory(nc, ctx, "b")
        norm_buffers(m)
        m.w_a, m.wq, m.wvo = m.sb("w_a", [P, KD, NA]), m.sb("wq", [QR, HB, DK]), m.sb("wvo", [P, PAIRS, D])
        m.kv_norm, m.ident_b, m.minus_head = m.sb("kv_norm", [P, KVR]), m.sb("ident_b", [P, P], BF16), m.sb("minus_head", [HB, HB, P], BF16)
        m.keys = m.sb("keys", [P, 2, 2, DK + 1])
        attention_b_weights(nc, g, m, dram)
        x_t, junk, sums = m.sb("x_t", [P, KD, 2, P]), m.sb("junk", [P, QR]), m.sb("sums", [P, 2, 2])
        means, inverse, q_low = m.sb("means", [P, 2, 2]), m.sb("inverse", [P, 2, 2]), m.sb("q_low", [P, 2, QR])
        by_cos, by_sin, k_sin = m.sb("by_cos", [P, QUAD, ROPE]), m.sb("by_sin", [P, QUAD, ROPE]), m.sb("k_sin", [P, 2, ROPE])
        q_low_t, k_tb, queries = m.sb("q_low_t", [QR, 2, P]), m.sb("k_tb", [P, 2, P], BF16), m.sb("queries", [P, 3, QUAD, DK])
        q_tb, row_max = m.sb("q_tb", [P, HB, 2, P], BF16), m.sb("row_max", [P, 2, HB], BF16)
        k_t, max_t = m.sb("k_t", [P, 2, 2, P]), m.sb("max_t", [HB, 2, 2 * P], BF16)
        q_t = m.sb("q_t", [P, HB // 2 + 2 * (HB // 2), 2, P])
        probs, recip = m.sb("probs", [P, 2, 2, 2 * P]), m.sb("recip", [P, 2, 2, 2, 1])
        ctx_n, ctx_t = m.sb("ctx_n", [P, 2, 2, KVR]), m.sb("ctx_t", [P, 2, P])
        combine = Combine(nc, g, m, 2 * EARLY, 1)
        norm_pause = m.sb("norm_pause", [P, 1], U32)
        slots_now, weights_now = m.sb("slots_now", [P, 2, TOPK], U32), m.sb("weights_now", [P, 2, TOPK])
        ps_s, ps_o, ps_w, ps_y = m.ps("ps_s", [P, 2, 512]), m.ps("ps_o", [P, 2, 512]), m.ps("ps_w", [P, WORK_BANKS, 512]), m.ps("ps_y", [P, 512])

        chain_sem, low_chain, rope_sem = m.sem("chain"), m.sem("low_chain"), m.sem("rope")
        ready = {kind: m.sem(f"{kind}_ready") for kind in COUNT}
        left = [m.sem(f"left_w{n}") for n in range(WORK_BANKS)]
        sums_ready, means_ready, inverse_ready = m.sem("sums_ready"), m.sem("means_ready"), m.sem("inverse_ready")
        latents_ready, q_rotated, q_narrowed, max_ready = m.sem("latents_ready"), m.sem("q_rotated"), m.sem("q_narrowed"), m.sem("max_ready")
        s_ready, p_ready, weighed, recips = m.sem("s_ready"), m.sem("p_ready"), m.sem("weighed"), m.sem("recips")
        ctx_ready, y_ready, x_added, now_ready = m.sem("ctx_ready"), m.sem("y_ready"), m.sem("x_added"), m.sem("now_ready")
        ident = g.const("ident")
        block = ctx.enter_context(nc.Block())

        def combines(t):
            return present(t, -2) and not (isinstance(t, int) and t + 2 < EARLY)

        def run_steps(eng, body):
            for t in range(-1, 2):
                body(t, t % 2)
            with eng.Fori(1, B // 2 - 1) as lap:
                for s in range(2):
                    body(lap * 2 + s, s)
            for t in range(B - 2, B + 2):
                body(t, t % 2)

        def first_head(n):
            return (n // 2 * QUAD + HB // 2) % HB

        def at(s, h):
            return h if h < HB // 2 else h + s * HB // 2

        def read(eng, t, kind, n):
            eng.wait_ge(left[bank_of[kind, n]], taken_before(t, (kind, n)) + 1)

        def made(eng, b, kind, n):
            eng.wait_ge(ready[kind], b * COUNT[kind] + n + 1)
            return ps_w[:, bank_of[kind, n]]

        @block.gpsimd
        def _(pool):
            def layer_roots(b):
                for c in range(2):
                    pool.wait_ge(m.veps_ready, b * 2 + c + 1)
                    nc.gpsimd.tensor_tensor(m.rstd[:, c:c + 1], m.veps[:, c:c + 1], g.minus_half[:], ALU.pow).then_inc(m.rstd_ready, 1)

            def step(t, s):
                if present(t, 0):
                    for c in range(2):
                        pool.wait_ge(means_ready, t * 2 + c + 1)
                        nc.gpsimd.tensor_tensor(inverse[:, c], means[:, c], g.minus_half[:].broadcast_to([P, 2]), ALU.pow).then_inc(inverse_ready, 1)
                if present(t, -1):
                    layer_roots(t + 1)
                if combines(t):
                    pool.wait_ge(now_ready, (t + 2 - EARLY + 1) * 2)
                    for i in range(2):
                        combine.gather(pool, (t + 2) * 2 + i, slots_now[:, i], i)

            run_steps(pool, step)

        @block.tensor
        def _(pe):
            def take(t, kind, n):
                wait(pe, left[bank_of[kind, n]], taken_before(t, (kind, n)))
                return bank_of[kind, n]

            def prepare(t, s, kind, n):
                if kind == "X":
                    pe.wait_ge(m.xn_ready, (t + 1) * 2 + 2)
                    bank = take(t, kind, n)
                    for c in range(2):
                        for k in range(KD):
                            last = nc.tensor.transpose(ps_w[:, bank, (k * 2 + c) * P:(k * 2 + c + 1) * P], m.xn[:, c, k * P:(k + 1) * P], ident)
                elif kind == "L":
                    read(pe, t, "X", 0)
                    bank = take(t, kind, n)
                    for k in range(KD):
                        last = nc.tensor.matmul(ps_w[:, bank, 0:NA], x_t[:, k, n], m.w_a[:, k, :], start=(k == 0), stop=(k == KD - 1))
                elif kind == "T":
                    pe.wait_ge(latents_ready, t + 1)
                    bank = take(t, kind, n)
                    for c in range(2):
                        nc.tensor.transpose(ps_w[0:QR, bank, c * P:(c + 1) * P], q_low[:, c], ident)
                        last = nc.tensor.transpose(ps_w[:, bank, (2 + c) * P:(3 + c) * P], m.keys[:, s, c, 0:DK], ident)
                elif kind == "M":
                    read(pe, t, "T", 0)
                    bank = take(t, kind, n)
                    h = first_head(n)
                    last = nc.tensor.matmul(ps_w[:, bank], q_low_t[:, n % 2], m.wq[:, h:h + QUAD, :].rearrange("p h d -> p (h d)"), start=True, stop=True)
                elif kind == "R":
                    pe.wait_ge(q_rotated, t * UNITS + n + 1)
                    bank = take(t, kind, n)
                    for i in range(QUAD):
                        last = nc.tensor.transpose(ps_w[:, bank, i * P:(i + 1) * P], queries[:, n % 3, i], ident)
                elif kind == "S":
                    pe.wait_ge(q_narrowed, t * UNITS + n // QUAD * 2 + 2)
                    bank = take(t, kind, n)
                    for c in range(2):
                        last = nc.tensor.matmul(ps_w[:, bank, c * T:(c + 1) * T], q_tb[:, (n + HB // 2) % HB, c], k_tb[:].rearrange("p c s -> p (c s)"), start=True, stop=True)
                else:
                    for h in range(HB - WORK_BANKS, HB):
                        read(pe, t, "S", h)
                    bank = take(t, kind, n)
                    for c in range(2):
                        last = nc.tensor.transpose(ps_w[0:HB, bank].bitcast(BF16)[:, c * P:(c + 1) * P], row_max[:, c], m.ident_b[:])
                last.then_inc(ready[kind], 1)

            def scores(b, s, h):
                wait(pe, p_ready, b * HB + h - 1)
                for s_blk in range(2):
                    nc.tensor.matmul(ps_s[:, h % 2, s_blk * T:(s_blk + 1) * T], k_t[:, s, s_blk], q_t[:, at(s, h)].rearrange("p c t -> p (c t)"),
                                     start=(s_blk == 0), stop=False)
                if h == 0:
                    pe.wait_ge(max_ready, b + 1)
                nc.tensor.matmul(ps_s[:, h % 2].rearrange("p (a t) -> p a t", a=2), m.minus_head[:, h],
                                 max_t[:, s].rearrange("p (a t) -> p a t", a=1).broadcast_to([HB, 2, T]), start=False, stop=True).then_inc(s_ready, 1)

            def weigh(b, s, h):
                pair, n = h // 2, h % 2
                pe.wait_ge(p_ready, b * HB + h + 1)
                if n == 0:
                    wait(pe, ctx_ready, b * PAIRS + pair - 1)
                for c in range(2):
                    at = (c * 2 + n) * (KVR + 1)
                    for s_blk in range(2):
                        last = nc.tensor.matmul(ps_o[:, pair % 2, at:at + KVR + 1], probs[:, n, s_blk, c * P:(c + 1) * P],
                                                m.keys[:, s, s_blk, ROPE:], start=(s_blk == 0), stop=(s_blk == 1))
                last.then_inc(weighed, 1)

            def turn_ctx(t, b, pair):
                pe.wait_ge(ctx_ready, b * PAIRS + pair + 1)
                bank = take(t, "C", pair)
                for c in range(2):
                    last = nc.tensor.transpose(ps_w[:, bank, c * P:(c + 1) * P], ctx_n[:, c].rearrange("p n d -> p (n d)"), ident)
                last.then_inc(ready["C"], 1)

            def project(t, b, pair):
                read(pe, t, "C", pair)
                if pair == 0:
                    wait(pe, x_added, b)
                for c in range(2):
                    last = nc.tensor.matmul(ps_y[:, c * D:(c + 1) * D], ctx_t[:, c], m.wvo[:, pair, :],
                                            start=(pair == 0 and c == 0), stop=(pair == PAIRS - 1 and c == 1))
                if pair == PAIRS - 1:
                    last.then_inc(y_ready, 1)

            def step(t, s):
                for v in range(HB):
                    if present(t, 1):
                        scores(t - 1, 1 - s, v)
                    if v % 2:
                        pair, back = pair_turned(v)
                        if present(t, back):
                            turn_ctx(t, t - back, pair)
                    if v and present(t, 1):
                        weigh(t - 1, 1 - s, v - 1)
                    if v == 0 and present(t, 2):
                        weigh(t - 2, s, HB - 1)
                    for kind, n in PREPARE[v]:
                        if kind not in "SZ" and present(t, BACK.get(kind, 0)):
                            prepare(t, s, kind, n)
                    if v % 2 and present(t, back):
                        project(t, t - back, pair)
                    for kind, n in PREPARE[v]:
                        if kind in "SZ" and present(t, 0):
                            prepare(t, s, kind, n)

            run_steps(pe, step)

        @block.scalar
        def _(act):
            def prepare(t, s, kind, n):
                if kind in "SZ":
                    return
                b = t - BACK.get(kind, 0)
                src = made(act, b, kind, n)
                if kind == "L":
                    wait(act, sums_ready, b * 4 + n * 2)
                    nc.scalar.activation(junk[:], src[:, 0:QR], ACT.Square, accum_out=sums[:, n, 0:1]).then_inc(sums_ready, 1)
                    act.wait_ge(sums_ready, b * 4 + n * 2 + 1)
                    nc.scalar.activation(junk[:, 0:KVR], src[:, QR:QR + KVR], ACT.Square, accum_out=sums[:, n, 1:2]).then_inc(sums_ready, 1)
                    return
                if kind == "X":
                    last = nc.scalar.copy(x_t[:].rearrange("p k c t -> p (k c t)"), src)
                elif kind == "T":
                    nc.scalar.copy(q_low_t[:].rearrange("p c t -> p (c t)"), src[0:QR, 0:2 * P])
                    nc.scalar.copy(k_t[:, s].rearrange("p c t -> p (c t)"), src[:, 2 * P:4 * P])
                    last = nc.scalar.copy(k_tb[:].rearrange("p c t -> p (c t)"), src[:, 2 * P:4 * P])
                elif kind == "M":
                    last = nc.scalar.copy(queries[:, n % 3].rearrange("p h d -> p (h d)"), src)
                else:
                    h = first_head(n)
                    last = nc.scalar.copy(q_t[:, at(s, h):at(s, h) + QUAD, n % 2], src.rearrange("p (h t) -> p h t", t=P))
                last.then_inc(left[bank_of[kind, n]], 1)

            def step(t, s):
                for v in range(HB):
                    if present(t, 1):
                        act.wait_ge(s_ready, (t - 1) * HB + v + 1)
                        nc.scalar.activation(probs[:, v % 2].rearrange("p a t -> p (a t)"), ps_s[:, v % 2], ACT.Exp, scale=float(DK) ** -0.5).then_inc(p_ready, 1)
                    if v % 2:
                        pair, back = pair_turned(v)
                        if present(t, back):
                            src = made(act, t - back, "C", pair)
                            nc.scalar.copy(ctx_t[:].rearrange("p c t -> p (c t)"), src[:, 0:2 * P]).then_inc(left[bank_of["C", pair]], 1)
                    for kind, n in PREPARE[v]:
                        if present(t, BACK.get(kind, 0)):
                            prepare(t, s, kind, n)

            run_steps(act, step)

        @block.vector
        def _(dve):
            norm, low = Chain(dve, chain_sem, 4), Chain(dve, low_chain, 2)
            cos, sin = (g.const(name).rearrange("p (c o d) -> p c o d", c=2, o=1) for name in ("cos_b", "sin_b"))
            half = ROPE // 2

            def normalise(b):
                norm.at(b)
                wait(dve, ready["X"], b)
                nc.vector.memset(norm_pause[:], 0)
                for c in range(2):
                    normalise_tile(nc, dve, g, m, b * 2 + c, c, b * 2 + c, norm)

            def latents(t, s):
                low.at(t)
                for c in range(2):
                    dve.wait_ge(sums_ready, t * 4 + c * 2 + 2)
                    nc.vector.tensor_scalar(means[:, c, 0:1], sums[:, c, 0:1], 1.0 / QR, RMS_EPS_B, ALU.mult, ALU.add)
                    nc.vector.tensor_scalar(means[:, c, 1:2], sums[:, c, 1:2], 1.0 / KVR, RMS_EPS_B, ALU.mult, ALU.add).then_inc(means_ready, 1)
                for c in range(2):
                    src = ps_w[:, bank_of["L", c]]
                    rotated = src[:, QR + KVR:NA]
                    nc.vector.tensor_tensor(m.keys[:, s, c, 0:ROPE], rotated, cos[:, c, 0], ALU.mult)
                    nc.vector.tensor_tensor(k_sin[:, c, 0:half], rotated[:, half:], sin[:, c, 0, 0:half], ALU.mult)
                    low.then(nc.vector.tensor_tensor(k_sin[:, c, half:], rotated[:, 0:half], sin[:, c, 0, half:], ALU.mult))
                    nc.vector.tensor_tensor(m.keys[:, s, c, 0:ROPE], m.keys[:, s, c, 0:ROPE], k_sin[:, c], ALU.add)
                    dve.wait_ge(inverse_ready, t * 2 + c + 1)
                    nc.vector.tensor_scalar(q_low[:, c], src[:, 0:QR], inverse[:, c, 0:1], None, ALU.mult)
                    nc.vector.scalar_tensor_tensor(out=m.keys[:, s, c, ROPE:DK], in0=src[:, QR:QR + KVR], scalar=inverse[:, c, 1:2],
                                                   in1=m.kv_norm[:], op0=ALU.mult, op1=ALU.mult).then_inc(left[bank_of["L", c]], 1)
                nc.vector.memset(m.pause[:], 0).then_inc(latents_ready, 1)

            def rotate(t, n):
                c = n % 2
                wait(dve, q_rotated, t * UNITS + n)
                read(dve, t, "M", n)
                src = queries[:, n % 3]
                nc.vector.tensor_tensor(by_cos[:], src[:, :, 0:ROPE], cos[:, c].broadcast_to([P, QUAD, ROPE]), ALU.mult)
                nc.vector.tensor_tensor(by_sin[:, :, 0:half], src[:, :, half:ROPE], sin[:, c, :, 0:half].broadcast_to([P, QUAD, half]), ALU.mult)
                nc.vector.tensor_tensor(by_sin[:, :, half:], src[:, :, 0:half], sin[:, c, :, half:].broadcast_to([P, QUAD, half]), ALU.mult).then_inc(rope_sem, 1)
                dve.wait_ge(rope_sem, t * UNITS + n + 1)
                nc.vector.tensor_tensor(src[:, :, 0:ROPE], by_cos[:], by_sin[:], ALU.add).then_inc(q_rotated, 1)

            def narrow(t, s, n):
                read(dve, t, "R", n)
                h = first_head(n)
                nc.vector.tensor_copy(q_tb[:, h:h + QUAD, n % 2], q_t[:, at(s, h):at(s, h) + QUAD, n % 2]).then_inc(q_narrowed, 1)

            def divide(b, pair):
                dve.wait_ge(weighed, b * HB + 2 * pair + 2)
                out = ps_o[:, pair % 2, 0:4 * (KVR + 1)].rearrange("p (c n d) -> p c n d", c=2, n=2)
                nc.vector.reciprocal(recip[:, pair % 2], out[:, :, :, KVR:]).then_inc(recips, 1)
                dve.wait_ge(recips, b * PAIRS + pair + 1)
                wait(dve, ready["C"], b * PAIRS + pair)
                nc.vector.tensor_tensor(ctx_n[:], out[:, :, :, 0:KVR], recip[:, pair % 2].broadcast_to([P, 2, 2, KVR]),
                                        ALU.mult).then_inc(ctx_ready, 1)

            def maxima(t, s, kind, n):
                src = made(dve, t, kind, n)
                if kind == "S":
                    h = (n + HB // 2) % HB
                    nc.vector.tensor_reduce(row_max[:, :, h:h + 1], src.rearrange("p (c s) -> p c s", c=2), AX.X, ALU.max).then_inc(left[bank_of[kind, n]], 1)
                else:
                    nc.vector.tensor_copy(max_t[:, s], src[0:HB].bitcast(BF16)[:, 0:2 * P]).then_inc(left[bank_of[kind, n]], 1)
                    read(dve, t, kind, n)
                    nc.vector.memset(m.pause[:], 0).then_inc(max_ready, 1)

            def step(t, s):
                for v in range(HB):
                    if v == 2 and present(t, 2):
                        dve.wait_ge(y_ready, t - 2 + 1)
                        tiles = g.x[:, bass.ds((t - 2) * 2, 2), :]
                        nc.vector.tensor_tensor(tiles, tiles, ps_y[:].rearrange("p (c d) -> p c d", c=2), ALU.add).then_inc(x_added, 1)
                    if v == 1 and present(t, 0):
                        latents(t, s)
                    for kind, n in PREPARE[v - 1] if v else []:
                        if kind == "M" and present(t, 0):
                            rotate(t, n)
                        if kind == "R" and present(t, 0):
                            narrow(t, s, n)
                    if v % 2 == 0:
                        if v and present(t, 1):
                            divide(t - 1, v // 2 - 1)
                        if v == 0 and present(t, 2):
                            divide(t - 2, PAIRS - 1)
                    if v == 3 and combines(t):
                        tiles = bass.ds((t + 2) * 2, 2)
                        nc.vector.tensor_copy(slots_now[:], g.slot_out[:, tiles]).then_inc(now_ready, 1)
                        nc.vector.tensor_copy(weights_now[:], g.weight[:, tiles]).then_inc(now_ready, 1)
                    if v == 5 and present(t, -1):
                        normalise(t + 1)
                    if v in (8, 12) and combines(t):
                        combine.add(dve, (t + 2) * 2 + v // 12, weights_now[:, v // 12])
                    for kind, n in PREPARE[v]:
                        if kind in "SZ" and present(t, 0):
                            maxima(t, s, kind, n)

            run_steps(dve, step)
            dve.wait_ge(x_added, B)



class Route:

    def __init__(self, nc, g, m, ps):
        self.nc, self.g, self.ps = nc, g, ps
        self.off, self.total = m.sb("off", [P, TILES, TOPK]), m.sb("total", [P, TILES])
        self.count, self.used = m.sb("count", [P, E]), [m.sb(f"used{i}", [P, E]) for i in range(2)]
        self.ends, self.unused = [m.sb(f"ends{i}", [P, E]) for i in range(2)], m.sb("unused", [P, E])
        self.passed, self.skipped, self.owner = m.sb("passed", [P, E]), m.sb("skipped", [P, E]), m.sb("owner", [P, 2])
        self.shift = m.sb("shift", [P, E])
        self.chain, self.totalled, self.counted = m.sem("chain"), m.sem("totalled"), m.sem("counted")
        self.owned, self.turned, self.diffs, self.exps = m.sem("owned"), m.sem("owners_turned"), m.sem("diffs"), m.sem("exps")

    def tensor(self, pe):
        nc, g, ps, owner = self.nc, self.g, self.ps, self.owner
        pe.wait_ge(self.totalled, 1)
        nc.tensor.matmul(ps[:, 0:E], g.ones[:], g.totals[:], start=True, stop=True).then_inc(self.counted, 1)
        pe.wait_ge(self.owned, 1)
        for n in range(2):
            last = nc.tensor.matmul(ps[0:1, P * n:P * n + P], owner[:, n:n + 1], g.const("ident"), start=True, stop=True)
        last.then_inc(self.turned, 1)

    def scalar(self, act):
        act.wait_ge(self.diffs, 1)
        self.nc.scalar.activation(self.off[:], self.off[:], ACT.Exp).then_inc(self.exps, 1)

    def vector(self, dve):
        g, ps, off, total, count, used, ends = self.g, self.ps, self.off, self.total, self.count, self.used, self.ends
        unused, passed, skipped, owner, shift = self.unused, self.passed, self.skipped, self.owner, self.shift
        link = Chain(dve, self.chain, 0).then
        v = self.nc.vector
        v.tensor_tensor(off[:], g.top[:], g.top[:, :, 0:1].broadcast_to([P, TILES, TOPK]), ALU.subtract).then_inc(self.diffs, 1)
        dve.wait_ge(self.counted, 1)
        link(v.tensor_copy(count[:], ps[:, 0:E]))
        link(v.tensor_scalar(used[0][:], count[:], 0.0, None, ALU.is_gt))
        for n, at in enumerate(range(P, CAP, P)):
            link(v.scalar_tensor_tensor(out=used[(n + 1) % 2][:], in0=count[:], scalar=float(at), in1=used[n % 2][:],
                                        op0=ALU.is_gt, op1=ALU.add))
        src = blocks = used[(CAP // P - 1) % 2]
        link(v.tensor_scalar(unused[:], blocks[:], -1.0, float(CAP // P), ALU.mult, ALU.add))
        step, n = 1, 0
        while step < E:
            dst = ends[n % 2]
            v.tensor_copy(dst[:, 0:step], src[:, 0:step])
            link(v.tensor_tensor(dst[:, step:], src[:, step:], src[:, 0:E - step], ALU.add))
            src, step, n = dst, 2 * step, n + 1
        link(v.tensor_scalar(passed[:], src[:], g.const("blocks"), None, ALU.is_le))
        v.tensor_reduce(owner[:, 0:1], passed[:], AX.X, ALU.add)
        link(v.tensor_tensor(skipped[:], passed[:], unused[:], ALU.mult))
        link(v.tensor_reduce(owner[:, 1:2], skipped[:], AX.X, ALU.add))
        link(v.tensor_tensor(owner[:, 1:2], owner[:, 1:2], g.const("blocks"), ALU.add))
        v.tensor_scalar(owner[:, 0:1], owner[:, 0:1], float(E - 1), None, ALU.min)
        v.tensor_scalar(owner[:, 1:2], owner[:, 1:2], float(E * CAP // P), None, ALU.min).then_inc(self.owned, 1)
        dve.wait_ge(self.exps, 1)
        link(v.tensor_reduce(total[:], off[:], AX.X, ALU.add))
        link(v.reciprocal(total[:], total[:]))
        link(v.tensor_tensor(g.weight[:], off[:], total[:].rearrange("p (a o) -> p a o", o=1).broadcast_to([P, TILES, TOPK]), ALU.mult))
        dve.wait_ge(self.turned, 1)
        v.tensor_copy(g.owner[:, TABLE_PAD:], ps[0:1, 0:P])
        link(v.tensor_copy(g.place[:, TABLE_PAD:], ps[0:1, P:2 * P]))
        link(v.tensor_tensor(shift[:], src[:], blocks[:], ALU.subtract))
        link(v.scalar_tensor_tensor(out=g.shift[:], in0=shift[:], scalar=float(P), in1=g.const("first_slots"), op0=ALU.mult, op1=ALU.subtract))


def ffn_router(nc, g, tag):
    R = 4
    with ExitStack() as ctx:
        m = Memory(nc, ctx, tag + "_router")
        stats, mv = m.sb("stats", [P, R, 6]), m.sb("mv", [P, R, 2])
        rstd, ssq, rrms = m.sb("rstd", [P, R]), m.sb("ssq", [P, R]), m.sb("rrms", [P, R])
        veps, meps, pause = m.sb("veps", [P, R]), m.sb("meps", [P, R]), m.sb("pause", [P, 1], U32)
        h, junk, xin = m.sb("h", [P, R, D]), m.sb("junk", [P, D]), m.sb("xin", [P, R, D])
        xin_t, act_t = m.sb("xin_t", [P, R, KD, P]), m.sb("act_t", [P, R, P])
        silu, act = m.sb("silu", [P, R, INNER]), m.sb("act", [P, R, INNER])
        top8, idx8 = m.sb("top8", [P, R, 8]), m.sb("idx8", [P, R, 8], U32)
        hot, chose, before = m.sb("hot", [P, R, TOPK, E]), m.sb("chose", [P, R, E]), m.sb("before", [P, R, E])
        picked, pos, over = m.sb("picked", [P, R, TOPK, E]), m.sb("pos", [P, R, TOPK]), m.sb("over", [P, R, TOPK])
        slot_in, pool_pause = m.sb("slot_in", [P, R, TOPK], U32), m.sb("pool_pause", [P, R])
        ps_t, ps_g, ps_o, ps_p = (m.ps(name, [P, 2, 512]) for name in ("ps_t", "ps_g", "ps_o", "ps_p"))
        names = ("norm_chain route_chain count_chain slot_chain veps_ready rstd_ready meps_ready rrms_ready h_ready ssq_ready xin_ready "
                 "turned xin_t_ready gates_ready chosen_ready first_ready silu_ready act_ready act_turned act_t_ready down_ready "
                 "chose_ready before_ready pos_ready pos_read slots_ready x_h_added x_added").split()
        sem = {name: m.sem(name) for name in names}
        sent = [m.sem(f"sent{r}") for r in range(R)]
        route = Route(nc, g, m, ps_t[:, 0])
        ident = g.const("ident")
        block = ctx.enter_context(nc.Block())

        @block.vector
        def _(dve):
            norm, picks = Chain(dve, sem["norm_chain"], 2), Chain(dve, sem["route_chain"], 2)
            count_link, place = Chain(dve, sem["count_chain"], 1), Chain(dve, sem["slot_chain"], 3)
            nc.vector.memset(before[:, 0], 0.0).then_inc(sem["before_ready"], 1)
            g.wait_weights(dve)

            def normalise(i, s, lap):
                norm.at(i)
                norm.then(nc.vector.bn_stats(stats[:, s], g.x[:, i, :]))
                nc.vector.memset(pause[:], 0)
                norm.then(nc.vector.bn_aggr(mv[:, s], stats[:, s]))
                nc.vector.tensor_scalar(veps[:, s:s + 1], mv[:, s, 1:2], LN_EPS, None, ALU.add).then_inc(sem["veps_ready"], 1)

            def make_h(i, s, lap):
                dve.wait_ge(sem["rstd_ready"], i + 1)
                nc.vector.tensor_scalar(h[:, s], g.x[:, i, :], mv[:, s, 0:1], rstd[:, s:s + 1],
                                        ALU.subtract, ALU.mult).then_inc(sem["h_ready"], 1)
                dve.wait_ge(sem["h_ready"], i + 1)
                nc.vector.tensor_tensor(g.x[:, i, :], g.x[:, i, :], h[:, s], ALU.add).then_inc(sem["x_h_added"], 1)

            def mean_square(i, s, lap):
                dve.wait_ge(sem["ssq_ready"], i + 1)
                nc.vector.tensor_scalar(meps[:, s:s + 1], ssq[:, s:s + 1], 1.0 / D, RMS_EPS, ALU.mult, ALU.add).then_inc(sem["meps_ready"], 1)

            def scale(i, s, lap):
                dve.wait_ge(sem["rrms_ready"], i + 1)
                wait(dve, sent[s], lap * 16 * TOPK)
                nc.vector.scalar_tensor_tensor(out=xin[:, s], in0=h[:, s], scalar=rrms[:, s:s + 1], in1=g.norm_w[:],
                                               op0=ALU.mult, op1=ALU.mult).then_inc(sem["xin_ready"], 1)

            def choose(i, s, lap):
                dve.wait_ge(sem["gates_ready"], i + 1)
                picks.at(i)
                nc.vector.memset(pause[:], 0)
                picks.then(nc.vector.max(top8[:, s], ps_g[:, s % 2, 0:E]))
                nc.vector.memset(pause[:], 0)
                picks.then(nc.vector.max_index(idx8[:, s], top8[:, s], ps_g[:, s % 2, 0:E]))
                nc.vector.memset(pause[:], 0).then_inc(sem["chosen_ready"], 1)

            def activate(i, s, lap):
                dve.wait_ge(sem["silu_ready"], i + 1)
                nc.vector.tensor_tensor(act[:, s], silu[:, s], ps_g[:, s % 2, E + INNER:GATES], ALU.mult).then_inc(sem["act_ready"], 1)

            def count(i, s, lap):
                dve.wait_ge(sem["first_ready"], i + 1)
                count_link.at(i)
                firsts = g.const("first_slots").rearrange("p (a e) -> p a e", a=1).broadcast_to([P, TOPK, E])
                count_link.then(nc.vector.tensor_tensor(hot[:, s], firsts, g.first[:, i].rearrange("p (k o) -> p k o", o=1).broadcast_to([P, TOPK, E]), ALU.is_equal))
                nc.vector.tensor_reduce(chose[:, s], hot[:, s].rearrange("p k e -> p e k"), AX.X, ALU.add).then_inc(sem["chose_ready"], 1)
                dve.wait_ge(sem["chose_ready"], i + 1)
                nc.vector.tensor_tensor(before[:, (s + 1) % R], before[:, s], chose[:, s], ALU.add).then_inc(sem["before_ready"], 1)

            def locate(i, s, lap):
                dve.wait_ge(sem["pos_ready"], i + 1)
                place.at(i)
                nc.vector.tensor_tensor(picked[:, s], hot[:, s], ps_p[:, s % 2, 0:E].rearrange("p (a e) -> p a e", a=1).broadcast_to([P, TOPK, E]),
                                        ALU.mult).then_inc(sem["pos_read"], 1)
                dve.wait_ge(sem["pos_read"], i + 1)
                place.then(nc.vector.tensor_reduce(pos[:, s], picked[:, s], AX.X, ALU.add))
                place.then(nc.vector.tensor_scalar(over[:, s], pos[:, s], float(CAP), float(DROPPED), ALU.is_ge, ALU.mult))
                place.then(nc.vector.scalar_tensor_tensor(out=g.slot_out[:, i], in0=pos[:, s], scalar=float(CAP - 1), in1=g.first[:, i], op0=ALU.min, op1=ALU.add))
                nc.vector.tensor_tensor(slot_in[:, s], g.slot_out[:, i], over[:, s], ALU.add).then_inc(sem["slots_ready"], 1)

            def add_shared(i, s, lap):
                dve.wait_ge(sem["down_ready"], i + 1)
                dve.wait_ge(sem["x_h_added"], i + 1)
                nc.vector.tensor_tensor(g.x[:, i, :], g.x[:, i, :], ps_o[:, s % 2, 0:D], ALU.add).then_inc(sem["x_added"], 1)

            pipeline(dve, TILES, [(1, make_h), (4, locate), (1, mean_square), (0, normalise), (3, choose), (3, count), (3, activate),
                                   (5, add_shared), (1, scale)], R)
            dve.wait_ge(sem["x_added"], TILES)
            nc.vector.tensor_copy(g.totals[:], before[:, TILES % R]).then_inc(route.totalled, 1)
            route.vector(dve)

        @block.gpsimd
        def _(pool):
            g.wait_cleared(pool)

            def layer_root(i, s, lap):
                pool.wait_ge(sem["veps_ready"], i + 1)
                nc.gpsimd.tensor_tensor(rstd[:, s:s + 1], veps[:, s:s + 1], g.minus_half[:], ALU.pow).then_inc(sem["rstd_ready"], 1)

            def rms_root(i, s, lap):
                pool.wait_ge(sem["meps_ready"], i + 1)
                nc.gpsimd.tensor_tensor(rrms[:, s:s + 1], meps[:, s:s + 1], g.minus_half[:], ALU.pow).then_inc(sem["rrms_ready"], 1)

            def send(i, s, lap):
                pool.wait_ge(sem["slots_ready"], i + 1)
                nc.gpsimd.tensor_tensor(pool_pause[:, s:s + 1], g.minus_half[:], g.minus_half[:], ALU.add)
                for k in range(TOPK):
                    nc.gpsimd.indirect_dma_start(
                        out=g.slots_in, out_offset=bass.IndirectOffsetOnAxis(ap=slot_in[:, s, k:k + 1], axis=0),
                        in_=xin[:, s], in_offset=None, bounds_check=E * CAP - 1, oob_is_err=False).then_inc(sent[s], 16)

            pipeline(pool, TILES, [(1, rms_root), (0, layer_root), (4, send)], R)
            for s in range(R):
                pool.wait_ge(sent[s], 16 * TOPK * (TILES // R))

        @block.scalar
        def _(act_e):
            def squares(i, s, lap):
                act_e.wait_ge(sem["h_ready"], i + 1)
                wait(act_e, sem["ssq_ready"], i)
                nc.scalar.activation(junk[:], h[:, s], ACT.Square, accum_out=ssq[:, s:s + 1]).then_inc(sem["ssq_ready"], 1)

            def move_xin(i, s, lap):
                act_e.wait_ge(sem["turned"], i + 1)
                nc.scalar.copy(xin_t[:, s], ps_t[:, s % 2, 0:D].rearrange("p (k t) -> p k t", k=KD)).then_inc(sem["xin_t_ready"], 1)

            def gate_silu(i, s, lap):
                act_e.wait_ge(sem["chosen_ready"], i + 1)
                nc.scalar.activation(g.first[:, i], idx8[:, s, 0:TOPK], ACT.Copy, scale=float(CAP)).then_inc(sem["first_ready"], 1)
                nc.scalar.copy(g.top[:, i, :], top8[:, s, 0:TOPK])
                nc.scalar.activation(silu[:, s], ps_g[:, s % 2, E:E + INNER], ACT.Silu).then_inc(sem["silu_ready"], 1)

            def move_act(i, s, lap):
                act_e.wait_ge(sem["act_turned"], i + 1)
                nc.scalar.copy(act_t[:, s], ps_o[:, s % 2, D:D + P]).then_inc(sem["act_t_ready"], 1)

            pipeline(act_e, TILES, [(1, squares), (2, move_xin), (4, move_act), (3, gate_silu)], R)
            route.scalar(act_e)

        @block.tensor
        def _(pe):
            g.wait_weights(pe)

            def turn(i, s, lap):
                pe.wait_ge(sem["xin_ready"], i + 1)
                wait(pe, sem["xin_t_ready"], i - 1)
                for k in range(KD):
                    last = nc.tensor.transpose(ps_t[:, s % 2, k * P:(k + 1) * P], xin[:, s, k * P:(k + 1) * P], ident)
                last.then_inc(sem["turned"], 1)

            def gates(i, s, lap):
                pe.wait_ge(sem["xin_t_ready"], i + 1)
                wait(pe, sem["act_ready"], i - 1)
                for k in range(KD):
                    last = nc.tensor.matmul(ps_g[:, s % 2, 0:GATES], xin_t[:, s, k], g.w_gates[:, k, :], start=(k == 0), stop=(k == KD - 1))
                last.then_inc(sem["gates_ready"], 1)

            def positions(i, s, lap):
                pe.wait_ge(sem["chose_ready"], i + 1)
                pe.wait_ge(sem["before_ready"], i + 1)
                wait(pe, sem["pos_read"], i - 1)
                nc.tensor.matmul(ps_p[:, s % 2, 0:E], g.const("before"), chose[:, s], start=True, stop=False)
                nc.tensor.matmul(ps_p[:, s % 2, 0:E], g.ones[:], before[:, s], start=False, stop=True).then_inc(sem["pos_ready"], 1)

            def turn_act(i, s, lap):
                pe.wait_ge(sem["act_ready"], i + 1)
                wait(pe, sem["x_added"], i - 1)
                nc.tensor.transpose(ps_o[:, s % 2, D:D + P], act[:, s], ident).then_inc(sem["act_turned"], 1)

            def down(i, s, lap):
                pe.wait_ge(sem["act_t_ready"], i + 1)
                nc.tensor.matmul(ps_o[:, s % 2, 0:D], act_t[:, s], g.w_down[:], start=True, stop=True).then_inc(sem["down_ready"], 1)

            pipeline(pe, TILES, [(2, turn), (4, turn_act), (2, gates), (4, down), (3, positions)], R)
            route.tensor(pe)


def load_table(eng, table, registers, lap, largest):
    eng.load(registers, table[0:1, bass.ds(lap * RING, TABLE_PAD + RING)])
    return [eng.snap(r, min_val=0, max_val=largest) for r in registers]


def ffn_experts(nc, g, tag):
    with ExitStack() as ctx:
        m = Memory(nc, ctx, tag + "_experts")
        rows, rows_t = m.sb("rows", [P, RING, D]), m.sb("rows_t", [P, 4, KD, P])
        silu = m.sb("silu", [P, 4, INNER])
        act, act_t, res = m.sb("act", [P, 4, INNER]), m.sb("act_t", [P, 4, P]), m.sb("res", [P, RING, D])
        ps_t, ps_g, ps_o = m.ps("ps_t", [P, 2, 512]), m.ps("ps_g", [P, 2, 512]), m.ps("ps_o", [P, 2, 512])
        loads = [m.sem(f"loaded{r}") for r in range(RING)]
        stores = [m.sem(f"stored{r}") for r in range(RING)]
        turned, rows_t_ready, gu_ready = m.sem("turned"), m.sem("rows_t_ready"), m.sem("gu_ready")
        silu_ready, act_ready, act_turned, act_t_ready = m.sem("silu_ready"), m.sem("act_ready"), m.sem("act_turned"), m.sem("act_t_ready")
        out_ready, res_ready = m.sem("out_ready"), m.sem("res_ready")
        hot, moved = m.sb("hot", [P, 2, TOPK, E]), m.sb("moved", [P, 2, TOPK])
        found, shifted, summed, relocated = m.sem("found"), m.sem("shifted"), m.sem("summed"), m.sem("relocated")
        ident = g.const("ident")
        block = ctx.enter_context(nc.Block())

        @block.sync
        def _(sp):
            registers = [sp.alloc_register(f"{tag}_place{n}") for n in range(TABLE_PAD + RING)]
            place = []

            def next_places(lap):
                place[:] = load_table(sp, g.place, registers, lap, E * CAP // P)

            def load(j, s, lap):
                wait(sp, turned, j - RING + 1)
                sp.dma_start(rows[:, s], g.slots_in[bass.ds(place[TABLE_PAD + s] * P, P), :]).then_inc(loads[s], 16)

            def store(j, s, lap):
                sp.wait_ge(res_ready, j + 1)
                sp.dma_start(g.results[bass.ds(j * P, P), :], res[:, s]).then_inc(stores[s], 16)

            pipeline(sp, BLOCKS, [(7, store), (0, load)], RING, next_places)
            for s in range(RING):
                sp.wait_ge(stores[s], 16 * (BLOCKS // RING))

        @block.tensor
        def _(pe):
            registers = [pe.alloc_register(f"{tag}_owner{n}") for n in range(TABLE_PAD + RING)]
            owner = []

            def next_owners(lap):
                owner[:] = load_table(pe, g.owner, registers, lap, E - 1)

            def owner_of(s, delay):
                return owner[TABLE_PAD + s if s < RING - delay else TABLE_PAD + s - RING]

            def turn(j, s, lap):
                pe.wait_ge(loads[s], lap * 16 + 16)
                wait(pe, rows_t_ready, j - 1)
                for k in range(KD):
                    last = nc.tensor.transpose(ps_t[:, s % 2, k * P:(k + 1) * P], rows[:, s, k * P:(k + 1) * P], ident)
                last.then_inc(turned, 1)

            def gate_up(j, s, lap):
                pe.wait_ge(rows_t_ready, j + 1)
                wait(pe, act_ready, j - 1)
                for k in range(KD):
                    last = nc.tensor.matmul(ps_g[:, s % 2, 0:2 * INNER], rows_t[:, s % 4, k],
                                            g.w13[:, bass.ds(owner_of(s, 1), 1), k, :].rearrange("p o f -> p (o f)"), start=(k == 0), stop=(k == KD - 1))
                last.then_inc(gu_ready, 1)

            def turn_act(j, s, lap):
                pe.wait_ge(act_ready, j + 1)
                wait(pe, res_ready, j - 1)
                nc.tensor.transpose(ps_o[:, s % 2, D:D + P], act[:, s % 4], ident).then_inc(act_turned, 1)

            def down(j, s, lap):
                pe.wait_ge(act_t_ready, j + 1)
                nc.tensor.matmul(ps_o[:, s % 2, 0:D], act_t[:, s % 4], g.w2[:, bass.ds(owner_of(s, 3), 1), :].rearrange("p o f -> p (o f)"),
                                 start=True, stop=True).then_inc(out_ready, 1)

            pipeline(pe, BLOCKS, [(0, turn), (1, gate_up), (2, turn_act), (3, down)], RING, next_owners)
        @block.scalar
        def _(act_e):
            def move_rows(j, s, lap):
                act_e.wait_ge(turned, j + 1)
                wait(act_e, gu_ready, j - 3)
                nc.scalar.copy(rows_t[:, s % 4], ps_t[:, s % 2, 0:D].rearrange("p (k t) -> p k t", k=KD)).then_inc(rows_t_ready, 1)

            def gate_silu(j, s, lap):
                act_e.wait_ge(gu_ready, j + 1)
                wait(act_e, act_ready, j - 3)
                nc.scalar.activation(silu[:, s % 4], ps_g[:, s % 2, 0:INNER], ACT.Silu).then_inc(silu_ready, 1)

            def move_act(j, s, lap):
                act_e.wait_ge(act_turned, j + 1)
                wait(act_e, out_ready, j - 3)
                nc.scalar.copy(act_t[:, s % 4], ps_o[:, s % 2, D:D + P]).then_inc(act_t_ready, 1)

            pipeline(act_e, BLOCKS, [(0, move_rows), (1, gate_silu), (2, move_act)], RING)

        @block.vector
        def _(dve):
            def activate(j, s, lap):
                dve.wait_ge(silu_ready, j + 1)
                wait(dve, act_turned, j - 3)
                nc.vector.tensor_tensor(act[:, s % 4], silu[:, s % 4], ps_g[:, s % 2, INNER:2 * INNER], ALU.mult).then_inc(act_ready, 1)

            def move_out(j, s, lap):
                dve.wait_ge(out_ready, j + 1)
                wait(dve, stores[s], lap * 16)
                nc.vector.tensor_copy(res[:, s], ps_o[:, s % 2, 0:D]).then_inc(res_ready, 1)

            def relocate(j, s, lap):
                if not isinstance(j, int) or j >= TILES:
                    return
                wide = [P, TOPK, E]
                steps = [lambda i: nc.vector.tensor_tensor(hot[:, i % 2], g.const("first_slots").rearrange("p (a e) -> p a e", a=1).broadcast_to(wide),
                                                           g.first[:, i].rearrange("p (k o) -> p k o", o=1).broadcast_to(wide), ALU.is_equal).then_inc(found, 1),
                         lambda i: nc.vector.tensor_tensor(hot[:, i % 2], hot[:, i % 2], g.shift[:].rearrange("p (a e) -> p a e", a=1).broadcast_to(wide),
                                                           ALU.mult).then_inc(shifted, 1),
                         lambda i: nc.vector.tensor_reduce(moved[:, i % 2], hot[:, i % 2], AX.X, ALU.add).then_inc(summed, 1),
                         lambda i: nc.vector.tensor_tensor(g.slot_out[:, i], g.slot_out[:, i], moved[:, i % 2], ALU.add).then_inc(relocated, 1)]
                done = (found, shifted, summed)
                for t in range(j, j + (4 if j == TILES - 1 else 1)):
                    for n in (3, 2, 1, 0):
                        if 0 <= t - n < TILES:
                            if n:
                                dve.wait_ge(done[n - 1], t - n + 1)
                            else:
                                wait(dve, summed, t - 1)
                            steps[n](t - n)

            pipeline(dve, BLOCKS, [(1, activate), (3, move_out), (0, relocate)], RING)
            dve.wait_ge(relocated, TILES)


class Combine:

    def __init__(self, nc, g, m, first, ring):
        self.nc, self.g, self.first, self.ring = nc, g, first, ring
        self.got, self.pause = m.sb("got", [P, ring * TOPK, D]), m.sb("pool_pause", [P, 2 * TOPK])
        self.gathered = [m.sem(f"gathered{r}") for r in range(ring * TOPK)]
        self.added = m.sem("added")

    def gather(self, pool, i, slots, turn=0):
        for k in range(TOPK):
            wait(pool, self.added, (i - self.first - self.ring) * TOPK + k + 1)
            at = (i - self.first) % self.ring * TOPK + k if self.ring > 1 else k
            if not isinstance(i, int):
                at_pause = turn * TOPK + k
                self.nc.gpsimd.tensor_tensor(self.pause[:, at_pause:at_pause + 1], self.g.minus_half[:], self.g.minus_half[:], ALU.add)
            self.nc.gpsimd.indirect_dma_start(
                out=self.got[:, at], out_offset=None, in_=self.g.results,
                in_offset=bass.IndirectOffsetOnAxis(ap=slots[:, k:k + 1], axis=0),
                bounds_check=BLOCKS * P - 1, oob_is_err=False).then_inc(self.gathered[at], 16)

    def add(self, dve, i, weights):
        for k in range(TOPK):
            n = i - self.first
            at, lap = (n % self.ring * TOPK + k, n // self.ring) if self.ring > 1 else (k, n)
            dve.wait_ge(self.gathered[at], lap * 16 + 16)
            wait(dve, self.added, n * TOPK + k)
            x = self.g.x[:, i, :]
            self.nc.vector.scalar_tensor_tensor(out=x, in0=self.got[:, at], scalar=weights[:, k:k + 1],
                                                in1=x, op0=ALU.mult, op1=ALU.add).then_inc(self.added, 1)


def ffn(nc, g, tag):
    ffn_router(nc, g, tag)
    ffn_experts(nc, g, tag)


def combine_and_store(nc, g, out):
    with ExitStack() as ctx:
        m = Memory(nc, ctx, "store")
        combine, stored = Combine(nc, g, m, 0, 2), m.sem("stored")
        block = ctx.enter_context(nc.Block())

        @block.gpsimd
        def _(pool):
            for i in range(TILES):
                combine.gather(pool, i, g.slot_out[:, i])

        @block.vector
        def _(dve):
            for i in range(TILES):
                combine.add(dve, i, g.weight[:, i])

        @block.sync
        def _(sp):
            for b in range(B):
                sp.wait_ge(combine.added, (b + 1) * 2 * TOPK)
                sp.dma_start(out[b].rearrange("(h p) d -> p h d", p=P), g.x[:, b * 2:b * 2 + 2]).then_inc(stored, 16)
            sp.wait_ge(stored, 16 * B)


class Globals:

    def __init__(self, nc, ctx):
        m = Memory(nc, ctx, "g")
        self.consts = m.sb("consts", [P, CONST_COLS])
        self.ones, self.minus_half = m.sb("ones", [P, P]), m.sb("minus_half", [P, 1])
        self.x = m.sb("x", [P, TILES, D])
        self.w_gates, self.w_down = m.sb("w_gates", [P, KD, GATES]), m.sb("w_down", [P, D])
        self.norm_w = m.sb("norm_w", [P, D])
        self.w13, self.w2 = m.sb("w13", [P, E, KD, 2 * INNER]), m.sb("w2", [P, E, D])
        self.top = m.sb("top", [P, TILES, TOPK])
        self.weight = m.sb("weight", [P, TILES, TOPK])
        self.slot_out, self.totals = m.sb("slot_out", [P, TILES, TOPK], U32), m.sb("totals", [P, E])
        self.first, self.shift = m.sb("first", [P, TILES, TOPK]), m.sb("shift", [P, E])
        self.owner, self.place = m.sb("owner", [1, TABLE_PAD + P], I32), m.sb("place", [1, TABLE_PAD + P], I32)
        self.weights_loaded, self.cleared = m.sem("weights_loaded"), m.sem("cleared")
        self.first_layer = True
        self.slots_in = nc.dram_tensor("slots_in", [SLOTS, D], F32, kind="Internal").ap()
        self.results = nc.dram_tensor("results", [BLOCKS * P, D], F32, kind="Internal").ap()

    def wait_weights(self, eng):
        if self.first_layer:
            eng.wait_ge(self.weights_loaded, 16 * (5 + 2 * (E // 8)))

    def wait_cleared(self, eng):
        if self.first_layer:
            eng.wait_ge(self.cleared, 16 * CLEARS)

    def const(self, name):
        a, b = CONST[name]
        return self.consts[:, a:b]


def build(nc, dram, out):
    Memory.sems.clear()
    with ExitStack() as ctx:
        g = Globals(nc, ctx)
        load_all(nc, g, dram)
        attention_a(nc, g, dram)
        ffn(nc, g, "f1")
        g.first_layer = False
        zero_semaphores(nc)
        attention_b(nc, g, dram)
        ffn(nc, g, "f2")
        combine_and_store(nc, g, out)


def kernel(**inputs):
    import concourse.bacc as bacc
    from concourse.bass_utils import run_bass_kernel_spmd

    nc = bacc.Bacc("TRN2", target_bir_lowering=False, num_devices=1)
    laid = {
        "x": inputs["L0_attn_a_x"], "consts": constants(),
        "gate_t": np.asarray(inputs["L0_ffn_gate_w"]).T,
    }
    for name in inputs:
        if name not in ("L0_attn_a_x", "L0_ffn_gate_w"):
            laid[name.replace("L0_ffn_", "").replace("L0_attn_a_", "a_").replace("L0_attn_b_", "b_")] = np.asarray(inputs[name])
    wq = laid.pop("a_Wq").reshape(D, GA // 2, 2, REP, DA).transpose(0, 1, 3, 2, 4).reshape(D, HA * DA)
    laid["a_Wqkv"] = np.concatenate([wq, laid.pop("a_Wk"), laid.pop("a_Wv")], 1)
    wq_b = laid.pop("b_wq_b").reshape(QR, HB, DK)
    laid["b_wqn_t"], laid["b_wqp"] = wq_b[:, :, :NOPE].transpose(2, 1, 0), wq_b[:, :, NOPE:]
    wkv_b = laid.pop("b_wkv_b").reshape(KVR, HB, NOPE + VD)
    laid["b_wk_t"], laid["b_wv_t"] = wkv_b[:, :, :NOPE].transpose(2, 1, 0), wkv_b[:, :, NOPE:].transpose(2, 1, 0)
    laid["b_w_a"] = np.concatenate([laid.pop("b_wq_a"), laid.pop("b_wkv_a")], 1)
    arrays, dram = {}, {}
    for name, value in laid.items():
        value = np.ascontiguousarray(value)
        arrays[f"in_{name}"] = value
        dram[name] = nc.dram_tensor(f"in_{name}", value.shape, mybir.dt.from_np(value.dtype), kind="ExternalInput").ap()
    out = nc.dram_tensor("out_x", (B, T, D), F32, kind="ExternalOutput").ap()
    build(nc, dram, out)
    return run_bass_kernel_spmd(nc, [arrays], core_ids=[0]).results[0]["out_x"]
```
